# Optimizing a Trainium2 kernel written in Bass

```python
import numpy as np
import jax
import jax.numpy as jnp

def _softmax(x, axis=-1):
    return jax.nn.softmax(x, axis=axis)

def _gelu(x):
    return jax.nn.gelu(x, approximate=True)

def _silu(x):
    return jax.nn.silu(x)

def _sigmoid(x):
    return jax.nn.sigmoid(x)

def _layernorm(x, axis=-1, eps=1e-05):
    m = jnp.mean(x, axis=axis, keepdims=True)
    v = jnp.var(x, axis=axis, keepdims=True)
    return (x - m) / jnp.sqrt(v + eps)

def _scatter_add(tgt, idx, src, axis=0):
    return tgt.at[idx].add(src)

def _segment_sum(src, seg, n):
    return jax.ops.segment_sum(src, seg, n)
kernel_name = 'mk_recurrent_d4_jaxref_r8_a1195b'

def setup_inputs(seed: int=0):
    np.random.seed(seed)
    _w = jnp.asarray

    def _L0_attn_setup():
        import jax, jax.numpy as jnp
        import numpy as np
        EMB, KDIM, B, S = (128, 64, 8, 256)
        key = jax.random.key(seed)
        kx, kq, kk, kv1, kv2 = jax.random.split(key, 5)

        def xavier(k, shape):
            fan_in, fan_out = shape
            lim = (6.0 / (fan_in + fan_out)) ** 0.5
            return jax.random.uniform(k, shape, jnp.float32, -lim, lim)
        return {'x': jax.random.normal(kx, (B, S, EMB), jnp.float32), 'w_q': xavier(kq, (EMB, KDIM)), 'w_k': xavier(kk, (EMB, KDIM)), 'w_v1': xavier(kv1, (EMB, KDIM)), 'w_v2': xavier(kv2, (KDIM, EMB))}
    _L0_attn_in = _L0_attn_setup()

    def _L0_ffn_setup():
        import jax, jax.numpy as jnp
        import numpy as np
        DIM = 128
        HIDDEN = 384
        SCALE = 1.0 / 127.0

        def _dequant(w_int, dtype):
            return w_int.astype(dtype) * jnp.asarray(SCALE, dtype)
        key = jax.random.key(seed)
        k_x, k_g, k_u, k_d = jax.random.split(key, 4)
        x = jax.random.normal(k_x, (4, 256, DIM), dtype=jnp.float32)
        w_gate = jax.random.randint(k_g, (HIDDEN, DIM), -127, 128, dtype=jnp.int32)
        w_up = jax.random.randint(k_u, (HIDDEN, DIM), -127, 128, dtype=jnp.int32)
        w_down = jax.random.randint(k_d, (DIM, HIDDEN), -127, 128, dtype=jnp.int32)
        return {'x': x, 'w_gate': w_gate, 'w_up': w_up, 'w_down': w_down}
    _L0_ffn_in = _L0_ffn_setup()

    def _L1_attn_setup():
        import math
        import jax, jax.numpy as jnp
        import numpy as np
        SEQ, BATCH, D_MODEL, NHEAD, FEAT = (256, 2, 128, 8, 128)

        def _sinusoid_pe(length, d_model, dtype):
            pos = jnp.arange(length, dtype=dtype)[:, None]
            div = jnp.exp(jnp.arange(0, d_model, 2, dtype=dtype) * (-math.log(10000.0) / d_model))
            ang = pos * div
            return jnp.stack([jnp.sin(ang), jnp.cos(ang)], axis=-1).reshape(length, d_model)

        def _left_shift(x):
            I, J, B, N = x.shape
            zero = jnp.zeros((I, 1, B, N), x.dtype)
            padded = jnp.concatenate([zero, x], axis=1)
            padded = padded.reshape(J + 1, I, B, N)[1:]
            x = padded.reshape(I, J, B, N)
            return jnp.tril(x)
        key = jax.random.key(seed)
        ks = jax.random.split(key, 8)
        s = 0.02
        return {'x': jax.random.normal(ks[0], (SEQ, BATCH, D_MODEL), dtype=jnp.float32), 'gamma': jnp.ones((D_MODEL,), jnp.float32), 'beta': jnp.zeros((D_MODEL,), jnp.float32), 'Wq': jax.random.normal(ks[1], (D_MODEL, NHEAD * FEAT), jnp.float32) * s, 'Wv': jax.random.normal(ks[2], (D_MODEL, NHEAD * FEAT), jnp.float32) * s, 'Wr': jax.random.normal(ks[3], (D_MODEL, NHEAD * FEAT), jnp.float32) * s, 'u_bias': jax.random.normal(ks[4], (NHEAD, FEAT), jnp.float32) * s, 'v_bias': jax.random.normal(ks[5], (NHEAD, FEAT), jnp.float32) * s, 'Wout': jax.random.normal(ks[6], (NHEAD * FEAT, D_MODEL), jnp.float32) * s, 'bout': jnp.zeros((D_MODEL,), jnp.float32)}
    _L1_attn_in = _L1_attn_setup()

    def _L1_ffn_setup():
        import jax, jax.numpy as jnp
        import numpy as np
        BLOCK = 16
        _GRID = jnp.array([0.0, 0.5, 1.0, 1.5, 2.0, 3.0, 4.0, 6.0], dtype=jnp.float32)
        _MID = jnp.array([0.25, 0.75, 1.25, 1.75, 2.5, 3.5, 5.0], dtype=jnp.float32)

        def fp4_quant_dequant(x):
            shape = x.shape
            xb = x.reshape(shape[:-1] + (shape[-1] // BLOCK, BLOCK))
            scale = jnp.max(jnp.abs(xb), axis=-1, keepdims=True) / 6.0
            scale = jnp.maximum(scale, jnp.float32(1e-12))
            xn = xb / scale
            idx = jnp.searchsorted(_MID, jnp.abs(xn))
            q = _GRID[idx] * jnp.sign(xn) * scale
            return q.reshape(shape)

        def fp4_linear(x, w):
            xq = fp4_quant_dequant(x)
            wq = fp4_quant_dequant(w)
            return jnp.einsum('bsk,nk->bsn', xq, wq)
        key = jax.random.key(seed)
        k1, k2, k3, k4 = jax.random.split(key, 4)
        H, I = (128, 352)
        x = jax.random.normal(k1, (4, 512, H), dtype=jnp.float32)
        w_gate = jax.random.normal(k2, (I, H), dtype=jnp.float32) * 0.02
        w_up = jax.random.normal(k3, (I, H), dtype=jnp.float32) * 0.02
        w_down = jax.random.normal(k4, (H, I), dtype=jnp.float32) * 0.02
        return {'x': x, 'w_gate': w_gate, 'w_up': w_up, 'w_down': w_down}
    _L1_ffn_in = _L1_ffn_setup()

    def _L2_attn_setup():
        import jax, jax.numpy as jnp
        import numpy as np
        N_HEAD = 16
        key = jax.random.key(seed)
        ks = jax.random.split(key, 5)
        B, T, C = (4, 128, 128)
        d = C // N_HEAD
        x = jax.random.normal(ks[0], (B, T, C), dtype=jnp.float32)
        w_attn = jax.random.normal(ks[1], (C, 3 * C), dtype=jnp.float32) * 0.02
        w_proj = jax.random.normal(ks[2], (C, C), dtype=jnp.float32) * 0.02
        embk = 0.02 * jax.random.normal(ks[3], (T, d), dtype=jnp.float32)
        embv = 0.02 * jax.random.normal(ks[4], (T, d), dtype=jnp.float32)
        return {'x': x, 'w_attn': w_attn, 'w_proj': w_proj, 'embk': embk, 'embv': embv}
    _L2_attn_in = _L2_attn_setup()

    def _L2_ffn_setup():
        import jax, jax.numpy as jnp
        import numpy as np
        BLOCK = 16
        _GRID = jnp.array([0.0, 0.5, 1.0, 1.5, 2.0, 3.0, 4.0, 6.0], dtype=jnp.float32)
        _MID = jnp.array([0.25, 0.75, 1.25, 1.75, 2.5, 3.5, 5.0], dtype=jnp.float32)

        def fp4_quant_dequant(x):
            shape = x.shape
            xb = x.reshape(shape[:-1] + (shape[-1] // BLOCK, BLOCK))
            scale = jnp.max(jnp.abs(xb), axis=-1, keepdims=True) / 6.0
            scale = jnp.maximum(scale, jnp.float32(1e-12))
            xn = xb / scale
            idx = jnp.searchsorted(_MID, jnp.abs(xn))
            q = _GRID[idx] * jnp.sign(xn) * scale
            return q.reshape(shape)

        def fp4_linear(x, w):
            xq = fp4_quant_dequant(x)
            wq = fp4_quant_dequant(w)
            return jnp.einsum('bsk,nk->bsn', xq, wq)
        key = jax.random.key(seed)
        k1, k2, k3, k4 = jax.random.split(key, 4)
        H, I = (128, 352)
        x = jax.random.normal(k1, (4, 512, H), dtype=jnp.float32)
        w_gate = jax.random.normal(k2, (I, H), dtype=jnp.float32) * 0.02
        w_up = jax.random.normal(k3, (I, H), dtype=jnp.float32) * 0.02
        w_down = jax.random.normal(k4, (H, I), dtype=jnp.float32) * 0.02
        return {'x': x, 'w_gate': w_gate, 'w_up': w_up, 'w_down': w_down}
    _L2_ffn_in = _L2_ffn_setup()

    def _L3_attn_setup():
        import jax, jax.numpy as jnp
        import numpy as np
        import math
        B, T, C = (2, 256, 128)
        H, L = (16, 64)
        DH = C // H
        DHE = DH // 2
        THETA = 10000.0

        def _rope_cache(t, dim):
            inv_freq = 1.0 / THETA ** (jnp.arange(0, dim, 2, dtype=jnp.float32) / dim)
            freqs = jnp.arange(t, dtype=jnp.float32)[:, None] * inv_freq[None, :]
            emb = jnp.concatenate((freqs, freqs), axis=-1)
            return (jnp.cos(emb), jnp.sin(emb))

        def _apply_rope(x, cos, sin):
            x1 = x[..., 0::2]
            x2 = x[..., 1::2]
            rot = jnp.stack((-x2, x1), axis=-1).reshape(x.shape)
            return x * cos[None, None] + rot * sin[None, None]
        key = jax.random.key(seed)
        ks = jax.random.split(key, 10)
        s = 0.02
        return {'x': jax.random.normal(ks[0], (B, T, C), jnp.float32), 'Wq_down': jax.random.normal(ks[1], (C, H * L), jnp.float32) * s, 'Wk_down': jax.random.normal(ks[2], (C, H * L), jnp.float32) * s, 'Wv_down': jax.random.normal(ks[3], (C, H * L), jnp.float32) * s, 'Wq_up_c': jax.random.normal(ks[4], (L, DHE), jnp.float32) * s, 'Wq_up_e': jax.random.normal(ks[5], (L, DHE), jnp.float32) * s, 'Wk_up_c': jax.random.normal(ks[6], (L, DHE), jnp.float32) * s, 'Wk_up_e': jax.random.normal(ks[7], (L, DHE), jnp.float32) * s, 'Wv_up': jax.random.normal(ks[8], (L, DH), jnp.float32) * s, 'Wc': jax.random.normal(ks[9], (C, C), jnp.float32) * s}
    _L3_attn_in = _L3_attn_setup()

    def _L3_ffn_setup():
        import jax, jax.numpy as jnp
        import numpy as np
        D_MODEL = 128
        N_EXPERTS = 8
        TOP_K = 2
        key = jax.random.key(seed)
        k1, k2, k3, k4 = jax.random.split(key, 4)
        B, S, D, E = (4, 256, D_MODEL, N_EXPERTS)
        dff = 4 * D
        lim = float(np.sqrt(6.0 / (D + dff)))
        return {'x': jax.random.normal(k1, (B, S, D), dtype=jnp.float32), 'router_w': jax.random.normal(k2, (D, E), dtype=jnp.float32) * (1.0 / np.sqrt(D)), 'router_b': jnp.zeros((E,), dtype=jnp.float32), 'expert_up': jax.random.uniform(k3, (E, dff, D), dtype=jnp.float32, minval=-lim, maxval=lim), 'expert_down': jax.random.uniform(k4, (E, D, dff), dtype=jnp.float32, minval=-lim, maxval=lim)}
    _L3_ffn_in = _L3_ffn_setup()
    _d = {'L0_attn_x': _L0_attn_in['x'], 'L0_attn_w_q': _L0_attn_in['w_q'], 'L0_attn_w_k': _L0_attn_in['w_k'], 'L0_attn_w_v1': _L0_attn_in['w_v1'], 'L0_attn_w_v2': _L0_attn_in['w_v2'], 'L0_ffn_w_gate': _L0_ffn_in['w_gate'], 'L0_ffn_w_up': _L0_ffn_in['w_up'], 'L0_ffn_w_down': _L0_ffn_in['w_down'], 'L1_attn_gamma': _L1_attn_in['gamma'], 'L1_attn_beta': _L1_attn_in['beta'], 'L1_attn_Wq': _L1_attn_in['Wq'], 'L1_attn_Wv': _L1_attn_in['Wv'], 'L1_attn_Wr': _L1_attn_in['Wr'], 'L1_attn_u_bias': _L1_attn_in['u_bias'], 'L1_attn_v_bias': _L1_attn_in['v_bias'], 'L1_attn_Wout': _L1_attn_in['Wout'], 'L1_attn_bout': _L1_attn_in['bout'], 'L1_ffn_w_gate': _L1_ffn_in['w_gate'], 'L1_ffn_w_up': _L1_ffn_in['w_up'], 'L1_ffn_w_down': _L1_ffn_in['w_down'], 'L2_attn_w_attn': _L2_attn_in['w_attn'], 'L2_attn_w_proj': _L2_attn_in['w_proj'], 'L2_attn_embk': _L2_attn_in['embk'], 'L2_attn_embv': _L2_attn_in['embv'], 'L2_ffn_w_gate': _L2_ffn_in['w_gate'], 'L2_ffn_w_up': _L2_ffn_in['w_up'], 'L2_ffn_w_down': _L2_ffn_in['w_down'], 'L3_attn_Wq_down': _L3_attn_in['Wq_down'], 'L3_attn_Wk_down': _L3_attn_in['Wk_down'], 'L3_attn_Wv_down': _L3_attn_in['Wv_down'], 'L3_attn_Wq_up_c': _L3_attn_in['Wq_up_c'], 'L3_attn_Wq_up_e': _L3_attn_in['Wq_up_e'], 'L3_attn_Wk_up_c': _L3_attn_in['Wk_up_c'], 'L3_attn_Wk_up_e': _L3_attn_in['Wk_up_e'], 'L3_attn_Wv_up': _L3_attn_in['Wv_up'], 'L3_attn_Wc': _L3_attn_in['Wc'], 'L3_ffn_router_w': _L3_ffn_in['router_w'], 'L3_ffn_router_b': _L3_ffn_in['router_b'], 'L3_ffn_expert_up': _L3_ffn_in['expert_up'], 'L3_ffn_expert_down': _L3_ffn_in['expert_down']}
    _x0 = _d['L0_attn_x']
    _d['L0_attn_x'] = jax.random.normal(jax.random.fold_in(jax.random.key(seed), 1), (8, 512, 128), dtype=_x0.dtype)
    del _x0
    return _d

def reference(L0_attn_x, L0_attn_w_q, L0_attn_w_k, L0_attn_w_v1, L0_attn_w_v2, L0_ffn_w_gate, L0_ffn_w_up, L0_ffn_w_down, L1_attn_gamma, L1_attn_beta, L1_attn_Wq, L1_attn_Wv, L1_attn_Wr, L1_attn_u_bias, L1_attn_v_bias, L1_attn_Wout, L1_attn_bout, L1_ffn_w_gate, L1_ffn_w_up, L1_ffn_w_down, L2_attn_w_attn, L2_attn_w_proj, L2_attn_embk, L2_attn_embv, L2_ffn_w_gate, L2_ffn_w_up, L2_ffn_w_down, L3_attn_Wq_down, L3_attn_Wk_down, L3_attn_Wv_down, L3_attn_Wq_up_c, L3_attn_Wq_up_e, L3_attn_Wk_up_c, L3_attn_Wk_up_e, L3_attn_Wv_up, L3_attn_Wc, L3_ffn_router_w, L3_ffn_router_b, L3_ffn_expert_up, L3_ffn_expert_down):

    def _L0_attn_ref(x, w_q, w_k, w_v1, w_v2):
        import jax, jax.numpy as jnp
        import numpy as np
        EMB, KDIM, B, S = (128, 64, 8, 256)
        seq = x.shape[1]
        queries = jnp.einsum('bse,ek->bsk', x, w_q)
        keys = jnp.einsum('bse,ek->bsk', x, w_k)
        scale = w_q.shape[1] ** (-0.5)
        scores = jnp.einsum('bqk,bsk->bqs', queries, keys) * scale
        causal = jnp.tril(jnp.ones((seq, seq), dtype=bool))
        scores = jnp.where(causal[None, :, :], scores, -jnp.inf)
        attn = jax.nn.softmax(scores, axis=-1)
        values = jnp.einsum('bsk,ke->bse', jnp.einsum('bse,ek->bsk', x, w_v1), w_v2)
        return jnp.einsum('bqs,bse->bqe', attn, values)

    def _L0_ffn_ref(x, w_gate, w_up, w_down):
        import jax, jax.numpy as jnp
        import numpy as np
        DIM = 128
        HIDDEN = 384
        SCALE = 1.0 / 127.0

        def _dequant(w_int, dtype):
            return w_int.astype(dtype) * jnp.asarray(SCALE, dtype)
        wg = _dequant(w_gate, x.dtype)
        wu = _dequant(w_up, x.dtype)
        wd = _dequant(w_down, x.dtype)
        gate = jnp.einsum('bsd,hd->bsh', x, wg)
        up = jnp.einsum('bsd,hd->bsh', x, wu)
        h = jax.nn.silu(gate) * up
        return jnp.einsum('bsh,dh->bsd', h, wd)

    def _L1_attn_ref(x, gamma, beta, Wq, Wv, Wr, u_bias, v_bias, Wout, bout):
        import math
        import jax, jax.numpy as jnp
        import numpy as np
        SEQ, BATCH, D_MODEL, NHEAD, FEAT = (256, 2, 128, 8, 128)

        def _sinusoid_pe(length, d_model, dtype):
            pos = jnp.arange(length, dtype=dtype)[:, None]
            div = jnp.exp(jnp.arange(0, d_model, 2, dtype=dtype) * (-math.log(10000.0) / d_model))
            ang = pos * div
            return jnp.stack([jnp.sin(ang), jnp.cos(ang)], axis=-1).reshape(length, d_model)

        def _left_shift(x):
            I, J, B, N = x.shape
            zero = jnp.zeros((I, 1, B, N), x.dtype)
            padded = jnp.concatenate([zero, x], axis=1)
            padded = padded.reshape(J + 1, I, B, N)[1:]
            x = padded.reshape(I, J, B, N)
            return jnp.tril(x)
        I, B, D = x.shape
        H, F = u_bias.shape
        sqrt_d = jnp.asarray(math.sqrt(D), x.dtype)
        mu = jnp.mean(x, axis=-1, keepdims=True)
        var = jnp.mean((x - mu) ** 2, axis=-1, keepdims=True)
        h = (x - mu) * jax.lax.rsqrt(var + 1e-05) * gamma + beta
        pe = _sinusoid_pe(I, D, x.dtype)[::-1]
        q = (h @ Wq).reshape(I, B, H, F)
        k = (h @ Wq).reshape(I, B, H, F)
        v = (h @ Wv).reshape(I, B, H, F)
        r = (pe @ Wr).reshape(I, H, F)
        content = jnp.einsum('ibnf,jbnf->ijbn', q + u_bias, k)
        pos = jnp.einsum('ibnf,jnf->ijbn', q + v_bias, r)
        pos = _left_shift(pos)
        attn = jax.nn.softmax((content + pos) / sqrt_d, axis=1)
        o = jnp.einsum('ijbn,jbnf->ibnf', attn, v).reshape(I, B, H * F)
        return o @ Wout + bout

    def _L1_ffn_ref(x, w_gate, w_up, w_down):
        import jax, jax.numpy as jnp
        import numpy as np
        BLOCK = 16
        _GRID = jnp.array([0.0, 0.5, 1.0, 1.5, 2.0, 3.0, 4.0, 6.0], dtype=jnp.float32)
        _MID = jnp.array([0.25, 0.75, 1.25, 1.75, 2.5, 3.5, 5.0], dtype=jnp.float32)

        def fp4_quant_dequant(x):
            shape = x.shape
            xb = x.reshape(shape[:-1] + (shape[-1] // BLOCK, BLOCK))
            scale = jnp.max(jnp.abs(xb), axis=-1, keepdims=True) / 6.0
            scale = jnp.maximum(scale, jnp.float32(1e-12))
            xn = xb / scale
            idx = jnp.searchsorted(_MID, jnp.abs(xn))
            q = _GRID[idx] * jnp.sign(xn) * scale
            return q.reshape(shape)

        def fp4_linear(x, w):
            xq = fp4_quant_dequant(x)
            wq = fp4_quant_dequant(w)
            return jnp.einsum('bsk,nk->bsn', xq, wq)
        gate = fp4_linear(x, w_gate)
        y = fp4_linear(x, w_up)
        h = jax.nn.silu(gate) * y
        return fp4_linear(h, w_down)

    def _L2_attn_ref(x, w_attn, w_proj, embk, embv):
        import jax, jax.numpy as jnp
        import numpy as np
        N_HEAD = 16
        B, T, C = x.shape
        H = N_HEAD
        d = C // H
        qkv = x @ w_attn
        q, k, v = jnp.split(qkv, 3, axis=2)
        q = q.reshape(B, T, H, d).transpose(0, 2, 1, 3)
        k = k.reshape(B, T, H, d).transpose(0, 2, 1, 3)
        v = v.reshape(B, T, H, d).transpose(0, 2, 1, 3)
        idx = jnp.arange(T)
        rel = jnp.tril(idx[:, None] - idx[None, :])
        rk = embk[rel]
        rv = embv[rel]
        scale = 1.0 / np.sqrt(d).astype(np.float32)
        att = jnp.einsum('bhtd,bhsd->bhts', q, k) * scale + jnp.einsum('bhtd,tsd->bhts', q, rk)
        causal = idx[None, :] <= idx[:, None]
        att = jnp.where(causal[None, None], att, -jnp.inf)
        att = jax.nn.softmax(att, axis=-1)
        y = jnp.einsum('bhts,bhsd->bhtd', att, v) + jnp.einsum('bhts,tsd->bhtd', att, rv)
        y = y.transpose(0, 2, 1, 3).reshape(B, T, C)
        return y @ w_proj

    def _L2_ffn_ref(x, w_gate, w_up, w_down):
        import jax, jax.numpy as jnp
        import numpy as np
        BLOCK = 16
        _GRID = jnp.array([0.0, 0.5, 1.0, 1.5, 2.0, 3.0, 4.0, 6.0], dtype=jnp.float32)
        _MID = jnp.array([0.25, 0.75, 1.25, 1.75, 2.5, 3.5, 5.0], dtype=jnp.float32)

        def fp4_quant_dequant(x):
            shape = x.shape
            xb = x.reshape(shape[:-1] + (shape[-1] // BLOCK, BLOCK))
            scale = jnp.max(jnp.abs(xb), axis=-1, keepdims=True) / 6.0
            scale = jnp.maximum(scale, jnp.float32(1e-12))
            xn = xb / scale
            idx = jnp.searchsorted(_MID, jnp.abs(xn))
            q = _GRID[idx] * jnp.sign(xn) * scale
            return q.reshape(shape)

        def fp4_linear(x, w):
            xq = fp4_quant_dequant(x)
            wq = fp4_quant_dequant(w)
            return jnp.einsum('bsk,nk->bsn', xq, wq)
        gate = fp4_linear(x, w_gate)
        y = fp4_linear(x, w_up)
        h = jax.nn.silu(gate) * y
        return fp4_linear(h, w_down)

    def _L3_attn_ref(x, Wq_down, Wk_down, Wv_down, Wq_up_c, Wq_up_e, Wk_up_c, Wk_up_e, Wv_up, Wc):
        import jax, jax.numpy as jnp
        import numpy as np
        import math
        B, T, C = (2, 256, 128)
        H, L = (16, 64)
        DH = C // H
        DHE = DH // 2
        THETA = 10000.0

        def _rope_cache(t, dim):
            inv_freq = 1.0 / THETA ** (jnp.arange(0, dim, 2, dtype=jnp.float32) / dim)
            freqs = jnp.arange(t, dtype=jnp.float32)[:, None] * inv_freq[None, :]
            emb = jnp.concatenate((freqs, freqs), axis=-1)
            return (jnp.cos(emb), jnp.sin(emb))

        def _apply_rope(x, cos, sin):
            x1 = x[..., 0::2]
            x2 = x[..., 1::2]
            rot = jnp.stack((-x2, x1), axis=-1).reshape(x.shape)
            return x * cos[None, None] + rot * sin[None, None]
        b, t, c = x.shape
        q_lat = (x @ Wq_down).reshape(b, t, H, L)
        k_lat = (x @ Wk_down).reshape(b, t, H, L)
        v_lat = (x @ Wv_down).reshape(b, t, H, L)
        q_c = jnp.einsum('bthl,ld->bhtd', q_lat, Wq_up_c)
        q_e = jnp.einsum('bthl,ld->bhtd', q_lat, Wq_up_e)
        k_c = jnp.einsum('bthl,ld->bhtd', k_lat, Wk_up_c)
        k_e = jnp.einsum('bthl,ld->bhtd', k_lat, Wk_up_e)
        v = jnp.einsum('bthl,ld->bhtd', v_lat, Wv_up)
        cos, sin = _rope_cache(t, DHE)
        q = jnp.concatenate([q_c, _apply_rope(q_e, cos, sin)], axis=-1)
        k = jnp.concatenate([k_c, _apply_rope(k_e, cos, sin)], axis=-1)
        scale = 1.0 / math.sqrt(DH)
        scores = jnp.einsum('bhqd,bhkd->bhqk', q, k) * scale
        causal = jnp.tril(jnp.ones((t, t), dtype=bool))
        scores = jnp.where(causal[None, None], scores, -jnp.inf)
        att = jax.nn.softmax(scores, axis=-1)
        y = jnp.einsum('bhqk,bhkd->bhqd', att, v)
        y = y.transpose(0, 2, 1, 3).reshape(b, t, c)
        return y @ Wc

    def _L3_ffn_ref(x, router_w, router_b, expert_up, expert_down):
        import jax, jax.numpy as jnp
        import numpy as np
        D_MODEL = 128
        N_EXPERTS = 8
        TOP_K = 2
        B, S, D = x.shape
        E = expert_up.shape[0]
        x_flat = x.reshape(-1, D)
        logits = x_flat @ router_w + router_b
        probs = jax.nn.softmax(logits, axis=-1)
        top_w, top_idx = jax.lax.top_k(probs, TOP_K)
        comb = jnp.sum(top_w[..., None] * jax.nn.one_hot(top_idx, E, dtype=x.dtype), axis=1)
        output = jnp.zeros_like(x_flat)
        for e in range(E):
            h = jax.nn.gelu(x_flat @ expert_up[e].T, approximate=False)
            out_e = h @ expert_down[e].T
            output = output + comb[:, e:e + 1] * out_e
        return output.reshape(B, S, D)
    x = L0_attn_x
    xn = _layernorm(x, axis=-1)
    s = _L0_attn_ref(xn, L0_attn_w_q, L0_attn_w_k, L0_attn_w_v1, L0_attn_w_v2)
    g = _silu(_L0_ffn_ref(xn, L0_ffn_w_gate, L0_ffn_w_up, L0_ffn_w_down))
    x = x + s * g
    xn = _layernorm(x, axis=-1)
    s = _L1_attn_ref(xn, L1_attn_gamma, L1_attn_beta, L1_attn_Wq, L1_attn_Wv, L1_attn_Wr, L1_attn_u_bias, L1_attn_v_bias, L1_attn_Wout, L1_attn_bout)
    g = _silu(_L1_ffn_ref(xn, L1_ffn_w_gate, L1_ffn_w_up, L1_ffn_w_down))
    x = x + s * g
    xn = _layernorm(x, axis=-1)
    s = _L2_attn_ref(xn, L2_attn_w_attn, L2_attn_w_proj, L2_attn_embk, L2_attn_embv)
    g = _silu(_L2_ffn_ref(xn, L2_ffn_w_gate, L2_ffn_w_up, L2_ffn_w_down))
    x = x + s * g
    xn = _layernorm(x, axis=-1)
    s = _L3_attn_ref(xn, L3_attn_Wq_down, L3_attn_Wk_down, L3_attn_Wv_down, L3_attn_Wq_up_c, L3_attn_Wq_up_e, L3_attn_Wk_up_c, L3_attn_Wk_up_e, L3_attn_Wv_up, L3_attn_Wc)
    g = _silu(_L3_ffn_ref(xn, L3_ffn_router_w, L3_ffn_router_b, L3_ffn_expert_up, L3_ffn_expert_down))
    x = x + s * g
    return x

_drawn_inputs = setup_inputs


def setup_inputs(seed=0):
    import zlib

    import numpy as np

    out = dict(_drawn_inputs(seed))
    spreads = {'L1_attn_gamma': (1.0, 0.6),
     'L1_attn_beta': (0.0, 0.8),
     'L1_attn_bout': (0.0, 0.8),
     'L3_ffn_router_b': (0.0, 0.8)}
    factors = {'L1_attn_Wq': 8.0,
     'L1_attn_Wv': 8.0,
     'L1_attn_Wr': 8.0,
     'L1_attn_u_bias': 30.676,
     'L1_attn_v_bias': 180.231,
     'L1_attn_Wout': 8.0,
     'L1_ffn_w_gate': 8.0,
     'L1_ffn_w_up': 8.0,
     'L1_ffn_w_down': 8.0,
     'L2_attn_w_attn': 8.0,
     'L2_attn_w_proj': 8.0,
     'L2_attn_embk': 8.0,
     'L2_attn_embv': 8.0,
     'L2_ffn_w_gate': 8.0,
     'L2_ffn_w_up': 8.0,
     'L2_ffn_w_down': 8.0,
     'L3_attn_Wq_down': 8.0,
     'L3_attn_Wk_down': 8.0,
     'L3_attn_Wv_down': 8.0,
     'L3_attn_Wq_up_c': 8.0,
     'L3_attn_Wq_up_e': 8.0,
     'L3_attn_Wk_up_c': 8.0,
     'L3_attn_Wk_up_e': 8.0,
     'L3_attn_Wv_up': 8.0,
     'L3_attn_Wc': 8.0,
     'L3_ffn_router_w': 8.0,
     'L3_ffn_expert_up': 8.0,
     'L3_ffn_expert_down': 8.0}
    for name, (base, spread) in spreads.items():
        noise = np.random.default_rng([zlib.crc32(name.encode()), seed]).standard_normal(out[name].shape)
        drawn = base * np.exp(spread * noise) if base else spread * noise
        out[name] = jnp.asarray(drawn.astype(out[name].dtype))
    for name, factor in factors.items():
        out[name] = (out[name] * factor).astype(out[name].dtype)
    return out
```

```python
from contextlib import ExitStack, contextmanager

import numpy as np

import concourse.bass as bass
from concourse import mybir

F32 = mybir.dt.float32
BF16 = mybir.dt.bfloat16
I32 = mybir.dt.int32
ALU = mybir.AluOpType
ACT = mybir.ActivationFunctionType
AX = mybir.AxisListType

P = 128
D = 128
B, S = 8, 512
NT = S // P
EPS = 1e-5
BIG = 1e30


class Event:

    def __init__(self, scope, name, per, credit=False, step=1):
        self.sem = scope.sem(name)
        self.per, self.step = per * step, step
        self.base = self.per if credit else 0

    def at(self, i, n):
        return self.sem, i * self.per + self.base + n * self.step


class Chain:

    def __init__(self, eng, event, i):
        self.eng, self.event, self.i, self.n = eng, event, i, 0

    def then(self, instruction):
        self.n += 1
        instruction.then_inc(self.event.sem, 1)
        self.eng.wait_ge(*self.event.at(self.i, self.n))

    def done(self):
        assert self.n == self.event.per, f"chain of {self.n} steps"


class Scope:

    def __init__(self, nc, stack, prefix):
        self.nc, self.stack, self.prefix = nc, stack, prefix
        self.semaphores = []
        stack.callback(self.clear)

    def clear(self):
        self.nc.clear_and_free_semaphores(self.semaphores)
        self.nc.all_engine_barrier()

    def sb(self, name, shape, dt=F32):
        return self.stack.enter_context(self.nc.sbuf_tensor(self.prefix + name, shape, dt))

    def ps(self, name, shape, dt=F32):
        return self.stack.enter_context(self.nc.psum_tensor(self.prefix + name, shape, dt))

    def sem(self, name):
        self.semaphores.append(self.nc.alloc_semaphore(name=self.prefix + name))
        return self.semaphores[-1]

    def ev(self, name, per, credit=False):
        return Event(self, name, per, credit)

    def ev16(self, name, per):
        return Event(self, name, per, step=16)


def rows(x, i):
    return x.rearrange("(b t p) d -> b p t d", b=B, p=P)[i, :, :, :]


def quantise(dve, link, q, src, dst, n):
    nb = n // 16
    blocks = lambda z: z.rearrange("p (b k) -> p b k", k=16)
    each = lambda z: z[:, 0:nb].unsqueeze(2).to_broadcast([P, nb, 16])
    norm, mag, grid, low = q.norm[:, 0:n], q.mag[:, 0:n], q.grid[:, 0:n], q.low[:, 0:n]
    link.then(dve.tensor_reduce(q.peak[:, 0:nb], blocks(src), AX.X, ALU.max, apply_absolute_value=True))
    yield
    link.then(dve.tensor_scalar(q.scale[:, 0:nb], q.peak[:, 0:nb], float(np.float32(1 / 6)), 1e-12, ALU.mult, ALU.max))
    yield
    link.then(dve.reciprocal(q.rscale[:, 0:nb], q.scale[:, 0:nb]))
    yield
    link.then(dve.tensor_tensor(blocks(norm), blocks(src), each(q.rscale), ALU.mult))
    yield
    link.then(dve.tensor_scalar(mag.bitcast(I32), norm.bitcast(I32), 0x7FFFFFFF, None, ALU.bitwise_and))
    yield
    link.then(dve.tensor_scalar(grid, mag, 1.0, None, ALU.max))
    yield
    dve.tensor_scalar(low, mag, 0.25, 0.5, ALU.is_gt, ALU.mult)
    link.then(dve.tensor_tensor(grid.bitcast(I32), grid.bitcast(I32), q.half_step[:, 0:n], ALU.add))
    yield
    link.then(dve.tensor_scalar(grid.bitcast(I32), grid.bitcast(I32), -0x400000, None, ALU.bitwise_and))
    yield
    link.then(dve.scalar_tensor_tensor(grid, mag, 0.75, grid, ALU.is_gt, ALU.mult))
    yield
    link.then(dve.tensor_tensor(grid, grid, low, ALU.max))
    yield
    link.then(dve.scalar_tensor_tensor(grid.bitcast(I32), norm.bitcast(I32), -0x80000000, grid.bitcast(I32), ALU.bitwise_and, ALU.bitwise_or))
    yield
    link.then(dve.tensor_tensor(blocks(dst), blocks(grid), each(q.scale), ALU.mult))
    yield


QUANTISE_STEPS = 12


class QuantBuffers:
    def __init__(self, m, n):
        self.norm, self.mag, self.grid, self.low = [m.sb("q_" + s, [P, n]) for s in ("norm", "mag", "grid", "low")]
        self.half_step = m.sb("q_half_step", [P, n], I32)
        self.peak, self.scale, self.rscale = [m.sb("q_" + s, [P, n // 16]) for s in ("peak", "scale", "rscale")]


HN, HD = 16, 8
ITEMS = HN * NT
TERMS = ((0, 0), (0, 1), (1, 0), (1, 1), (0, 2), (2, 0))
KR6 = len(TERMS) * HD
SB, TB = 3, 2


def split3(eng, link, src, parts, rest):
    link.then(eng.tensor_copy(parts[0], src))
    link.then(eng.tensor_tensor(rest, src, parts[0], ALU.subtract))
    link.then(eng.tensor_copy(parts[1], rest))
    link.then(eng.tensor_tensor(parts[2], rest, parts[1], ALU.subtract))


def layer0(nc, w, x_in, x_out):
    KD, HID = 64, 384
    HC = HID // P
    with ExitStack() as stack:
        m = Scope(nc, stack, "a_")
        ident, maskb, identb = m.sb("ident", [P, P]), m.sb("maskb", [P, P], BF16), m.sb("identb", [P, P], BF16)
        wq, wk = m.sb("wq", [P, KD]), m.sb("wk", [P, KD])
        wv1T, wv2, wv = m.sb("wv1T", [KD, P]), m.sb("wv2", [KD, P]), m.sb("wv", [P, P])
        wint = [m.sb(f"wint{n}", [P, HID], I32) for n in range(3)]
        wg, wu, wd = [m.sb(n, [P, HID]) for n in ("wg", "wu", "wd")]
        half, eps = m.sb("half", [P, NT]), m.sb("eps", [P, NT])
        x, spare = m.sb("x", [P, NT, D]), m.sb("spare", [P, 1])
        stat, mv, rstd = m.sb("stat", [P, NT, 6]), m.sb("mv", [P, NT, 2]), m.sb("rstd", [P, NT])
        xn, xnT = m.sb("xn", [P, NT, D]), m.sb("xnT", [P, S])
        qT, kT, v = m.sb("qT", [KD, S]), m.sb("kT", [KD, S]), m.sb("v", [P, NT, D])
        th, act_in, hT = m.sb("th", [P, 2, S]), m.sb("act_in", [P, S]), m.sb("hT", [P, HC, S])
        low, total, inv = m.sb("low", [P, NT]), m.sb("total", [P, NT]), m.sb("inv", [P, NT])
        prob, probT = m.sb("prob", [P, 2, S]), m.sb("probT", [P, 2, S])
        s_out, g_a, x_new = m.sb("s_out", [P, NT, D]), m.sb("g_a", [P, NT, D]), m.sb("x_new", [P, NT, D])
        g_th = m.sb("g_th", [P, NT, D])
        pX, pQ, pK, pV = [m.ps(n, [P, S]) for n in ("pX", "pQ", "pK", "pV")]
        pS, pP = m.ps("pS", [P, 2, S]), m.ps("pP", [P, 2, S])
        pY, pF, pG, pU = pX, pQ, pK, pV

        loaded, pool_set, dve_set = m.sem("loaded"), m.sem("pool_set"), m.sem("dve_set")
        wv_made, x_read, x_sent = m.sem("wv_made"), m.sem("x_read"), m.sem("x_sent")
        centred = m.ev("centred", 1)
        rstd_made = m.ev("rstd_made", 2)
        xn_made = m.ev("xn_made", 1)
        xT_ready = m.ev("xT_ready", 1)
        xT_kept = m.ev("xT_kept", 1)
        qkv_ready = m.ev("qkv_ready", 3)
        q_kept = m.ev("q_kept", 1)
        kv_kept = m.ev("kv_kept", 2)
        gu_ready = m.ev("gu_ready", HC)
        gate_tanh = m.ev("gate_tanh", HC)
        h_made = m.ev("h_made", HC)
        scored = m.ev("scored", NT)
        low_made = m.ev("low_made", NT)
        exp_made = m.ev("exp_made", NT)
        probT_ready = m.ev("probT_ready", NT)
        probT_kept = m.ev("probT_kept", NT)
        attended = m.ev("attended", NT)
        ffn_ready = m.ev("ffn_ready", 1)
        ffn_tanh = m.ev("ffn_tanh", 1)
        finished = m.ev("finished", 1, credit=True)
        chain = m.ev("chain", 9)
        stored = m.ev("stored", 1, credit=True)
        weights = [(ident[:, :], w["ident"]), (identb[:, :], w["identb"]), (maskb[:, :], w["maskb"]),
                   (wq[:, :], w["L0_attn_w_q"]), (wk[:, :], w["L0_attn_w_k"]),
                   (wv1T[:, :], w["L0_wv1T"]), (wv2[:, :], w["L0_attn_w_v2"]),
                   (wint[0][:, :], w["L0_wgT"]), (wint[1][:, :], w["L0_wuT"]),
                   (wint[2][:, :].rearrange("p (c d) -> p c d", d=D), w["L0_wdT"].rearrange("(c p) d -> p c d", p=P))]
        with nc.Block() as block:
            @block.sync
            def _(sp):
                for dst, src in weights:
                    sp.dma_start(dst, src).then_inc(loaded, 16)
                sp.wait_ge(loaded, 16 * len(weights))
                with sp.Fori(0, B) as i:
                    sp.wait_ge(*finished.at(i, 0))
                    sp.nop()
                    sp.dma_start(x[:, :, :], rows(x_in, i)).then_inc(x_read, 16)

            @block.gpsimd
            def _(pool):
                pool.memset(half[:, :], -0.5).then_inc(pool_set, 1)
                pool.memset(eps[:, :], EPS).then_inc(pool_set, 1)
                pool.sem_inc(stored.sem, 1)
                pool.wait_ge(pool_set, 2)
                with pool.Fori(0, B) as i:
                    pool.wait_ge(*centred.at(i, 1))
                    pool.tensor_tensor(rstd[:, :], mv[:, :, 1], eps[:, :], ALU.add).then_inc(rstd_made.sem, 1)
                    pool.wait_ge(*rstd_made.at(i, 1))
                    pool.tensor_tensor(rstd[:, :], rstd[:, :], half[:, :], ALU.pow).then_inc(rstd_made.sem, 1)
                    pool.wait_ge(*finished.at(i, 1))
                    pool.dma_start(rows(x_out, i), x_new[:, :, :]).then_inc(x_sent, 16)
                    pool.wait_ge(x_sent, i * 16 + 16)
                    pool.sem_inc(stored.sem, 1)

            @block.vector
            def _(dve):
                dve.wait_ge(loaded, 16 * len(weights))
                for src, dst in zip(wint, (wg, wu, wd)):
                    dve.tensor_scalar(dst[:, :], src[:, :], float(np.float32(1.0 / 127.0)), None, ALU.mult)
                dve.wait_ge(wv_made, 1)
                dve.tensor_copy(wv[:, :], pV[:, 0:D]).then_inc(dve_set, 1)
                dve.sem_inc(finished.sem, 1)
                with dve.Fori(0, B) as i:
                    link = Chain(dve, chain, i)
                    dve.wait_ge(x_read, i * 16 + 16)
                    for t in range(NT):
                        last = dve.bn_stats(stat[:, t, :], x[:, t, :])
                    link.then(last)
                    dve.memset(spare[:, :], 0.0)
                    for t in range(NT):
                        last = dve.bn_aggr(mv[:, t, :], stat[:, t, :])
                    last.then_inc(centred.sem, 1)
                    dve.wait_ge(*rstd_made.at(i, 2))
                    for t in range(NT):
                        last = dve.tensor_scalar(xn[:, t, :], x[:, t, :], mv[:, t, 0:1], rstd[:, t:t + 1], ALU.subtract, ALU.mult)
                    last.then_inc(xn_made.sem, 1)
                    dve.wait_ge(*qkv_ready.at(i, 2))
                    dve.tensor_scalar(kT[:, :], pK[0:KD, :], -float(KD) ** -0.5, None, ALU.mult).then_inc(kv_kept.sem, 1)
                    dve.wait_ge(*qkv_ready.at(i, 3))
                    dve.tensor_copy(v[:, :, :], pV[:, :].rearrange("p (t d) -> p t d", t=NT)).then_inc(kv_kept.sem, 1)

                    def hidden(c):
                        dve.wait_ge(*gate_tanh.at(i, c + 1))
                        link.then(dve.scalar_tensor_tensor(act_in[:, :], th[:, c % 2, :], 1.0, pG[:, :], ALU.add, ALU.mult))
                        dve.scalar_tensor_tensor(hT[:, c, :], act_in[:, :], 0.5, pU[:, :], ALU.mult, ALU.mult).then_inc(h_made.sem, 1)

                    def lowest(t):
                        dve.wait_ge(*scored.at(i, t + 1))
                        dve.tensor_reduce(low[:, t:t + 1], pS[:, t % 2, 0:(t + 1) * P], AX.X, ALU.min).then_inc(low_made.sem, 1)

                    def keep_probT(t):
                        dve.wait_ge(*probT_ready.at(i, t + 1))
                        dve.tensor_copy(probT[:, t % 2, 0:(t + 1) * P], pP[:, t % 2, 0:(t + 1) * P]).then_inc(probT_kept.sem, 1)

                    hidden(0)
                    lowest(0)
                    lowest(1)
                    hidden(1)
                    keep_probT(0)
                    lowest(2)
                    hidden(2)
                    keep_probT(1)
                    lowest(3)
                    keep_probT(2)
                    keep_probT(3)
                    dve.wait_ge(*exp_made.at(i, NT))
                    link.then(dve.reciprocal(inv[:, :], total[:, :]))
                    dve.wait_ge(*attended.at(i, NT))
                    link.then(dve.tensor_tensor(s_out[:, :, :], pY[:, :].rearrange("p (t d) -> p t d", t=NT),
                                                inv[:, :].unsqueeze(2).to_broadcast([P, NT, D]), ALU.mult))
                    dve.wait_ge(*ffn_tanh.at(i, 1))
                    link.then(dve.scalar_tensor_tensor(g_a[:, :, :], g_th[:, :, :], 1.0,
                                                       pF[:, :].rearrange("p (t d) -> p t d", t=NT), ALU.add, ALU.mult))
                    link.then(dve.scalar_tensor_tensor(g_a[:, :, :], g_a[:, :, :], 0.5, s_out[:, :, :], ALU.mult, ALU.mult))
                    dve.wait_ge(*stored.at(i, 0))
                    link.then(dve.tensor_tensor(x_new[:, :, :], g_a[:, :, :], x[:, :, :], ALU.add))
                    dve.sem_inc(finished.sem, 1)
                    link.done()

            @block.scalar
            def _(act):
                with act.Fori(0, B) as i:
                    act.wait_ge(*xT_ready.at(i, 1))
                    act.copy(xnT[:, :], pX[:, :]).then_inc(xT_kept.sem, 1)
                    act.wait_ge(*qkv_ready.at(i, 1))
                    act.copy(qT[:, :], pQ[0:KD, :]).then_inc(q_kept.sem, 1)

                    def gate(c):
                        act.wait_ge(*gu_ready.at(i, c + 1))
                        act.activation(th[:, c % 2, :], pG[:, :], ACT.Tanh, scale=0.5).then_inc(gate_tanh.sem, 1)

                    def exps(t):
                        act.wait_ge(*low_made.at(i, t + 1))
                        if t >= 2:
                            act.wait_ge(*probT_ready.at(i, t - 1))
                        n = (t + 1) * P
                        act.activation(prob[:, t % 2, 0:n], pS[:, t % 2, 0:n], ACT.Exp, bias=low[:, t:t + 1], scale=-1.0,
                                       accum_out=total[:, t:t + 1]).then_inc(exp_made.sem, 1)

                    gate(0)
                    exps(0)
                    exps(1)
                    gate(1)
                    exps(2)
                    gate(2)
                    exps(3)
                    act.wait_ge(*ffn_ready.at(i, 1))
                    act.activation(g_th[:, :, :], pF[:, :].rearrange("p (t d) -> p t d", t=NT), ACT.Tanh, scale=0.5).then_inc(ffn_tanh.sem, 1)

            @block.tensor
            def _(pe):
                pe.wait_ge(loaded, 16 * len(weights))
                pe.matmul(pV[:, 0:D], wv1T[:, :], wv2[:, :], start=True, stop=True).then_inc(wv_made, 1)
                pe.wait_ge(dve_set, 1)
                with pe.Fori(0, B) as i:
                    pe.wait_ge(*xn_made.at(i, 1))
                    pe.wait_ge(*finished.at(i, 0))
                    for t in range(NT):
                        last = pe.transpose(pX[:, t * P:(t + 1) * P], xn[:, t, :], ident[:, :])
                    last.then_inc(xT_ready.sem, 1)
                    pe.wait_ge(*xT_kept.at(i, 1))
                    pe.matmul(pQ[0:KD, :], wq[:, :], xnT[:, :], start=True, stop=True).then_inc(qkv_ready.sem, 1)
                    pe.matmul(pK[0:KD, :], wk[:, :], xnT[:, :], start=True, stop=True).then_inc(qkv_ready.sem, 1)
                    for t in range(NT):
                        last = pe.matmul(pV[:, t * P:(t + 1) * P], xnT[:, t * P:(t + 1) * P], wv[:, :], start=True, stop=True)
                    last.then_inc(qkv_ready.sem, 1)

                    def gate_up(c):
                        if c == 0:
                            pe.wait_ge(*kv_kept.at(i, 2))
                        else:
                            pe.wait_ge(*h_made.at(i, c))
                        pe.matmul(pG[:, :], wg[:, c * P:(c + 1) * P], xnT[:, :], start=True, stop=True)
                        pe.matmul(pU[:, :], wu[:, c * P:(c + 1) * P], xnT[:, :], start=True, stop=True).then_inc(gu_ready.sem, 1)

                    def scores(t):
                        if t == 0:
                            pe.wait_ge(*q_kept.at(i, 1))
                        if t >= 2:
                            pe.wait_ge(*exp_made.at(i, t - 1))
                        n = (t + 1) * P
                        pe.matmul(pS[:, t % 2, 0:n], qT[:, t * P:n], kT[:, 0:n], start=True, stop=True)
                        pe.matmul(pS[:, t % 2, t * P:n], identb[:, :], maskb[:, :], start=False, stop=True,
                                  skip_group_check=True).then_inc(scored.sem, 1)

                    def turn(t):
                        pe.wait_ge(*exp_made.at(i, t + 1))
                        if t >= 2:
                            pe.wait_ge(*probT_kept.at(i, t - 1))
                        for u in range(t + 1):
                            last = pe.transpose(pP[:, t % 2, u * P:(u + 1) * P], prob[:, t % 2, u * P:(u + 1) * P], ident[:, :])
                        last.then_inc(probT_ready.sem, 1)

                    def attend(t):
                        pe.wait_ge(*probT_kept.at(i, t + 1))
                        for u in range(t + 1):
                            last = pe.matmul(pY[:, t * P:(t + 1) * P], probT[:, t % 2, u * P:(u + 1) * P], v[:, u, :],
                                             start=(u == 0), stop=(u == t))
                        last.then_inc(attended.sem, 1)

                    gate_up(0)
                    scores(0)
                    scores(1)
                    turn(0)
                    gate_up(1)
                    scores(2)
                    attend(0)
                    turn(1)
                    gate_up(2)
                    scores(3)
                    attend(1)
                    turn(2)
                    attend(2)
                    turn(3)
                    attend(3)
                    pe.wait_ge(*h_made.at(i, HC))
                    for t in range(NT):
                        for c in range(HC):
                            last = pe.matmul(pF[:, t * P:(t + 1) * P], hT[:, c, t * P:(t + 1) * P], wd[:, c * D:(c + 1) * D],
                                             start=(c == 0), stop=(c == HC - 1))
                    last.then_inc(ffn_ready.sem, 1)


HID4 = 352
HID4P = 384
HC4 = HID4P // P


def layer1(nc, w, x_in, x_out):
    H, F = 8, 128
    BB = 16
    G = NT
    C = float(np.float32(1 / np.sqrt(D)))
    KR = B * B + BB
    with ExitStack() as stack:
        m = Scope(nc, stack, "b_")
        ident, ones, bout = m.sb("ident", [P, P]), m.sb("ones", [1, P]), m.sb("bout", [1, D])
        wq, wqT = m.sb("wq", [P, H * F]), m.sb("wqT", [P, H, D])
        wr = m.sb("wr", [P, H * F])
        wvT, wout, wvo = m.sb("wvT", [P, H, D]), m.sb("wout", [P, H, D]), m.sb("wvo", [P, H * D])
        peT = m.sb("peT", [P, B])
        uT, vT, gammaT, betaT = m.sb("uT", [P, H]), m.sb("vT", [P, H]), m.sb("gammaT", [P, 1]), m.sb("betaT", [P, 1])
        rel, gpos, gbias = m.sb("rel", [P, H, B, B]), m.sb("gpos", [P, H, B * B]), m.sb("gbias", [B * B, H])
        gnext, is_own, is_next = m.sb("gnext", [P, H, B * B]), m.sb("is_own", [P, B * B]), m.sb("is_next", [P, B * B])
        late = m.sb("late", [B * B, H, P])
        own_i, place = m.sb("own_i", [B * B, S]), m.sb("place", [KR, P])
        wnat, wqd = m.sb("wnat", [P, 2 * HID4P + HID4]), m.sb("wqd", [P, 2 * HID4P + HID4])
        wg, wu, wd = m.sb("wg", [P, HID4P]), m.sb("wu", [P, HID4P]), m.sb("wd", [P, HC4, D])
        half, eps, spare = m.sb("half", [P, NT]), m.sb("eps", [P, NT]), m.sb("spare", [P, 1])
        q4 = QuantBuffers(m, G * HID4)
        x, stat, mv, rstd = m.sb("x", [P, G, D]), m.sb("stat", [P, G, 6]), m.sb("mv", [P, G, 2]), m.sb("rstd", [P, G])
        xn, hh, hT = m.sb("xn", [P, G * D]), m.sb("hh", [P, G, D]), m.sb("hT", [P, S])
        xq, xqT, vo = m.sb("xq", [P, G * D]), m.sb("xqT", [P, S]), m.sb("vo", [P, G, H * D])
        qu, kT, pos = m.sb("qu", [P, 2, S]), m.sb("kT", [P, 2, S]), m.sb("pos", [KR, 2, S])
        top, total, inv = [m.sb(n, [P, 2, G]) for n in ("top", "total", "inv")]
        prob, probT = m.sb("prob", [P, 2, S]), m.sb("probT", [P, 2, S])
        th, act_in = m.sb("th", [P, 2, HID4]), m.sb("act_in", [P, HID4])
        hid, hidT = m.sb("hid", [P, G * HID4]), m.sb("hidT", [P, HC4, S])
        g_th, g_a, x_new = m.sb("g_th", [P, S]), m.sb("g_a", [P, S]), m.sb("x_new", [P, G, D])
        pA, pB, pQ, pR, pT, pO = [m.ps(n, [P, S]) for n in ("pA", "pB", "pQ", "pR", "pT", "pO")]
        pS = m.ps("pS", [P, 2, S])
        loaded, dve_set, pool_set, pe_set, x_read, x_sent = [m.sem(n) for n in ("loaded", "dve_set", "pool_set", "pe_set", "x_read", "x_sent")]
        late_read = m.sem("late_read")
        made_weights = m.ev("made_weights", QUANTISE_STEPS)
        centred, rstd_made = m.ev("centred", 2), m.ev("rstd_made", 4)
        hh_made, xq_made = m.ev("hh_made", 1), m.ev("xq_made", 1)
        turned_in = m.ev("turned_in", 2)
        xqT_kept, hT_kept = m.ev("xqT_kept", 1), m.ev("hT_kept", 1)
        gu_ready, gate_tanh, hid_made = m.ev("gu_ready", G), m.ev("gate_tanh", G), m.ev("hid_made", G)
        vo_ready, vo_kept = m.ev("vo_ready", 2 * G), m.ev("vo_kept", 2 * G)
        q_ready, pos_ready = m.ev("q_ready", H), m.ev("pos_ready", H)
        k_kept, qu_made, pos_made = m.ev("k_kept", H), m.ev("qu_made", H), m.ev("pos_made", H)
        scored, top_made, exp_made = m.ev("scored", H), m.ev("top_made", H), m.ev("exp_made", H)
        own_made = m.ev("own_made", H)
        inv_made, normed = m.ev("inv_made", H), m.ev("normed", H)
        probT_ready, probT_kept, attended = m.ev("probT_ready", H), m.ev("probT_kept", H), m.ev("attended", H)
        hid_quantised = m.ev("hid_quantised", 1)
        hidT_ready, hidT_kept = m.ev("hidT_ready", HC4), m.ev("hidT_kept", HC4)
        ffn_ready, ffn_tanh = m.ev("ffn_ready", 1), m.ev("ffn_tanh", 1)
        finished = m.ev("finished", 1, credit=True)
        stored = m.ev("stored", 1, credit=True)
        chain = m.ev("chain", 2 + 1 + 2 * QUANTISE_STEPS + G + 3)
        of_batch = lambda t, c, a: t.rearrange("(a c g b) d -> c a b g d", a=B, c=B, g=G)[c, a, :, :, :]
        heads = lambda t: t.rearrange("(h f) d -> f h d", f=F)
        weights = [(ident[:, :], w["ident"]), (ones[:, :], w["ones_row"]), (bout[:, :], w["L1_bout"]), (wq[:, :], w["L1_attn_Wq"]),
                   (wqT[:, :, :], heads(w["L1_WqT"])), (wr[:, :], w["L1_attn_Wr"]), (wvT[:, :, :], heads(w["L1_WvT"])),
                   (wout[:, :, :], heads(w["L1_attn_Wout"])), (peT[:, :], w["L1_peT"]), (uT[:, :], w["L1_uT"]),
                   (vT[:, :], w["L1_vT"]), (gammaT[:, :], w["L1_gammaT"]), (betaT[:, :], w["L1_betaT"]),
                   (own_i[:, :], w["L1_own_i"]), (is_own[:, :], w["L1_is_own"]), (is_next[:, :], w["L1_is_next"]), (place[:, :], w["L1_place"]),
                   (pos[B * B:KR, 0, :], w["L1_own_b"]), (pos[B * B:KR, 1, :], w["L1_own_b"]),
                   (wnat[:, 0:HID4P].rearrange("p (c d) -> p c d", c=HC4), w["L1_wg"].rearrange("(c p) d -> p c d", p=P)),
                   (wnat[:, HID4P:2 * HID4P].rearrange("p (c d) -> p c d", c=HC4), w["L1_wu"].rearrange("(c p) d -> p c d", p=P)),
                   (wnat[:, 2 * HID4P:], w["L1_ffn_w_down"])]
        SETS = 8
        with nc.Block() as block:
            @block.sync
            def _(sp):
                for dst, src in weights:
                    sp.dma_start(dst, src).then_inc(loaded, 16)
                with sp.Fori(0, B) as i:
                    sp.wait_ge(*finished.at(i, 0))
                    sp.nop()
                    for a in range(B):
                        sp.dma_start(x[a * BB:(a + 1) * BB, :, :], of_batch(x_in, i, a)).then_inc(x_read, 16)
                    sp.dma_start(late[:, :, :].rearrange("p h t -> p (h t)"), w["L1_late"][i, :].partition_broadcast(B * B)).then_inc(late_read, 16)

            @block.gpsimd
            def _(pool):
                pool.memset(half[:, :], -0.5).then_inc(pool_set, 1)
                pool.memset(eps[:, :], EPS).then_inc(pool_set, 1)
                pool.memset(q4.half_step[:, :], 0x1FFFFF).then_inc(pool_set, 1)
                pool.sem_inc(stored.sem, 1)
                pool.wait_ge(pool_set, 3)
                with pool.Fori(0, B) as i:
                    for k in range(2):
                        pool.wait_ge(*centred.at(i, k + 1))
                        pool.tensor_tensor(rstd[:, :], mv[:, :, 1], eps[:, :], ALU.add).then_inc(rstd_made.sem, 1)
                        pool.wait_ge(*rstd_made.at(i, 2 * k + 1))
                        pool.tensor_tensor(rstd[:, :], rstd[:, :], half[:, :], ALU.pow).then_inc(rstd_made.sem, 1)
                    for n in range(H):
                        pool.wait_ge(*inv_made.at(i, n + 1))
                        z = prob[:, n % 2, :].rearrange("p (g j) -> p g j", g=G)
                        pool.tensor_tensor(z, z, inv[:, n % 2, :].unsqueeze(2).to_broadcast([P, G, P]), ALU.mult).then_inc(normed.sem, 1)
                    pool.wait_ge(*finished.at(i, 1))
                    for a in range(B):
                        pool.dma_start(of_batch(x_out, i, a), x_new[a * BB:(a + 1) * BB, :, :]).then_inc(x_sent, 16)
                    pool.wait_ge(x_sent, i * 16 * B + 16 * B)
                    pool.sem_inc(stored.sem, 1)

            @block.vector
            def _(dve):
                dve.wait_ge(loaded, 16 * len(weights))
                dve.wait_ge(pool_set, 3)
                for _ in quantise(dve, Chain(dve, made_weights, 0), q4, wnat[:, :], wqd[:, :], 2 * HID4P + HID4):
                    pass
                dve.sem_inc(dve_set, 1)
                dve.wait_ge(pe_set, 1)
                dve.tensor_copy(rel[:, :, :, :], pA[:, 0:H * B].rearrange("p (h j) -> p h j", h=H).unsqueeze(2).to_broadcast([P, H, B, B])).then_inc(dve_set, 1)
                dve.wait_ge(pe_set, 2)
                for n in range(H):
                    for dst, part in ((gpos, is_own), (gnext, is_next)):
                        dve.tensor_tensor(dst[:, n, :].rearrange("p (a j) -> p a j", a=B),
                                          pB[:, n * B:(n + 1) * B].unsqueeze(1).to_broadcast([P, B, B]),
                                          part[:, :].rearrange("p (a j) -> p a j", a=B), ALU.mult)
                dve.tensor_copy(gbias[:, :], pQ[0:B * B, 0:H])
                dve.tensor_copy(wvo[:, 0:S], pS[:, 0, :])
                dve.tensor_copy(wvo[:, S:2 * S], pS[:, 1, :])
                dve.tensor_copy(wg[:, :], pR[:, 0:HID4P])
                dve.tensor_copy(wu[:, :], pT[:, 0:HID4P])
                dve.tensor_copy(wd[:, 0:2, :], pO[:, 0:2 * D].rearrange("p (c d) -> p c d", c=2))
                dve.tensor_copy(wd[0:HID4 - 2 * P, 2, :], pO[0:HID4 - 2 * P, 2 * D:3 * D]).then_inc(dve_set, 1)
                dve.sem_inc(finished.sem, 1)
                with dve.Fori(0, B) as i:
                    link = Chain(dve, chain, i)

                    def stats(k, src, dst):
                        for t in range(G):
                            last = dve.bn_stats(stat[:, t, :], src(t))
                        link.then(last)
                        dve.memset(spare[:, :], 0.0)
                        for t in range(G):
                            last = dve.bn_aggr(mv[:, t, :], stat[:, t, :])
                        last.then_inc(centred.sem, 1)
                        dve.wait_ge(*rstd_made.at(i, 2 * k + 2))
                        for t in range(G):
                            last = dve.tensor_scalar(dst(t), src(t), mv[:, t, 0:1], rstd[:, t:t + 1], ALU.subtract, ALU.mult)
                        return last

                    dve.wait_ge(x_read, i * 16 * B + 16 * B)
                    link.then(stats(0, lambda t: x[:, t, :], lambda t: xn[:, t * D:(t + 1) * D]))
                    stats(1, lambda t: xn[:, t * D:(t + 1) * D], lambda t: hh[:, t, :]).then_inc(hh_made.sem, 1)
                    for _ in quantise(dve, link, q4, xn[:, :], xq[:, :], G * D):
                        pass
                    dve.sem_inc(xq_made.sem, 1)
                    dve.wait_ge(*turned_in.at(i, 2))
                    dve.tensor_scalar(hT[:, :], pB[:, :], gammaT[:, :], betaT[:, :], ALU.mult, ALU.add).then_inc(hT_kept.sem, 1)
                    for g in range(G):
                        dve.wait_ge(*gate_tanh.at(i, g + 1))
                        link.then(dve.scalar_tensor_tensor(act_in[:, :], th[:, g % 2, :], 1.0, pA[:, 0:HID4], ALU.add, ALU.mult))
                        dve.scalar_tensor_tensor(hid[:, g * HID4:(g + 1) * HID4], act_in[:, :], 0.5, pB[:, 0:HID4], ALU.mult, ALU.mult).then_inc(hid_made.sem, 1)
                    dve.wait_ge(*hid_made.at(i, G))
                    steps = quantise(dve, link, q4, hid[:, :], hid[:, :], G * HID4)

                    def operands(n):
                        dve.wait_ge(*k_kept.at(i, n + 1))
                        if n >= 2:
                            dve.wait_ge(*scored.at(i, n - 1))
                        dve.tensor_scalar(qu[:, n % 2, :], kT[:, n % 2, :], uT[:, n:n + 1], C, ALU.add, ALU.mult).then_inc(qu_made.sem, 1)
                        dve.wait_ge(*pos_ready.at(i, n + 1))
                        dve.scalar_tensor_tensor(pos[0:B * B, n % 2, :], pR[0:B * B, :], gbias[:, n:n + 1], own_i[:, :], ALU.add, ALU.mult).then_inc(own_made.sem, 1)
                        dve.wait_ge(*own_made.at(i, n + 1))
                        first = pos[0:B * B, n % 2, 0:P]
                        dve.tensor_tensor(first, first, late[:, n, :], ALU.mult).then_inc(pos_made.sem, 1)

                    dve.wait_ge(late_read, i * 16 + 16)

                    def highest(n):
                        dve.wait_ge(*scored.at(i, n + 1))
                        dve.tensor_reduce(top[:, n % 2, :], pS[:, n % 2, :].rearrange("p (g j) -> p g j", g=G), AX.X, ALU.max, negate=True).then_inc(top_made.sem, 1)

                    def inverse(n):
                        dve.wait_ge(*exp_made.at(i, n + 1))
                        dve.reciprocal(inv[:, n % 2, :], total[:, n % 2, :]).then_inc(inv_made.sem, 1)

                    for k in range(H + 2):
                        if k < H:
                            operands(k)
                        if 0 <= k - 1 < H:
                            highest(k - 1)
                        next(steps, None)
                        if 0 <= k - 2 < H:
                            inverse(k - 2)
                    for _ in steps:
                        pass
                    dve.sem_inc(hid_quantised.sem, 1)
                    dve.wait_ge(*ffn_tanh.at(i, 1))
                    link.then(dve.scalar_tensor_tensor(g_a[:, :], g_th[:, :], 1.0, pR[:, :], ALU.add, ALU.mult))
                    dve.wait_ge(*attended.at(i, H))
                    link.then(dve.scalar_tensor_tensor(g_a[:, :], g_a[:, :], 0.5, pO[:, :], ALU.mult, ALU.mult))
                    dve.wait_ge(*stored.at(i, 0))
                    link.then(dve.tensor_tensor(x_new[:, :, :], g_a[:, :].rearrange("p (g d) -> p g d", g=G), x[:, :, :], ALU.add))
                    dve.sem_inc(finished.sem, 1)
                    link.done()

            @block.scalar
            def _(act):
                with act.Fori(0, B) as i:
                    act.wait_ge(*turned_in.at(i, 1))
                    act.copy(xqT[:, :], pA[:, :]).then_inc(xqT_kept.sem, 1)
                    for g in range(G):
                        act.wait_ge(*gu_ready.at(i, g + 1))
                        act.activation(th[:, g % 2, :], pA[:, 0:HID4], ACT.Tanh, scale=0.5).then_inc(gate_tanh.sem, 1)
                        for n in range(2 * g, 2 * g + 2):
                            act.wait_ge(*vo_ready.at(i, n + 1))
                            act.copy(vo[:, g, (n % 2) * S:(n % 2 + 1) * S], pS[:, n % 2, :]).then_inc(vo_kept.sem, 1)

                    def keep_k(n):
                        act.wait_ge(*q_ready.at(i, n + 1))
                        if n >= 2:
                            act.wait_ge(*scored.at(i, n - 1))
                        act.copy(kT[:, n % 2, :], pQ[:, :]).then_inc(k_kept.sem, 1)

                    def exps(n):
                        act.wait_ge(*top_made.at(i, n + 1))
                        if n >= 2:
                            act.wait_ge(*probT_ready.at(i, n - 1))
                        for g in range(G):
                            cut = slice(g * P, (g + 1) * P)
                            last = act.activation(prob[:, n % 2, cut], pS[:, n % 2, cut], ACT.Exp, bias=top[:, n % 2, g:g + 1],
                                                  accum_out=total[:, n % 2, g:g + 1])
                        last.then_inc(exp_made.sem, 1)

                    def keep_probT(n):
                        act.wait_ge(*probT_ready.at(i, n + 1))
                        if n >= 2:
                            act.wait_ge(*attended.at(i, n - 1))
                        act.copy(probT[:, n % 2, :], pT[:, :]).then_inc(probT_kept.sem, 1)

                    for k in range(H + 3):
                        if k < H:
                            keep_k(k)
                        if 0 <= k - 1 < H:
                            exps(k - 1)
                        if 0 <= k - 2 < H:
                            keep_probT(k - 2)
                    for c in range(HC4):
                        act.wait_ge(*hidT_ready.at(i, c + 1))
                        rows_of = min(P, HID4 - c * P)
                        act.copy(hidT[0:rows_of, c, :], (pA, pB, pQ)[c][0:rows_of, :]).then_inc(hidT_kept.sem, 1)
                    act.wait_ge(*ffn_ready.at(i, 1))
                    act.activation(g_th[:, :], pR[:, :], ACT.Tanh, scale=0.5).then_inc(ffn_tanh.sem, 1)

            @block.tensor
            def _(pe):
                pe.wait_ge(loaded, 16 * len(weights))
                for n in range(H):
                    last = pe.matmul(pA[:, n * B:(n + 1) * B], wr[:, n * F:(n + 1) * F], peT[:, :], start=True, stop=True)
                last.then_inc(pe_set, 1)
                pe.wait_ge(dve_set, 2)
                for n in range(H):
                    pe.matmul(pB[:, n * B:(n + 1) * B], wqT[:, n, :], rel[:, n, 0, :], start=True, stop=True)
                    pe.matmul(pQ[0:B * B, n:n + 1], rel[:, n, :, :].rearrange("p a j -> p (a j)"), vT[:, n:n + 1], start=True, stop=True)
                    pe.matmul(pS[:, n // 4, (n % 4) * D:(n % 4 + 1) * D], wvT[:, n, :], wout[:, n, :], start=True, stop=True)
                for c in range(HC4):
                    pe.transpose(pR[:, c * P:(c + 1) * P], wqd[:, c * P:(c + 1) * P], ident[:, :])
                    pe.transpose(pT[:, c * P:(c + 1) * P], wqd[:, HID4P + c * P:HID4P + (c + 1) * P], ident[:, :])
                    rows_of = min(P, HID4 - c * P)
                    last = pe.transpose(pO[0:rows_of, c * D:(c + 1) * D], wqd[:, 2 * HID4P + c * P:2 * HID4P + c * P + rows_of], ident[:, :])
                last.then_inc(pe_set, 1)
                pe.wait_ge(dve_set, 3)
                with pe.Fori(0, B) as i:
                    pe.wait_ge(*hh_made.at(i, 1))
                    pe.wait_ge(*finished.at(i, 0))
                    pe.wait_ge(*xq_made.at(i, 1))
                    for t in range(G):
                        last = pe.transpose(pA[:, t * P:(t + 1) * P], xq[:, t * D:(t + 1) * D], ident[:, :])
                    last.then_inc(turned_in.sem, 1)
                    for t in range(G):
                        last = pe.transpose(pB[:, t * P:(t + 1) * P], hh[:, t, :], ident[:, :])
                    last.then_inc(turned_in.sem, 1)
                    pe.wait_ge(*xqT_kept.at(i, 1))
                    pe.wait_ge(*hT_kept.at(i, 1))

                    def gate_up(g):
                        if g:
                            pe.wait_ge(*hid_made.at(i, g))
                        pe.matmul(pA[:, 0:HID4], xqT[:, g * P:(g + 1) * P], wg[:, 0:HID4], start=True, stop=True)
                        pe.matmul(pB[:, 0:HID4], xqT[:, g * P:(g + 1) * P], wu[:, 0:HID4], start=True, stop=True).then_inc(gu_ready.sem, 1)

                    def value(n):
                        if n >= 2:
                            pe.wait_ge(*vo_kept.at(i, n - 1))
                        pe.matmul(pS[:, n % 2, :], hT[:, (n // 2) * P:(n // 2 + 1) * P], wvo[:, (n % 2) * S:(n % 2 + 1) * S],
                                  start=True, stop=True).then_inc(vo_ready.sem, 1)

                    for g in range(G):
                        gate_up(g)
                        value(2 * g)
                        value(2 * g + 1)

                    def queries(n):
                        if n:
                            pe.wait_ge(*k_kept.at(i, n))
                        pe.matmul(pQ[:, :], wq[:, n * F:(n + 1) * F], hT[:, :], start=True, stop=True).then_inc(q_ready.sem, 1)
                        if n:
                            pe.wait_ge(*pos_made.at(i, n))
                        pe.matmul(pR[0:B * B, :], gpos[:, n, :], hT[:, :], start=True, stop=True)
                        pe.matmul(pR[0:B * B, :].rearrange("p (g t) -> p g t", g=G)[:, :, 0:P - BB], gnext[:, n, :],
                                  hT[:, :].rearrange("p (g t) -> p g t", g=G)[:, :, BB:P], start=False, stop=True,
                                  skip_group_check=True).then_inc(pos_ready.sem, 1)

                    def scores(n):
                        pe.wait_ge(*k_kept.at(i, n + 1))
                        pe.wait_ge(*pos_made.at(i, n + 1))
                        if n >= 2:
                            pe.wait_ge(*exp_made.at(i, n - 1))
                        else:
                            pe.wait_ge(*vo_kept.at(i, 2 * G))
                        for g in range(G):
                            cut = slice(g * P, (g + 1) * P)
                            pe.matmul(pS[:, n % 2, cut], qu[:, n % 2, cut], kT[:, n % 2, cut], start=True, stop=False)
                            last = pe.matmul(pS[:, n % 2, cut], pos[:, n % 2, cut], place[:, :], start=False, stop=True)
                        last.then_inc(scored.sem, 1)

                    def turn(n):
                        pe.wait_ge(*normed.at(i, n + 1))
                        if n:
                            pe.wait_ge(*probT_kept.at(i, n))
                        for g in range(G):
                            last = pe.transpose(pT[:, g * P:(g + 1) * P], prob[:, n % 2, g * P:(g + 1) * P], ident[:, :])
                        last.then_inc(probT_ready.sem, 1)

                    def attend(n):
                        pe.wait_ge(*probT_kept.at(i, n + 1))
                        for g in range(G):
                            if n == 0:
                                pe.matmul(pO[:, g * D:(g + 1) * D], ones[:, :], bout[:, :], start=(g == 0), stop=False, skip_group_check=True)
                            last = pe.matmul(pO[:, g * D:(g + 1) * D], probT[:, n % 2, g * P:(g + 1) * P], vo[:, g, n * D:(n + 1) * D],
                                             start=False, stop=(n == H - 1), skip_group_check=True)
                        last.then_inc(attended.sem, 1)

                    for k in range(H + 4):
                        if k < H:
                            queries(k)
                        if 0 <= k - 1 < H:
                            scores(k - 1)
                        if 0 <= k - 3 < H:
                            turn(k - 3)
                        if 0 <= k - 4 < H:
                            attend(k - 4)
                    pe.wait_ge(*hid_quantised.at(i, 1))
                    for c in range(HC4):
                        rows_of = min(P, HID4 - c * P)
                        for g in range(G):
                            last = pe.transpose((pA, pB, pQ)[c][0:rows_of, g * P:(g + 1) * P],
                                                hid[:, g * HID4 + c * P:g * HID4 + c * P + rows_of], ident[:, :])
                        last.then_inc(hidT_ready.sem, 1)
                    pe.wait_ge(*hidT_kept.at(i, HC4))
                    for g in range(G):
                        for c in range(HC4):
                            rows_of = min(P, HID4 - c * P)
                            last = pe.matmul(pR[:, g * D:(g + 1) * D], hidT[0:rows_of, c, g * P:(g + 1) * P], wd[0:rows_of, c, :],
                                             start=(c == 0), stop=(c == HC4 - 1))
                    last.then_inc(ffn_ready.sem, 1)


def layer2(nc, w, x_in, x_out):
    R = P
    W = 2 * P
    SLOTS = 4
    STEP = S + P
    with ExitStack() as stack:
        m = Scope(nc, stack, "c_")
        ident, identb, maskb = m.sb("ident", [P, P]), m.sb("identb", [P, P], BF16), m.sb("maskb", [P, P], BF16)
        wqkv = m.sb("wqkv", [P, 3 * D])
        last_k, minus_last = m.sb("last_k", [P, 1]), m.sb("minus_last", [P, 1])
        place_k, place_last, place_rest = m.sb("place_k", [HD, R]), m.sb("place_last", [HD, 1]), m.sb("place_rest", [HD, R])
        place_p = [m.sb(f"place_p{j}", [HD, R], BF16) for j in range(3)]
        places = m.sb("places", [KR6, R], BF16)
        last_v, place_v, every_last_v = m.sb("last_v", [1, D]), m.sb("place_v", [R, HD]), m.sb("every_last_v", [R, HD])
        wnat, wqd = m.sb("wnat", [P, 2 * HID4P + HID4]), m.sb("wqd", [P, 2 * HID4P + HID4])
        wg, wu, wd = m.sb("wg", [P, HID4P]), m.sb("wu", [P, HID4P]), m.sb("wd", [P, HC4, D])
        q4 = QuantBuffers(m, NT * HID4)
        zeros = m.sb("zeros", [P, NT * W])
        wc = m.sb("wc", [P, D])
        ones = m.sb("ones", [1, P])
        half, eps, spare = m.sb("half", [P, NT]), m.sb("eps", [P, NT]), m.sb("spare", [P, 1])
        x, stat, mv, rstd = m.sb("x", [P, NT, D]), m.sb("stat", [P, NT, 6]), m.sb("mv", [P, NT, 2]), m.sb("rstd", [P, NT])
        xn, xnT = m.sb("xn", [P, NT, D]), m.sb("xnT", [P, S])
        qf, kf, rest_q, rest_k = [m.sb(n, [P, S]) for n in ("qf", "kf", "rest_q", "rest_k")]
        qp, kp = [[m.sb(f"{n}{j}", [P, S], BF16) for j in range(3)] for n in ("qp", "kp")]
        qs, ks = m.sb("qs", [KR6, HN, S], BF16), m.sb("ks", [KR6, HN, S], BF16)
        v = m.sb("v", [P, NT, D])
        low, total, inv = m.sb("low", [P, ITEMS]), m.sb("total", [P, ITEMS]), m.sb("inv", [P, ITEMS])
        prob, probT = m.sb("prob", [P, 3, (NT - 1) * STEP + W]), m.sb("probT", [P, 3, S])
        far = m.sb("far", [P, 2])
        by_place, rel = m.sb("by_place", [P, 2, NT, R]), m.sb("rel", [P, 3, NT, W])
        band, bandT = m.sb("band", [P, 3, NT, R]), m.sb("bandT", [P, 2, S])
        yn, yT = m.sb("yn", [P, NT, D]), m.sb("yT", [P, S])
        xq, xqT = m.sb("xq", [P, NT * D]), m.sb("xqT", [P, S])
        th, act_in = m.sb("th", [P, 2, HID4]), m.sb("act_in", [P, HID4])
        hid, hidT = m.sb("hid", [P, NT * HID4]), m.sb("hidT", [P, HC4, S])
        y_all = m.sb("y_all", [P, NT, D])
        g_th, g_a, x_new = m.sb("g_th", [P, NT, D]), m.sb("g_a", [P, NT, D]), m.sb("x_new", [P, NT, D])
        pS, pT = m.ps("pS", [P, SB, S]), m.ps("pT", [P, TB, S])
        pY, pZ, pA = m.ps("pY", [P, S]), m.ps("pZ", [P, S]), m.ps("pA", [P, S])
        q_dram = [nc.dram_tensor(f"c_q{j}", (P, S), BF16).ap() for j in range(3)]
        k_dram = [nc.dram_tensor(f"c_k{j}", (P, S), BF16).ap() for j in range(3)]

        rel_dram = nc.dram_tensor("c_rel_dram", (SLOTS, NT * P * W), F32).ap()
        band_dram = nc.dram_tensor("c_band_dram", (SLOTS, NT * P * W), F32).ap()

        def straight(dram, h):
            return dram[h % SLOTS, :].rearrange("(t p c) -> p t c", t=NT, c=W)

        def skewed(dram, h):
            whole = straight(dram, h)
            return bass.AP(whole.tensor, whole.offset + 1, [[W + 1, P], [P * W, NT], [1, R]])

        loaded, pool_set, pe_set, dve_set, x_read, x_sent = [m.sem(n) for n in ("loaded", "pool_set", "pe_set", "dve_set", "x_read", "x_sent")]
        cleared, spread = m.sem("cleared"), m.sem("spread")
        past_sp, past_pool, past_dve = m.sem("past_sp"), m.sem("past_pool"), m.sem("past_dve")
        parts_sent, terms_read = m.sem("parts_sent"), m.sem("terms_read")
        by_slot = lambda n: [m.ev16(f"{n}{slot}", HN // SLOTS) for slot in range(SLOTS)]
        rel_sent, rel_read = by_slot("rel_sent"), by_slot("rel_read")
        band_sent, band_read = by_slot("band_sent"), by_slot("band_read")
        of_head = lambda events, i, h: events[h % SLOTS].at(i, h // SLOTS + 1)
        made_weights, made_places = m.ev("made_weights", QUANTISE_STEPS), m.ev("made_places", 6)
        centred, rstd_made, xn_made = m.ev("centred", 1), m.ev("rstd_made", 2), m.ev("xn_made", 1)
        xT_ready, xT_kept = m.ev("xT_ready", 1), m.ev("xT_kept", 1)
        proj_ready = m.ev("proj_ready", 3)
        q_split, k_split = m.ev("q_split", 1), m.ev("k_split", 1)
        v_kept = m.ev("v_kept", 1)
        xq_made, xqT_ready, xqT_kept = m.ev("xq_made", 1), m.ev("xqT_ready", 1), m.ev("xqT_kept", 1)
        gu_ready, gate_tanh, hid_made = m.ev("gu_ready", NT), m.ev("gate_tanh", NT), m.ev("hid_made", NT)
        hid_quantised, hidT_ready, hidT_kept = m.ev("hid_quantised", 1), m.ev("hidT_ready", HC4), m.ev("hidT_kept", HC4)
        ffn_ready, g_tanh = m.ev("ffn_ready", 1), m.ev("g_tanh", 1)
        places_ready, places_kept = m.ev("places_ready", HN), m.ev("places_kept", HN)
        scored, low_made, exp_made = m.ev("scored", ITEMS), m.ev("low_made", ITEMS), m.ev("exp_made", ITEMS)
        far_made = m.ev("far_made", ITEMS // 2)
        probT_ready, attended = m.ev("probT_ready", ITEMS), m.ev("attended", ITEMS)
        probT_kept_act, probT_kept_dve = m.ev("probT_kept_act", ITEMS // 2), m.ev("probT_kept_dve", ITEMS // 2)
        bandT_ready, bandT_kept, band_attended = m.ev("bandT_ready", HN), m.ev("bandT_kept", HN), m.ev("band_attended", HN)
        y_made, yT_ready, yT_kept, s_ready = m.ev("y_made", 1), m.ev("yT_ready", 1), m.ev("yT_kept", 1), m.ev("s_ready", 1)
        finished, stored = m.ev("finished", 1, credit=True), m.ev("stored", 1, credit=True)
        chain = m.ev("chain", 1 + 10 + 2 * QUANTISE_STEPS + NT + 5)
        k_of = lambda n: (n % NT + 1) * P
        kept_by_act = lambda n: n % NT < 2
        at_prob = lambda n: n % NT * S + P

        def kept_wait(eng, i, n):
            kept, nth = (probT_kept_act, n % NT) if kept_by_act(n) else (probT_kept_dve, n % NT - 2)
            eng.wait_ge(*kept.at(i, 2 * (n // NT) + nth + 1))

        LEAD, LAG = 2, 3
        turns = []
        for n in range(ITEMS + NT * LAG + 1):
            if 0 <= n - 2 < ITEMS:
                turns.append(("item", n - 2))
            if n % NT == 3 and 0 <= n // NT - LAG < HN:
                turns.append(("band", n // NT - LAG))
        bank_of = {one: r % TB for r, one in enumerate(turns)}

        def bank_free(eng, i, one):
            r = turns.index(one)
            if r >= TB:
                kind, n = turns[r - TB]
                if kind == "item":
                    kept_wait(eng, i, n)
                else:
                    eng.wait_ge(*bandT_kept.at(i, n + 1))

        weights = [(ident[:, :], w["ident"]), (identb[:, :], w["identb"]), (maskb[:, :], w["maskb"]),
                   (wqkv[:, :], w["L2_attn_w_attn"]), (wc[:, :], w["L2_attn_w_proj"]), (ones[:, :], w["ones_row"]),
                   (last_k[:, :], w["L2_last_k"]), (place_k[:, :], w["L2_place_k"]), (place_last[:, :], w["L2_place_last"]),
                   (last_v[:, :], w["L2_last_v"]), (place_v[:, :], w["L2_place_v"]),
                   (every_last_v[:, :], w["L2_last_v"][0, 0:HD].partition_broadcast(R)),
                   (wnat[:, 0:HID4P].rearrange("p (c d) -> p c d", c=HC4), w["L2_wg"].rearrange("(c p) d -> p c d", p=P)),
                   (wnat[:, HID4P:2 * HID4P].rearrange("p (c d) -> p c d", c=HC4), w["L2_wu"].rearrange("(c p) d -> p c d", p=P)),
                   (wnat[:, 2 * HID4P:], w["L2_ffn_w_down"])]
        with nc.Block() as block:
            @block.sync
            def _(sp):
                for dst, src in weights:
                    sp.dma_start(dst, src).then_inc(loaded, 16)
                sp.wait_ge(pool_set, 4)
                for slot in range(SLOTS):
                    for dram in (rel_dram, band_dram):
                        sp.dma_start(straight(dram, slot), zeros[:, :].rearrange("p (t c) -> p t c", t=NT)).then_inc(cleared, 16)
                sp.wait_ge(*made_places.at(0, 6))
                sp.sem_inc(past_sp, 1)
                for n, (_, j) in enumerate(TERMS):
                    sp.dma_start(places[n * HD:(n + 1) * HD, :], place_p[j][:, :]).then_inc(spread, 16)
                sp.wait_ge(cleared, 16 * 2 * SLOTS)
                sp.sem_inc(past_sp, 1)
                with sp.Fori(0, B) as i:
                    sp.wait_ge(*finished.at(i, 0))
                    sp.sem_inc(past_sp, 1)
                    sp.dma_start(x[:, :, :], rows(x_in, i)).then_inc(x_read, 16)
                    sp.wait_ge(*q_split.at(i, 1))
                    sp.sem_inc(past_sp, 1)
                    for j in range(3):
                        sp.dma_start(q_dram[j], qp[j][:, :]).then_inc(parts_sent, 16)
                    sp.wait_ge(*k_split.at(i, 1))
                    sp.sem_inc(past_sp, 1)
                    for j in range(3):
                        sp.dma_start(k_dram[j], kp[j][:, :]).then_inc(parts_sent, 16)
                    sp.wait_ge(parts_sent, i * 96 + 96)
                    sp.sem_inc(past_sp, 1)
                    by_head = lambda z: z.rearrange("(h d) t -> d h t", d=HD)
                    for n, (a, b) in enumerate(TERMS):
                        sp.dma_start(qs[n * HD:(n + 1) * HD, :, :], by_head(q_dram[a])).then_inc(terms_read, 16)
                        sp.dma_start(ks[n * HD:(n + 1) * HD, :, :], by_head(k_dram[b])).then_inc(terms_read, 16)
                    for k in range(HN + 1):
                        if k < HN:
                            if k >= SLOTS:
                                sp.wait_ge(*of_head(rel_read, i, k - SLOTS))
                                sp.sem_inc(past_sp, 1)
                            sp.wait_ge(*places_kept.at(i, k + 1))
                            sp.sem_inc(past_sp, 1)
                            sp.dma_start(skewed(rel_dram, k), by_place[:, k % 2, :, :]).then_inc(rel_sent[k % SLOTS].sem, 16)
                        if k >= 1:
                            h = k - 1
                            sp.wait_ge(*of_head(rel_sent, i, h))
                            sp.sem_inc(past_sp, 1)
                            if h >= 3:
                                sp.wait_ge(*low_made.at(i, NT * (h - 2)))
                                sp.sem_inc(past_sp, 1)
                            sp.dma_start(rel[:, h % 3, :, :], straight(rel_dram, h)).then_inc(rel_read[h % SLOTS].sem, 16)

            @block.gpsimd
            def _(pool):
                pool.memset(half[:, :], -0.5).then_inc(pool_set, 1)
                pool.memset(eps[:, :], EPS).then_inc(pool_set, 1)
                pool.memset(q4.half_step[:, :], 0x1FFFFF).then_inc(pool_set, 1)
                pool.memset(zeros[:, :], 0.0).then_inc(pool_set, 1)
                pool.memset(prob[:, :, 0:P], 0.0).then_inc(pool_set, 1)
                pool.sem_inc(stored.sem, 1)
                pool.wait_ge(pool_set, 5)
                pool.wait_ge(cleared, 16 * 2 * SLOTS)
                with pool.Fori(0, B) as i:
                    pool.wait_ge(*centred.at(i, 1))
                    pool.tensor_tensor(rstd[:, :], mv[:, :, 1], eps[:, :], ALU.add).then_inc(rstd_made.sem, 1)
                    pool.wait_ge(*rstd_made.at(i, 1))
                    pool.tensor_tensor(rstd[:, :], rstd[:, :], half[:, :], ALU.pow).then_inc(rstd_made.sem, 1)
                    for k in range(HN + 1):
                        if k < HN:
                            if k >= SLOTS:
                                pool.wait_ge(*of_head(band_read, i, k - SLOTS))
                            pool.wait_ge(*exp_made.at(i, NT * (k + 1)))
                            pool.sem_inc(past_pool, 1)
                            whole = prob[:, k % 3, :]
                            band_of_prob = bass.AP(whole.tensor, whole.offset, [list(whole.ap[0]), [STEP, NT], [1, W]])
                            pool.dma_start(straight(band_dram, k), band_of_prob).then_inc(band_sent[k % SLOTS].sem, 16)
                        if k >= 1:
                            h = k - 1
                            pool.wait_ge(*of_head(band_sent, i, h))
                            pool.sem_inc(past_pool, 1)
                            if h >= 3:
                                pool.wait_ge(*bandT_ready.at(i, h - 2))
                                pool.sem_inc(past_pool, 1)
                            pool.dma_start(band[:, h % 3, :, :], skewed(band_dram, h)).then_inc(band_read[h % SLOTS].sem, 16)
                    pool.wait_ge(*finished.at(i, 1))
                    pool.sem_inc(past_pool, 1)
                    pool.dma_start(rows(x_out, i), x_new[:, :, :]).then_inc(x_sent, 16)
                    pool.wait_ge(x_sent, i * 16 + 16)
                    pool.sem_inc(past_pool, 1)
                    pool.sem_inc(stored.sem, 1)

            @block.vector
            def _(dve):
                dve.wait_ge(loaded, 16 * len(weights))
                dve.wait_ge(pool_set, 5)
                link = Chain(dve, made_places, 0)
                dve.tensor_scalar(minus_last[:, :], last_k[:, :], -1.0, None, ALU.mult)
                link.then(dve.tensor_scalar(place_k[:, :], place_k[:, :], place_last[:, :], -1.0, ALU.subtract, ALU.mult))
                link.then(dve.tensor_tensor(place_v[:, :], place_v[:, :], every_last_v[:, :], ALU.subtract))
                split3(dve, link, place_k[:, :], [z[:, :] for z in place_p], place_rest[:, :])
                link.done()
                for _ in quantise(dve, Chain(dve, made_weights, 0), q4, wnat[:, :], wqd[:, :], 2 * HID4P + HID4):
                    pass
                dve.sem_inc(dve_set, 1)
                dve.wait_ge(pe_set, 1)
                dve.tensor_copy(wg[:, :], pS[:, 0, 0:HID4P])
                dve.tensor_copy(wu[:, :], pS[:, 1, 0:HID4P])
                dve.tensor_copy(wd[:, 0:2, :], pS[:, 2, 0:2 * D].rearrange("p (c d) -> p c d", c=2))
                dve.tensor_copy(wd[0:HID4 - 2 * P, 2, :], pS[0:HID4 - 2 * P, 2, 2 * D:3 * D]).then_inc(dve_set, 1)
                dve.sem_inc(finished.sem, 1)
                with dve.Fori(0, B) as i:
                    link = Chain(dve, chain, i)
                    dve.wait_ge(x_read, i * 16 + 16)
                    for t in range(NT):
                        last = dve.bn_stats(stat[:, t, :], x[:, t, :])
                    link.then(last)
                    dve.memset(spare[:, :], 0.0)
                    for t in range(NT):
                        last = dve.bn_aggr(mv[:, t, :], stat[:, t, :])
                    last.then_inc(centred.sem, 1)
                    dve.wait_ge(*rstd_made.at(i, 2))
                    for t in range(NT):
                        last = dve.tensor_scalar(xn[:, t, :], x[:, t, :], mv[:, t, 0:1], rstd[:, t:t + 1], ALU.subtract, ALU.mult)
                    last.then_inc(xn_made.sem, 1)
                    dve.wait_ge(*proj_ready.at(i, 1))
                    link.then(dve.tensor_copy(qf[:, :], pA[:, :]))
                    split3(dve, link, qf[:, :], [z[:, :] for z in qp], rest_q[:, :])
                    dve.sem_inc(q_split.sem, 1)
                    dve.wait_ge(*proj_ready.at(i, 2))
                    link.then(dve.tensor_scalar(kf[:, :], pS[:, 2, :], -float(np.float32(HD ** -0.5)), minus_last[:, :], ALU.mult, ALU.add))
                    split3(dve, link, kf[:, :], [z[:, :] for z in kp], rest_k[:, :])
                    dve.sem_inc(k_split.sem, 1)
                    for _ in quantise(dve, link, q4, xn[:, :, :].rearrange("p t d -> p (t d)"), xq[:, :], NT * D):
                        pass
                    dve.sem_inc(xq_made.sem, 1)
                    for t in range(NT):
                        dve.wait_ge(*gate_tanh.at(i, t + 1))
                        link.then(dve.scalar_tensor_tensor(act_in[:, :], th[:, t % 2, :], 1.0, pS[:, 0, 0:HID4], ALU.add, ALU.mult))
                        dve.scalar_tensor_tensor(hid[:, t * HID4:(t + 1) * HID4], act_in[:, :], 0.5, pS[:, 1, 0:HID4], ALU.mult, ALU.mult).then_inc(hid_made.sem, 1)
                    dve.wait_ge(*hid_made.at(i, NT))
                    steps = quantise(dve, link, q4, hid[:, :], hid[:, :], NT * HID4)

                    def lowest(n):
                        h, t, k = n // NT, n % NT, k_of(n)
                        dve.wait_ge(*scored.at(i, n + 1))
                        near = max(0, t - 1) * P
                        start = 3e38
                        if t >= 2:
                            start = far[:, t % 2:t % 2 + 1]
                            dve.tensor_reduce(start, pS[:, n % SB, 0:near], AX.X, ALU.min).then_inc(far_made.sem, 1)
                            dve.wait_ge(*far_made.at(i, 2 * h + t - 1))
                        if t == 0:
                            dve.wait_ge(*of_head(rel_read, i, h))
                        dve.sem_inc(past_dve, 1)
                        near_s = pS[:, n % SB, near:k]
                        dve.tensor_tensor_reduce(near_s, near_s, rel[:, h % 3, t, W - (k - near):W], 1.0, start, ALU.add, ALU.min,
                                                 low[:, n:n + 1]).then_inc(low_made.sem, 1)

                    def keep(n):
                        dve.wait_ge(*probT_ready.at(i, n + 1))
                        if n >= 3:
                            dve.wait_ge(*attended.at(i, n - 2))
                        dve.tensor_copy(probT[:, n % 3, 0:k_of(n)], pT[:, bank_of["item", n], 0:k_of(n)]).then_inc(probT_kept_dve.sem, 1)

                    for n in range(ITEMS + 2):
                        if n < ITEMS:
                            lowest(n)
                        if n >= 2 and not kept_by_act(n - 2):
                            keep(n - 2)
                        if n % NT == 2:
                            next(steps, None)
                    for _ in steps:
                        pass
                    dve.sem_inc(hid_quantised.sem, 1)
                    dve.wait_ge(*exp_made.at(i, ITEMS))
                    link.then(dve.reciprocal(inv[:, :], total[:, :]))
                    dve.wait_ge(*band_attended.at(i, HN))
                    heads = lambda z: z.rearrange("p (t h d) -> p t h d", t=NT, d=HD)
                    for src, dst in ((pY, yn), (pZ, y_all)):
                        for t in range(NT):
                            last = dve.tensor_tensor(dst[:, t, :].rearrange("p (h d) -> p h d", d=HD), heads(src[:, :])[:, t, :, :],
                                                     inv[:, :].rearrange("p (h t) -> p t h", t=NT)[:, t, :].unsqueeze(2).to_broadcast([P, HN, HD]), ALU.mult)
                    link.then(last)
                    dve.tensor_tensor(yn[:, :, :], yn[:, :, :], y_all[:, :, :], ALU.add).then_inc(y_made.sem, 1)
                    dve.wait_ge(*g_tanh.at(i, 1))
                    out_of = lambda z: z.rearrange("p (t d) -> p t d", t=NT)
                    link.then(dve.scalar_tensor_tensor(g_a[:, :, :], g_th[:, :, :], 1.0, out_of(pT[:, 0, :]), ALU.add, ALU.mult))
                    dve.wait_ge(*s_ready.at(i, 1))
                    link.then(dve.scalar_tensor_tensor(g_a[:, :, :], g_a[:, :, :], 0.5, out_of(pA[:, :]), ALU.mult, ALU.mult))
                    dve.wait_ge(*stored.at(i, 0))
                    link.then(dve.tensor_tensor(x_new[:, :, :], g_a[:, :, :], x[:, :, :], ALU.add))
                    dve.sem_inc(finished.sem, 1)
                    link.done()

            @block.scalar
            def _(act):
                act.wait_ge(pool_set, 5)
                with act.Fori(0, B) as i:
                    act.wait_ge(*xT_ready.at(i, 1))
                    act.copy(xnT[:, :], pA[:, :]).then_inc(xT_kept.sem, 1)
                    act.wait_ge(*proj_ready.at(i, 3))
                    act.copy(v[:, :, :], pT[:, 0, :].rearrange("p (t d) -> p t d", t=NT)).then_inc(v_kept.sem, 1)
                    act.wait_ge(*xqT_ready.at(i, 1))
                    act.copy(xqT[:, :], pT[:, 1, :]).then_inc(xqT_kept.sem, 1)
                    for t in range(NT):
                        act.wait_ge(*gu_ready.at(i, t + 1))
                        act.activation(th[:, t % 2, :], pS[:, 0, 0:HID4], ACT.Tanh, scale=0.5).then_inc(gate_tanh.sem, 1)

                    def exps(n):
                        h = n // NT
                        act.wait_ge(*low_made.at(i, n + 1))
                        if h >= 3 and n % NT == 0:
                            act.wait_ge(*probT_ready.at(i, NT * (h - 2)))
                            act.wait_ge(*of_head(band_sent, i, h - 3))
                        act.activation(prob[:, h % 3, at_prob(n):at_prob(n) + k_of(n)], pS[:, n % SB, 0:k_of(n)], ACT.Exp, bias=low[:, n:n + 1], scale=-1.0,
                                       accum_out=total[:, n:n + 1]).then_inc(exp_made.sem, 1)

                    def keep(n):
                        act.wait_ge(*probT_ready.at(i, n + 1))
                        if n >= 3:
                            act.wait_ge(*attended.at(i, n - 2))
                        act.copy(probT[:, n % 3, 0:k_of(n)], pT[:, bank_of["item", n], 0:k_of(n)]).then_inc(probT_kept_act.sem, 1)

                    def keep_places(h):
                        act.wait_ge(*places_ready.at(i, h + 1))
                        if h >= 2:
                            act.wait_ge(*of_head(rel_sent, i, h - 2))
                        act.copy(by_place[:, h % 2, :, :], pA[:, :].rearrange("p (t r) -> p t r", t=NT)).then_inc(places_kept.sem, 1)

                    def keep_band(h):
                        act.wait_ge(*bandT_ready.at(i, h + 1))
                        if h >= 2:
                            act.wait_ge(*band_attended.at(i, h - 1))
                        act.copy(bandT[:, h % 2, :], pT[:, bank_of["band", h], :]).then_inc(bandT_kept.sem, 1)

                    for h in range(LEAD):
                        keep_places(h)
                    for n in range(ITEMS + NT * LAG + 1):
                        if n % NT == 0 and n // NT + LEAD < HN:
                            keep_places(n // NT + LEAD)
                        if n < ITEMS:
                            exps(n)
                        if 0 <= n - 2 < ITEMS and kept_by_act(n - 2):
                            keep(n - 2)
                        if n % NT == 3 and 0 <= n // NT - LAG < HN:
                            keep_band(n // NT - LAG)
                    for c in range(HC4):
                        act.wait_ge(*hidT_ready.at(i, c + 1))
                        rows_of = min(P, HID4 - c * P)
                        act.copy(hidT[0:rows_of, c, :], pS[0:rows_of, c, :]).then_inc(hidT_kept.sem, 1)
                    act.wait_ge(*yT_ready.at(i, 1))
                    act.copy(yT[:, :], pY[:, :]).then_inc(yT_kept.sem, 1)
                    act.wait_ge(*ffn_ready.at(i, 1))
                    act.activation(g_th[:, :, :], pT[:, 0, :].rearrange("p (t d) -> p t d", t=NT), ACT.Tanh, scale=0.5).then_inc(g_tanh.sem, 1)

            @block.tensor
            def _(pe):
                pe.wait_ge(loaded, 16 * len(weights))
                pe.wait_ge(dve_set, 1)
                for c in range(HC4):
                    pe.transpose(pS[:, 0, c * P:(c + 1) * P], wqd[:, c * P:(c + 1) * P], ident[:, :])
                    pe.transpose(pS[:, 1, c * P:(c + 1) * P], wqd[:, HID4P + c * P:HID4P + (c + 1) * P], ident[:, :])
                    rows_of = min(P, HID4 - c * P)
                    last = pe.transpose(pS[0:rows_of, 2, c * D:(c + 1) * D], wqd[:, 2 * HID4P + c * P:2 * HID4P + c * P + rows_of], ident[:, :])
                last.then_inc(pe_set, 1)
                pe.wait_ge(dve_set, 2)
                pe.wait_ge(spread, 16 * len(TERMS))
                with pe.Fori(0, B) as i:
                    pe.wait_ge(*xn_made.at(i, 1))
                    pe.wait_ge(*finished.at(i, 0))
                    for t in range(NT):
                        last = pe.transpose(pA[:, t * P:(t + 1) * P], xn[:, t, :], ident[:, :])
                    last.then_inc(xT_ready.sem, 1)
                    pe.wait_ge(*xT_kept.at(i, 1))
                    pe.matmul(pA[:, :], wqkv[:, 0:D], xnT[:, :], start=True, stop=True).then_inc(proj_ready.sem, 1)
                    pe.matmul(pS[:, 2, :], wqkv[:, D:2 * D], xnT[:, :], start=True, stop=True).then_inc(proj_ready.sem, 1)
                    for t in range(NT):
                        out = pT[:, 0, t * P:(t + 1) * P]
                        pe.matmul(out, xnT[:, t * P:(t + 1) * P], wqkv[:, 2 * D:3 * D], start=True, stop=False)
                        last = pe.matmul(out, ones[:, :], last_v[:, :], start=False, stop=True)
                    last.then_inc(proj_ready.sem, 1)
                    pe.wait_ge(*xq_made.at(i, 1))
                    for t in range(NT):
                        last = pe.transpose(pT[:, 1, t * P:(t + 1) * P], xq[:, t * D:(t + 1) * D], ident[:, :])
                    last.then_inc(xqT_ready.sem, 1)
                    pe.wait_ge(*xqT_kept.at(i, 1))
                    for t in range(NT):
                        if t:
                            pe.wait_ge(*hid_made.at(i, t))
                        pe.matmul(pS[:, 0, 0:HID4], xqT[:, t * P:(t + 1) * P], wg[:, 0:HID4], start=True, stop=True)
                        pe.matmul(pS[:, 1, 0:HID4], xqT[:, t * P:(t + 1) * P], wu[:, 0:HID4], start=True, stop=True).then_inc(gu_ready.sem, 1)

                    def by_places(h):
                        if h:
                            pe.wait_ge(*places_kept.at(i, h))
                        for t in range(NT):
                            last = pe.matmul(pA[:, t * P:(t + 1) * P], qs[:, h, t * P:(t + 1) * P], places[:, :], start=True, stop=True)
                        last.then_inc(places_ready.sem, 1)

                    def scores(n):
                        h, t, k = n // NT, n % NT, k_of(n)
                        if n >= SB:
                            pe.wait_ge(*exp_made.at(i, n - SB + 1))
                        elif n == 0:
                            pe.wait_ge(*hid_made.at(i, NT))
                        pe.matmul(pS[:, n % SB, 0:k], qs[:, h, t * P:k], ks[:, h, 0:k], start=True, stop=True)
                        pe.matmul(pS[:, n % SB, t * P:k], identb[:, :], maskb[:, :], start=False, stop=True,
                                  skip_group_check=True).then_inc(scored.sem, 1)

                    def turn(n):
                        pe.wait_ge(*exp_made.at(i, n + 1))
                        bank_free(pe, i, ("item", n))
                        for u in range(n % NT + 1):
                            last = pe.transpose(pT[:, bank_of["item", n], u * P:(u + 1) * P],
                                                prob[:, n // NT % 3, at_prob(n) + u * P:at_prob(n) + (u + 1) * P], ident[:, :])
                        last.then_inc(probT_ready.sem, 1)

                    def attend(n):
                        h, t = n // NT, n % NT
                        kept_wait(pe, i, n)
                        for u in range(t + 1):
                            last = pe.matmul(pY[:, t * P + h * HD:t * P + (h + 1) * HD], probT[:, n % 3, u * P:(u + 1) * P],
                                             v[:, u, h * HD:(h + 1) * HD], start=(u == 0), stop=(u == t))
                        last.then_inc(attended.sem, 1)

                    def turn_band(h):
                        pe.wait_ge(*of_head(band_read, i, h))
                        bank_free(pe, i, ("band", h))
                        for t in range(NT):
                            last = pe.transpose(pT[:, bank_of["band", h], t * P:(t + 1) * P], band[:, h % 3, t, :], ident[:, :])
                        last.then_inc(bandT_ready.sem, 1)

                    def attend_band(h):
                        pe.wait_ge(*bandT_kept.at(i, h + 1))
                        for t in range(NT):
                            last = pe.matmul(pZ[:, t * P + h * HD:t * P + (h + 1) * HD], bandT[:, h % 2, t * P:(t + 1) * P], place_v[:, :],
                                             start=True, stop=True)
                        last.then_inc(band_attended.sem, 1)

                    pe.wait_ge(terms_read, i * 16 * 2 * len(TERMS) + 16 * 2 * len(TERMS))
                    pe.wait_ge(*v_kept.at(i, 1))
                    for h in range(LEAD):
                        by_places(h)
                    for n in range(ITEMS + NT * LAG + 3):
                        if n % NT == 0 and n // NT + LEAD < HN:
                            by_places(n // NT + LEAD)
                        if n < ITEMS:
                            scores(n)
                        if 0 <= n - 2 < ITEMS:
                            turn(n - 2)
                        if n % NT == 3 and 0 <= n // NT - LAG < HN:
                            turn_band(n // NT - LAG)
                        if 0 <= n - 4 < ITEMS:
                            attend(n - 4)
                        if (n - 2) % NT == 3 and 0 <= (n - 2) // NT - LAG < HN:
                            attend_band((n - 2) // NT - LAG)
                    pe.wait_ge(*hid_quantised.at(i, 1))
                    for c in range(HC4):
                        rows_of = min(P, HID4 - c * P)
                        for t in range(NT):
                            last = pe.transpose(pS[0:rows_of, c, t * P:(t + 1) * P],
                                                hid[:, t * HID4 + c * P:t * HID4 + c * P + rows_of], ident[:, :])
                        last.then_inc(hidT_ready.sem, 1)
                    pe.wait_ge(*y_made.at(i, 1))
                    for t in range(NT):
                        last = pe.transpose(pY[:, t * P:(t + 1) * P], yn[:, t, :], ident[:, :])
                    last.then_inc(yT_ready.sem, 1)
                    pe.wait_ge(*hidT_kept.at(i, HC4))
                    for t in range(NT):
                        for c in range(HC4):
                            rows_of = min(P, HID4 - c * P)
                            last = pe.matmul(pT[:, 0, t * D:(t + 1) * D], hidT[0:rows_of, c, t * P:(t + 1) * P], wd[0:rows_of, c, :],
                                             start=(c == 0), stop=(c == HC4 - 1))
                    last.then_inc(ffn_ready.sem, 1)
                    pe.wait_ge(*yT_kept.at(i, 1))
                    for t in range(NT):
                        last = pe.matmul(pA[:, t * P:(t + 1) * P], yT[:, t * P:(t + 1) * P], wc[:, :], start=True, stop=True)
                    last.then_inc(s_ready.sem, 1)


def layer3(nc, w, x_in, x_out):
    L = 64
    E, FF = 8, 512
    FC = FF // P
    with ExitStack() as stack:
        m = Scope(nc, stack, "d_")
        ident, identb, maskb = m.sb("ident", [P, P]), m.sb("identb", [P, P], BF16), m.sb("maskb", [P, P], BF16)
        wdn = m.sb("wdn", [L, 3, HN, D])
        ups = m.sb("ups", [L, 5, HD])
        weff = m.sb("weff", [P, 5, P])
        wc = m.sb("wc", [P, D])
        cosq, sinq, cosk, sink = [m.sb(n, [P, S]) for n in ("cosq", "sinq", "cosk", "sink")]
        rw, rb, ones = m.sb("rw", [P, E]), m.sb("rb", [1, E]), m.sb("ones", [1, P])
        earlier = m.sb("earlier", [P, E, E])
        wup, wdown = m.sb("wup", [P, E, FF]), m.sb("wdown", [P, E * FC, D])
        half, eps, spare = m.sb("half", [P, NT]), m.sb("eps", [P, NT]), m.sb("spare", [P, 1])
        x, stat, mv, rstd = m.sb("x", [P, NT, D]), m.sb("stat", [P, NT, 6]), m.sb("mv", [P, NT, 2]), m.sb("rstd", [P, NT])
        xn, xnT = m.sb("xn", [P, NT, D]), m.sb("xnT", [P, S])
        rot_a, rot_b, qf, kf, rest_q, rest_k = [m.sb(n, [P, S]) for n in ("rot_a", "rot_b", "qf", "kf", "rest_q", "rest_k")]
        qp, kp = [[m.sb(f"{n}{j}", [P, S], BF16) for j in range(3)] for n in ("qp", "kp")]
        qs, ks = m.sb("qs", [KR6, HN, S], BF16), m.sb("ks", [KR6, HN, S], BF16)
        v = m.sb("v", [P, NT, D])
        low, total, inv = m.sb("low", [P, ITEMS]), m.sb("total", [P, ITEMS]), m.sb("inv", [P, ITEMS])
        prob, probT = m.sb("prob", [P, 4, S]), m.sb("probT", [P, 3, S])
        yn, yT = m.sb("yn", [P, NT, D]), m.sb("yT", [P, S])
        lg, pr, comb = [m.sb(n, [P, NT, E]) for n in ("lg", "pr", "comb")]
        ltop, lsum, linv = m.sb("ltop", [P, NT]), m.sb("lsum", [P, NT]), m.sb("linv", [P, NT])
        more, same, rank = m.sb("more", [P, NT, E, E]), m.sb("same", [P, NT, E, E]), m.sb("rank", [P, NT, E])
        hid = m.sb("hid", [P, 2, FC, S])
        acc, g_th, g_a, x_new = m.sb("acc", [P, NT, D]), m.sb("g_th", [P, NT, D]), m.sb("g_a", [P, NT, D]), m.sb("x_new", [P, NT, D])
        pS, pT = m.ps("pS", [P, SB, S]), m.ps("pT", [P, TB, S])
        pY, pA, pB = m.ps("pY", [P, S]), m.ps("pA", [P, S]), m.ps("pB", [P, S])
        q_dram = [nc.dram_tensor(f"d_q{j}", (P, S), BF16).ap() for j in range(3)]
        k_dram = [nc.dram_tensor(f"d_k{j}", (P, S), BF16).ap() for j in range(3)]

        loaded, pool_set, pe_set, dve_set, x_read, x_sent = [m.sem(n) for n in ("loaded", "pool_set", "pe_set", "dve_set", "x_read", "x_sent")]
        parts_sent, terms_read = m.sem("parts_sent"), m.sem("terms_read")
        centred, rstd_made, xn_made = m.ev("centred", 1), m.ev("rstd_made", 2), m.ev("xn_made", 1)
        xT_ready, xT_kept = m.ev("xT_ready", 1), m.ev("xT_kept", 1)
        proj_ready = m.ev("proj_ready", 5)
        q_split, k_split = m.ev("q_split", 1), m.ev("k_split", 1)
        v_kept = m.ev("v_kept", 1)
        scored, low_made, exp_made = m.ev("scored", ITEMS), m.ev("low_made", ITEMS), m.ev("exp_made", ITEMS)
        probT_ready, attended = m.ev("probT_ready", ITEMS), m.ev("attended", ITEMS)
        probT_kept_act, probT_kept_dve = m.ev("probT_kept_act", ITEMS // 2), m.ev("probT_kept_dve", ITEMS // 2)
        y_made, yT_ready, yT_kept, s_ready = m.ev("y_made", 1), m.ev("yT_ready", 1), m.ev("yT_kept", 1), m.ev("s_ready", 1)
        lg_ready, lg_top, lg_exp, comb_made = m.ev("lg_ready", 1), m.ev("lg_top", 1), m.ev("lg_exp", 1), m.ev("comb_made", 1)
        up_ready, hid_made = m.ev("up_ready", E * FC), m.ev("hid_made", E * FC)
        down_ready, added = m.ev("down_ready", E), m.ev("added", E)
        summed, g_tanh = m.ev("summed", 1), m.ev("g_tanh", 1)
        finished, stored = m.ev("finished", 1, credit=True), m.ev("stored", 1, credit=True)
        chain = m.ev("chain", 24)
        k_of = lambda n: (n % NT + 1) * P
        kept_by_act = lambda n: n % NT < 2

        def kept_wait(eng, i, n):
            kept, nth = (probT_kept_act, n % NT) if kept_by_act(n) else (probT_kept_dve, n % NT - 2)
            eng.wait_ge(*kept.at(i, 2 * (n // NT) + nth + 1))

        weights = [(ident[:, :], w["ident"]), (identb[:, :], w["identb"]), (maskb[:, :], w["maskb"]),
                   (wdn[:, 0, :, :], w["L3_WqT"]), (wdn[:, 1, :, :], w["L3_WkT"]), (wdn[:, 2, :, :], w["L3_WvT"]),
                   (ups[:, 0, 0:4], w["L3_attn_Wq_up_c"]), (ups[:, 0, 4:8], w["L3_attn_Wq_up_e"]),
                   (ups[:, 2, 0:4], w["L3_attn_Wk_up_c"]), (ups[:, 2, 4:8], w["L3_attn_Wk_up_e"]),
                   (ups[:, 4, :], w["L3_attn_Wv_up"]), (wc[:, :], w["L3_attn_Wc"]),
                   (cosq[:, :], w["L3_cosq"]), (sinq[:, :], w["L3_sinq"]), (cosk[:, :], w["L3_cosk"]), (sink[:, :], w["L3_sink"]),
                   (rw[:, :], w["L3_ffn_router_w"]), (rb[:, :], w["L3_rb"]), (ones[:, :], w["ones_row"]), (earlier[:, :, :], w["L3_earlier"]),
                   (wup[:, :, :], w["L3_upT"]), (wdown[:, :, :], w["L3_downT"])]
        with nc.Block() as block:
            @block.sync
            def _(sp):
                for dst, src in weights:
                    sp.dma_start(dst, src).then_inc(loaded, 16)
                with sp.Fori(0, B) as i:
                    sp.wait_ge(*finished.at(i, 0))
                    sp.nop()
                    sp.dma_start(x[:, :, :], rows(x_in, i)).then_inc(x_read, 16)
                    sp.wait_ge(*q_split.at(i, 1))
                    for j in range(3):
                        sp.dma_start(q_dram[j], qp[j][:, :]).then_inc(parts_sent, 16)
                    sp.wait_ge(*k_split.at(i, 1))
                    for j in range(3):
                        sp.dma_start(k_dram[j], kp[j][:, :]).then_inc(parts_sent, 16)
                    sp.wait_ge(parts_sent, i * 96 + 96)
                    by_head = lambda z: z.rearrange("(h d) t -> d h t", d=HD)
                    for n, (a, b) in enumerate(TERMS):
                        sp.dma_start(qs[n * HD:(n + 1) * HD, :, :], by_head(q_dram[a])).then_inc(terms_read, 16)
                        sp.dma_start(ks[n * HD:(n + 1) * HD, :, :], by_head(k_dram[b])).then_inc(terms_read, 16)

            @block.gpsimd
            def _(pool):
                pool.memset(half[:, :], -0.5).then_inc(pool_set, 1)
                pool.memset(eps[:, :], EPS).then_inc(pool_set, 1)
                pool.sem_inc(stored.sem, 1)
                pool.wait_ge(pool_set, 2)
                with pool.Fori(0, B) as i:
                    pool.wait_ge(*centred.at(i, 1))
                    pool.tensor_tensor(rstd[:, :], mv[:, :, 1], eps[:, :], ALU.add).then_inc(rstd_made.sem, 1)
                    pool.wait_ge(*rstd_made.at(i, 1))
                    pool.tensor_tensor(rstd[:, :], rstd[:, :], half[:, :], ALU.pow).then_inc(rstd_made.sem, 1)
                    pool.wait_ge(*finished.at(i, 1))
                    pool.dma_start(rows(x_out, i), x_new[:, :, :]).then_inc(x_sent, 16)
                    pool.wait_ge(x_sent, i * 16 + 16)
                    pool.sem_inc(stored.sem, 1)

            @block.vector
            def _(dve):
                dve.wait_ge(loaded, 16 * len(weights))
                for one in (0, 2):
                    dve.memset(ups[:, one + 1, 0:4], 0.0)
                    pair = lambda z: z.rearrange("p (a b) -> p a b", b=2)
                    dve.tensor_scalar(pair(ups[:, one + 1, 4:8])[:, :, 0], pair(ups[:, one, 4:8])[:, :, 1], -1.0, None, ALU.mult)
                    last = dve.tensor_copy(pair(ups[:, one + 1, 4:8])[:, :, 1], pair(ups[:, one, 4:8])[:, :, 0])
                last.then_inc(dve_set, 1)
                dve.wait_ge(pe_set, 1)
                for n in range(5):
                    last = dve.tensor_copy(weff[:, n, :], (pA, pB, pY, pS[:, 0, :], pS[:, 1, :])[n][:, 0:P])
                last.then_inc(dve_set, 1)
                dve.sem_inc(finished.sem, 1)
                with dve.Fori(0, B) as i:
                    link = Chain(dve, chain, i)
                    dve.wait_ge(x_read, i * 16 + 16)
                    for t in range(NT):
                        last = dve.bn_stats(stat[:, t, :], x[:, t, :])
                    link.then(last)
                    dve.memset(spare[:, :], 0.0)
                    for t in range(NT):
                        last = dve.bn_aggr(mv[:, t, :], stat[:, t, :])
                    last.then_inc(centred.sem, 1)
                    dve.wait_ge(*rstd_made.at(i, 2))
                    for t in range(NT):
                        last = dve.tensor_scalar(xn[:, t, :], x[:, t, :], mv[:, t, 0:1], rstd[:, t:t + 1], ALU.subtract, ALU.mult)
                    last.then_inc(xn_made.sem, 1)
                    for one, (cos, sin, full) in enumerate(((cosq, sinq, qf), (cosk, sink, kf))):
                        dve.wait_ge(*proj_ready.at(i, 2 * one + 2))
                        straight, crossed = ((pA[:, :], pB[:, :]), (pS[:, 0, :], pS[:, 1, :]))[one]
                        dve.tensor_tensor(rot_a[:, :], straight, cos[:, :], ALU.mult)
                        link.then(dve.tensor_tensor(rot_b[:, :], crossed, sin[:, :], ALU.mult))
                        link.then(dve.tensor_tensor(full[:, :], rot_a[:, :], rot_b[:, :], ALU.add))
                        split3(dve, link, full[:, :], [z[:, :] for z in (qp, kp)[one]], (rest_q, rest_k)[one][:, :])
                        dve.sem_inc((q_split, k_split)[one].sem, 1)

                    def lowest(n):
                        dve.wait_ge(*scored.at(i, n + 1))
                        dve.tensor_reduce(low[:, n:n + 1], pS[:, n % SB, 0:k_of(n)], AX.X, ALU.min).then_inc(low_made.sem, 1)

                    def keep(n):
                        dve.wait_ge(*probT_ready.at(i, n + 1))
                        if n >= 3:
                            dve.wait_ge(*attended.at(i, n - 2))
                        dve.tensor_copy(probT[:, n % 3, 0:k_of(n)], pT[:, n % TB, 0:k_of(n)]).then_inc(probT_kept_dve.sem, 1)

                    for n in range(ITEMS + 2):
                        if n < ITEMS:
                            lowest(n)
                        if n >= 2 and not kept_by_act(n - 2):
                            keep(n - 2)
                    dve.wait_ge(*exp_made.at(i, ITEMS))
                    link.then(dve.reciprocal(inv[:, :], total[:, :]))
                    dve.wait_ge(*attended.at(i, ITEMS))
                    heads = lambda z: z.rearrange("p (t h d) -> p t h d", t=NT, d=HD)
                    for t in range(NT):
                        last = dve.tensor_tensor(yn[:, t, :].rearrange("p (h d) -> p h d", d=HD), heads(pY[:, :])[:, t, :, :],
                                                 inv[:, :].rearrange("p (h t) -> p t h", t=NT)[:, t, :].unsqueeze(2).to_broadcast([P, HN, HD]), ALU.mult)
                    last.then_inc(y_made.sem, 1)
                    dve.wait_ge(*lg_ready.at(i, 1))
                    dve.tensor_reduce(ltop[:, :], pA[:, 0:NT * E].rearrange("p (t e) -> p t e", t=NT), AX.X, ALU.max, negate=True).then_inc(lg_top.sem, 1)
                    dve.wait_ge(*lg_exp.at(i, 1))
                    link.then(dve.reciprocal(linv[:, :], lsum[:, :]))
                    link.then(dve.tensor_tensor(pr[:, :, :], lg[:, :, :], linv[:, :].unsqueeze(2).to_broadcast([P, NT, E]), ALU.mult))
                    for t in range(NT):
                        other = pr[:, t, :].unsqueeze(1).to_broadcast([P, E, E])
                        own = pr[:, t, :].unsqueeze(2).to_broadcast([P, E, E])
                        dve.tensor_tensor(more[:, t, :, :], other, own, ALU.is_gt)
                        last = dve.tensor_tensor(same[:, t, :, :], other, own, ALU.is_equal)
                    link.then(last)
                    for t in range(NT):
                        last = dve.tensor_tensor(same[:, t, :, :], same[:, t, :, :], earlier[:, :, :], ALU.mult)
                    link.then(last)
                    link.then(dve.tensor_tensor(more[:, :, :, :], more[:, :, :, :], same[:, :, :, :], ALU.add))
                    link.then(dve.tensor_reduce(rank[:, :, :], more[:, :, :, :], AX.X, ALU.add))
                    link.then(dve.scalar_tensor_tensor(comb[:, :, :], rank[:, :, :], 1.5, pr[:, :, :], ALU.is_lt, ALU.mult))
                    for e in range(E):
                        dve.wait_ge(*down_ready.at(i, e + 1))
                        for t in range(NT):
                            part, share = pT[:, e % TB, t * D:(t + 1) * D], comb[:, t, e:e + 1]
                            if e == 0:
                                last = dve.tensor_scalar(acc[:, t, :], part, share, None, ALU.mult)
                            else:
                                last = dve.scalar_tensor_tensor(acc[:, t, :], part, share, acc[:, t, :], ALU.mult, ALU.add)
                        last.then_inc(added.sem, 1)
                        dve.wait_ge(*added.at(i, e + 1))
                    dve.wait_ge(*g_tanh.at(i, 1))
                    link.then(dve.scalar_tensor_tensor(g_a[:, :, :], g_th[:, :, :], 1.0, acc[:, :, :], ALU.add, ALU.mult))
                    dve.wait_ge(*s_ready.at(i, 1))
                    link.then(dve.scalar_tensor_tensor(g_a[:, :, :], g_a[:, :, :], 0.5, pB[:, :].rearrange("p (t d) -> p t d", t=NT), ALU.mult, ALU.mult))
                    dve.wait_ge(*stored.at(i, 0))
                    link.then(dve.tensor_tensor(x_new[:, :, :], g_a[:, :, :], x[:, :, :], ALU.add))
                    dve.sem_inc(finished.sem, 1)
                    link.done()

            @block.scalar
            def _(act):
                with act.Fori(0, B) as i:
                    act.wait_ge(*xT_ready.at(i, 1))
                    act.copy(xnT[:, :], pA[:, :]).then_inc(xT_kept.sem, 1)
                    act.wait_ge(*proj_ready.at(i, 5))
                    act.copy(v[:, :, :], pT[:, 0, :].rearrange("p (t d) -> p t d", t=NT)).then_inc(v_kept.sem, 1)

                    def exps(n):
                        act.wait_ge(*low_made.at(i, n + 1))
                        if n >= 4:
                            act.wait_ge(*probT_ready.at(i, n - 3))
                        act.activation(prob[:, n % 4, 0:k_of(n)], pS[:, n % SB, 0:k_of(n)], ACT.Exp, bias=low[:, n:n + 1], scale=-1.0,
                                       accum_out=total[:, n:n + 1]).then_inc(exp_made.sem, 1)

                    def keep(n):
                        act.wait_ge(*probT_ready.at(i, n + 1))
                        if n >= 3:
                            act.wait_ge(*attended.at(i, n - 2))
                        act.copy(probT[:, n % 3, 0:k_of(n)], pT[:, n % TB, 0:k_of(n)]).then_inc(probT_kept_act.sem, 1)

                    for n in range(ITEMS + 2):
                        if n < ITEMS:
                            exps(n)
                        if n >= 2 and kept_by_act(n - 2):
                            keep(n - 2)
                    act.wait_ge(*lg_top.at(i, 1))
                    for t in range(NT):
                        last = act.activation(lg[:, t, :], pA[:, t * E:(t + 1) * E], ACT.Exp, bias=ltop[:, t:t + 1], accum_out=lsum[:, t:t + 1])
                    last.then_inc(lg_exp.sem, 1)
                    act.wait_ge(*yT_ready.at(i, 1))
                    act.copy(yT[:, :], pY[:, :]).then_inc(yT_kept.sem, 1)
                    for n in range(E * FC):
                        e, c = n // FC, n % FC
                        act.wait_ge(*up_ready.at(i, n + 1))
                        if e >= 2 and c == 0:
                            act.wait_ge(*down_ready.at(i, e - 1))
                        act.activation(hid[:, e % 2, c, :], pS[:, n % SB, :], ACT.Gelu).then_inc(hid_made.sem, 1)
                    act.wait_ge(*added.at(i, E))
                    act.activation(g_th[:, :, :], acc[:, :, :], ACT.Tanh, scale=0.5).then_inc(g_tanh.sem, 1)

            @block.tensor
            def _(pe):
                pe.wait_ge(loaded, 16 * len(weights))
                pe.wait_ge(dve_set, 1)
                for n in range(5):
                    for h in range(HN):
                        last = pe.matmul((pA, pB, pY, pS[:, 0, :], pS[:, 1, :])[n][:, h * HD:(h + 1) * HD], wdn[:, n // 2, h, :], ups[:, n, :], start=True, stop=True)
                last.then_inc(pe_set, 1)
                pe.wait_ge(dve_set, 2)
                with pe.Fori(0, B) as i:
                    pe.wait_ge(*xn_made.at(i, 1))
                    pe.wait_ge(*finished.at(i, 0))
                    for t in range(NT):
                        last = pe.transpose(pA[:, t * P:(t + 1) * P], xn[:, t, :], ident[:, :])
                    last.then_inc(xT_ready.sem, 1)
                    pe.wait_ge(*xT_kept.at(i, 1))
                    for n, dst in enumerate((pA[:, :], pB[:, :], pS[:, 0, :], pS[:, 1, :])):
                        pe.matmul(dst, weff[:, n, :], xnT[:, :], start=True, stop=True).then_inc(proj_ready.sem, 1)
                    for t in range(NT):
                        last = pe.matmul(pT[:, 0, t * P:(t + 1) * P], xnT[:, t * P:(t + 1) * P], weff[:, 4, :], start=True, stop=True)
                    last.then_inc(proj_ready.sem, 1)

                    def scores(n):
                        h, t, k = n // NT, n % NT, k_of(n)
                        if n >= SB:
                            pe.wait_ge(*exp_made.at(i, n - SB + 1))
                        pe.matmul(pS[:, n % SB, 0:k], qs[:, h, t * P:k], ks[:, h, 0:k], start=True, stop=True)
                        pe.matmul(pS[:, n % SB, t * P:k], identb[:, :], maskb[:, :], start=False, stop=True,
                                  skip_group_check=True).then_inc(scored.sem, 1)

                    def turn(n):
                        pe.wait_ge(*exp_made.at(i, n + 1))
                        if n >= TB:
                            kept_wait(pe, i, n - TB)
                        for u in range(n % NT + 1):
                            last = pe.transpose(pT[:, n % TB, u * P:(u + 1) * P], prob[:, n % 4, u * P:(u + 1) * P], ident[:, :])
                        last.then_inc(probT_ready.sem, 1)

                    def attend(n):
                        h, t = n // NT, n % NT
                        kept_wait(pe, i, n)
                        for u in range(t + 1):
                            last = pe.matmul(pY[:, t * P + h * HD:t * P + (h + 1) * HD], probT[:, n % 3, u * P:(u + 1) * P],
                                             v[:, u, h * HD:(h + 1) * HD], start=(u == 0), stop=(u == t))
                        last.then_inc(attended.sem, 1)

                    pe.wait_ge(terms_read, i * 16 * 2 * len(TERMS) + 16 * 2 * len(TERMS))
                    pe.wait_ge(*v_kept.at(i, 1))
                    for n in range(ITEMS + 4):
                        if n < ITEMS:
                            scores(n)
                        if 0 <= n - 2 < ITEMS:
                            turn(n - 2)
                        if 0 <= n - 4 < ITEMS:
                            attend(n - 4)
                    for t in range(NT):
                        pe.matmul(pA[:, t * E:(t + 1) * E], xnT[:, t * P:(t + 1) * P], rw[:, :], start=True, stop=False)
                        last = pe.matmul(pA[:, t * E:(t + 1) * E], ones[:, :], rb[:, :], start=False, stop=True)
                    last.then_inc(lg_ready.sem, 1)
                    pe.wait_ge(*y_made.at(i, 1))
                    for t in range(NT):
                        last = pe.transpose(pY[:, t * P:(t + 1) * P], yn[:, t, :], ident[:, :])
                    last.then_inc(yT_ready.sem, 1)

                    def down(e):
                        pe.wait_ge(*hid_made.at(i, (e + 1) * FC))
                        if e >= TB:
                            pe.wait_ge(*added.at(i, e - TB + 1))
                        for t in range(NT):
                            for c in range(FC):
                                last = pe.matmul(pT[:, e % TB, t * D:(t + 1) * D], hid[:, e % 2, c, t * P:(t + 1) * P], wdown[:, e * FC + c, :],
                                                 start=(c == 0), stop=(c == FC - 1))
                        last.then_inc(down_ready.sem, 1)

                    for e in range(E):
                        for c in range(FC):
                            n = e * FC + c
                            if n >= SB:
                                pe.wait_ge(*hid_made.at(i, n - SB + 1))
                            pe.matmul(pS[:, n % SB, :], wup[:, e, c * P:(c + 1) * P], xnT[:, :], start=True, stop=True).then_inc(up_ready.sem, 1)
                        if e >= 1:
                            down(e - 1)
                        if e == 0:
                            pe.wait_ge(*yT_kept.at(i, 1))
                            for t in range(NT):
                                last = pe.matmul(pB[:, t * P:(t + 1) * P], yT[:, t * P:(t + 1) * P], wc[:, :], start=True, stop=True)
                            last.then_inc(s_ready.sem, 1)
                    down(E - 1)


def host_arrays(inputs):
    a = {k: np.ascontiguousarray(v) for k, v in inputs.items()}
    out = {}
    keep = lambda *names: out.update({n: a[n] for n in names})
    t = lambda z: np.ascontiguousarray(z.T)
    out["x0"] = a["L0_attn_x"].reshape(B * S, D)
    keep("L0_attn_w_q", "L0_attn_w_k", "L0_attn_w_v2")
    out["L0_wv1T"] = t(a["L0_attn_w_v1"])
    out["L0_wgT"], out["L0_wuT"], out["L0_wdT"] = t(a["L0_ffn_w_gate"]), t(a["L0_ffn_w_up"]), t(a["L0_ffn_w_down"])
    out["ident"] = np.eye(P, dtype=np.float32)
    out["identb"] = np.eye(P).astype(mybir.dt.np(BF16))
    out["maskb"] = (BIG * (np.arange(P)[None, :] > np.arange(P)[:, None])).astype(mybir.dt.np(BF16))
    t = lambda z: np.ascontiguousarray(z.T)
    pad = lambda z: np.concatenate([z, np.zeros((HID4P - HID4, D), z.dtype)])
    for n in ("L1_attn_Wq", "L1_attn_Wr", "L1_attn_Wout", "L1_ffn_w_down"):
        out[n] = a[n]
    out["L1_WqT"], out["L1_WvT"] = t(a["L1_attn_Wq"]), t(a["L1_attn_Wv"])
    out["L1_uT"], out["L1_vT"] = t(a["L1_attn_u_bias"]), t(a["L1_attn_v_bias"])
    out["L1_gammaT"], out["L1_betaT"] = a["L1_attn_gamma"].reshape(D, 1), a["L1_attn_beta"].reshape(D, 1)
    out["L1_bout"] = a["L1_attn_bout"].reshape(1, D)
    out["L1_wg"], out["L1_wu"] = pad(a["L1_ffn_w_gate"]), pad(a["L1_ffn_w_up"])
    out["ones_row"] = np.ones((1, P), np.float32)
    place = np.arange(B, dtype=np.float32)[:, None]
    div = np.exp(np.arange(0, D, 2, dtype=np.float32) * np.float32(-np.log(10000.0) / D)).astype(np.float32)
    ang = (place * div).astype(np.float32)
    pe = np.stack([np.sin(ang), np.cos(ang)], axis=-1).reshape(B, D).astype(np.float32)
    out["L1_peT"] = t(pe[::-1])
    tok = np.arange(P)
    r = np.arange(B * B)
    c = np.float32(1 / np.sqrt(D))
    own_i = (r[:, None] // B == tok[None, :] // 16).astype(np.float32) * c
    out["L1_own_i"] = np.ascontiguousarray(np.tile(own_i, (1, NT)))
    own_b = (np.arange(16)[:, None] == tok[None, :] % 16).astype(np.float32)
    out["L1_own_b"] = np.ascontiguousarray(np.tile(own_b, (1, NT)))
    i, jj, j = r[:, None] // B, r[:, None] % B, tok[None, :] // 16
    put = (((jj == 7 + j - i) & (j <= i)) | ((jj == j - i - 2) & (j >= i + 2))).astype(np.float32)
    out["L1_is_own"] = np.ascontiguousarray(np.broadcast_to((r % B >= 7 - r // B), (P, B * B))).astype(np.float32)
    out["L1_is_next"] = np.ascontiguousarray(np.broadcast_to((r % B <= 5 - r // B), (P, B * B))).astype(np.float32)
    late = np.ones((B, B, P), np.float32)
    late[0] = np.arange(B)[:, None] <= tok[None, :] % 16
    out["L1_late"] = late.reshape(B, B * P)
    out["L1_place"] = np.concatenate([put, np.float32(-BIG) * (1 - own_b)]).astype(np.float32)
    t = lambda z: np.ascontiguousarray(z.T)
    for n in ("q", "k", "v"):
        out[f"L3_W{n}T"] = np.ascontiguousarray(a[f"L3_attn_W{n}_down"].reshape(D, 16, 64).transpose(2, 1, 0))
    for n in ("Wq_up_c", "Wq_up_e", "Wk_up_c", "Wk_up_e", "Wv_up", "Wc"):
        out[f"L3_attn_{n}"] = a[f"L3_attn_{n}"]
    inv_freq = (1.0 / np.float32(10000.0) ** (np.arange(0, 4, 2, dtype=np.float32) / np.float32(4))).astype(np.float32)
    ang = (np.arange(S, dtype=np.float32)[:, None] * inv_freq[None, :]).astype(np.float32)
    ang = np.concatenate([ang, ang], axis=-1)
    cos, sin = np.ones((S, HD), np.float32), np.zeros((S, HD), np.float32)
    cos[:, 4:], sin[:, 4:] = np.cos(ang), np.sin(ang)
    cos, sin = np.tile(cos.T, (HN, 1)), np.tile(sin.T, (HN, 1))
    neg = np.float32(-1 / np.sqrt(HD))
    out["L3_cosq"], out["L3_sinq"] = np.ascontiguousarray(cos), np.ascontiguousarray(sin)
    out["L3_cosk"], out["L3_sink"] = np.ascontiguousarray(cos * neg), np.ascontiguousarray(sin * neg)
    out["L3_ffn_router_w"] = a["L3_ffn_router_w"]
    out["L3_rb"] = a["L3_ffn_router_b"].reshape(1, 8)
    out["L3_earlier"] = np.ascontiguousarray(np.broadcast_to(np.tril(np.ones((8, 8), np.float32), -1), (P, 8, 8)))
    out["L3_upT"] = np.ascontiguousarray(a["L3_ffn_expert_up"].transpose(2, 0, 1))
    out["L3_downT"] = np.ascontiguousarray(a["L3_ffn_expert_down"].transpose(2, 0, 1).reshape(4, P, 8, D).transpose(1, 2, 0, 3).reshape(P, 32, D))
    pad = lambda z: np.concatenate([z, np.zeros((HID4P - HID4, D), z.dtype)])
    for n in ("L2_attn_w_attn", "L2_attn_w_proj", "L2_ffn_w_down"):
        out[n] = a[n]
    ek, ev = a["L2_attn_embk"], a["L2_attn_embv"]
    out["L2_last_k"] = np.tile(ek[-1], HN).reshape(D, 1)
    out["L2_place_k"] = np.ascontiguousarray(ek[::-1].T)
    out["L2_place_last"] = ek[-1].reshape(HD, 1)
    out["L2_last_v"] = np.tile(ev[-1], HN).reshape(1, D)
    out["L2_place_v"] = np.ascontiguousarray(ev[::-1])
    out["L2_wg"], out["L2_wu"] = pad(a["L2_ffn_w_gate"]), pad(a["L2_ffn_w_up"])
    return out


def build(nc, w, result):
    x1, x2, x3 = [nc.dram_tensor(f"x_after_{n}", (B * S, D), F32).ap() for n in range(3)]
    layer0(nc, w, w["x0"], x1)
    layer1(nc, w, x1, x2)
    layer2(nc, w, x2, x3)
    layer3(nc, w, x3, result)


def kernel(**inputs):
    import concourse.bacc as bacc
    from concourse.bass_utils import run_bass_kernel_spmd

    nc = bacc.Bacc("TRN2", target_bir_lowering=False, num_devices=1)
    arrays = host_arrays(inputs)
    w = {name: nc.dram_tensor(name, a.shape, mybir.dt.from_np(a.dtype), kind="ExternalInput").ap() for name, a in arrays.items()}
    result = nc.dram_tensor("result", (B * S, D), F32, kind="ExternalOutput").ap()
    build(nc, w, result)
    r = run_bass_kernel_spmd(nc, [arrays], core_ids=[0])
    return r.results[0]["result"].reshape(B, S, D)
```

```python
from contextlib import ExitStack, contextmanager

import numpy as np

import concourse.bass as bass
from concourse import mybir

F32 = mybir.dt.float32
BF16 = mybir.dt.bfloat16
I32 = mybir.dt.int32
ALU = mybir.AluOpType
ACT = mybir.ActivationFunctionType
AX = mybir.AxisListType

P = 128
D = 128
B, S = 8, 512
NT = S // P
EPS = 1e-5
BIG = 1e30


class Event:

    def __init__(self, scope, name, per, credit=False, step=1):
        self.sem = scope.sem(name)
        self.per, self.step = per * step, step
        self.base = self.per if credit else 0

    def at(self, i, n):
        return self.sem, i * self.per + self.base + n * self.step


class Chain:

    def __init__(self, eng, event, i):
        self.eng, self.event, self.i, self.n = eng, event, i, 0

    def then(self, instruction):
        self.n += 1
        instruction.then_inc(self.event.sem, 1)
        self.eng.wait_ge(*self.event.at(self.i, self.n))

    def done(self):
        assert self.n == self.event.per, f"chain of {self.n} steps"


class Scope:

    def __init__(self, nc, stack, prefix):
        self.nc, self.stack, self.prefix = nc, stack, prefix
        self.semaphores = []
        stack.callback(self.clear)

    def clear(self):
        self.nc.clear_and_free_semaphores(self.semaphores)
        self.nc.all_engine_barrier()

    def sb(self, name, shape, dt=F32):
        return self.stack.enter_context(self.nc.sbuf_tensor(self.prefix + name, shape, dt))

    def ps(self, name, shape, dt=F32):
        return self.stack.enter_context(self.nc.psum_tensor(self.prefix + name, shape, dt))

    def sem(self, name):
        self.semaphores.append(self.nc.alloc_semaphore(name=self.prefix + name))
        return self.semaphores[-1]

    def ev(self, name, per, credit=False):
        return Event(self, name, per, credit)

    def ev16(self, name, per):
        return Event(self, name, per, step=16)


def rows(x, i):
    return x.rearrange("(b t p) d -> b p t d", b=B, p=P)[i, :, :, :]


def quantise(dve, link, q, src, dst, n):
    nb = n // 16
    blocks = lambda z: z.rearrange("p (b k) -> p b k", k=16)
    each = lambda z: z[:, 0:nb].unsqueeze(2).to_broadcast([P, nb, 16])
    norm, mag, grid, low = q.norm[:, 0:n], q.mag[:, 0:n], q.grid[:, 0:n], q.low[:, 0:n]
    link.then(dve.tensor_reduce(q.peak[:, 0:nb], blocks(src), AX.X, ALU.max, apply_absolute_value=True))
    yield
    link.then(dve.tensor_scalar(q.scale[:, 0:nb], q.peak[:, 0:nb], float(np.float32(1 / 6)), 1e-12, ALU.mult, ALU.max))
    yield
    link.then(dve.reciprocal(q.rscale[:, 0:nb], q.scale[:, 0:nb]))
    yield
    link.then(dve.tensor_tensor(blocks(norm), blocks(src), each(q.rscale), ALU.mult))
    yield
    link.then(dve.tensor_scalar(mag.bitcast(I32), norm.bitcast(I32), 0x7FFFFFFF, None, ALU.bitwise_and))
    yield
    link.then(dve.tensor_scalar(grid, mag, 1.0, None, ALU.max))
    yield
    dve.tensor_scalar(low, mag, 0.25, 0.5, ALU.is_gt, ALU.mult)
    link.then(dve.tensor_tensor(grid.bitcast(I32), grid.bitcast(I32), q.half_step[:, 0:n], ALU.add))
    yield
    link.then(dve.tensor_scalar(grid.bitcast(I32), grid.bitcast(I32), -0x400000, None, ALU.bitwise_and))
    yield
    link.then(dve.scalar_tensor_tensor(grid, mag, 0.75, grid, ALU.is_gt, ALU.mult))
    yield
    link.then(dve.tensor_tensor(grid, grid, low, ALU.max))
    yield
    link.then(dve.scalar_tensor_tensor(grid.bitcast(I32), norm.bitcast(I32), -0x80000000, grid.bitcast(I32), ALU.bitwise_and, ALU.bitwise_or))
    yield
    link.then(dve.tensor_tensor(blocks(dst), blocks(grid), each(q.scale), ALU.mult))
    yield


QUANTISE_STEPS = 12


class QuantBuffers:
    def __init__(self, m, n):
        self.norm, self.mag, self.grid, self.low = [m.sb("q_" + s, [P, n]) for s in ("norm", "mag", "grid", "low")]
        self.half_step = m.sb("q_half_step", [P, n], I32)
        self.peak, self.scale, self.rscale = [m.sb("q_" + s, [P, n // 16]) for s in ("peak", "scale", "rscale")]


HN, HD = 16, 8
ITEMS = HN * NT
TERMS = ((0, 0), (0, 1), (1, 0), (1, 1), (0, 2), (2, 0))
KR6 = len(TERMS) * HD
KR9 = KR6 + 3
PIECES = 3
SB, TB = 3, 2


def split3(eng, link, src, parts, rest):
    link.then(eng.tensor_copy(parts[0], src))
    link.then(eng.tensor_tensor(rest, src, parts[0], ALU.subtract))
    link.then(eng.tensor_copy(parts[1], rest))
    link.then(eng.tensor_tensor(parts[2], rest, parts[1], ALU.subtract))


def layer0(nc, w, x_in, x_out):
    KD, HID = 64, 384
    HC = HID // P
    with ExitStack() as stack:
        m = Scope(nc, stack, "a_")
        ident, maskb, identb = m.sb("ident", [P, P]), m.sb("maskb", [P, P], BF16), m.sb("identb", [P, P], BF16)
        wq, wk = m.sb("wq", [P, KD]), m.sb("wk", [P, KD])
        wv1T, wv2, wv = m.sb("wv1T", [KD, P]), m.sb("wv2", [KD, P]), m.sb("wv", [P, P])
        wint = [m.sb(f"wint{n}", [P, HID], I32) for n in range(3)]
        wg, wu, wd = [m.sb(n, [P, HID]) for n in ("wg", "wu", "wd")]
        half, eps = m.sb("half", [P, NT]), m.sb("eps", [P, NT])
        x, spare = m.sb("x", [P, NT, D]), m.sb("spare", [P, 1])
        stat, mv, rstd = m.sb("stat", [P, NT, 6]), m.sb("mv", [P, NT, 2]), m.sb("rstd", [P, NT])
        xn, xnT = m.sb("xn", [P, NT, D]), m.sb("xnT", [P, S])
        qT, kT, v = m.sb("qT", [KD, S]), m.sb("kT", [KD, S]), m.sb("v", [P, NT, D])
        th, act_in, hT = m.sb("th", [P, 2, S]), m.sb("act_in", [P, S]), m.sb("hT", [P, HC, S])
        low, total, inv = m.sb("low", [P, NT]), m.sb("total", [P, NT]), m.sb("inv", [P, NT])
        prob, probT = m.sb("prob", [P, 2, S]), m.sb("probT", [P, 2, S])
        s_out, g_a, x_new = m.sb("s_out", [P, NT, D]), m.sb("g_a", [P, NT, D]), m.sb("x_new", [P, NT, D])
        g_th = m.sb("g_th", [P, NT, D])
        pX, pQ, pK, pV = [m.ps(n, [P, S]) for n in ("pX", "pQ", "pK", "pV")]
        pS, pP = m.ps("pS", [P, 2, S]), m.ps("pP", [P, 2, S])
        pY, pF, pG, pU = pX, pQ, pK, pV

        loaded, pool_set, dve_set = m.sem("loaded"), m.sem("pool_set"), m.sem("dve_set")
        wv_made, x_read, x_sent = m.sem("wv_made"), m.sem("x_read"), m.sem("x_sent")
        centred = m.ev("centred", 1)
        rstd_made = m.ev("rstd_made", 2)
        xn_made = m.ev("xn_made", 1)
        xT_ready = m.ev("xT_ready", 1)
        xT_kept = m.ev("xT_kept", 1)
        qkv_ready = m.ev("qkv_ready", 3)
        q_kept = m.ev("q_kept", 1)
        kv_kept = m.ev("kv_kept", 2)
        gu_ready = m.ev("gu_ready", HC)
        gate_tanh = m.ev("gate_tanh", HC)
        h_made = m.ev("h_made", HC)
        scored = m.ev("scored", NT)
        low_made = m.ev("low_made", NT)
        exp_made = m.ev("exp_made", NT)
        probT_ready = m.ev("probT_ready", NT)
        probT_kept = m.ev("probT_kept", NT)
        attended = m.ev("attended", NT)
        ffn_ready = m.ev("ffn_ready", 1)
        ffn_tanh = m.ev("ffn_tanh", 1)
        finished = m.ev("finished", 1, credit=True)
        chain = m.ev("chain", 9)
        stored = m.ev("stored", 1, credit=True)
        weights = [(ident[:, :], w["ident"]), (identb[:, :], w["identb"]), (maskb[:, :], w["maskb"]),
                   (wq[:, :], w["L0_attn_w_q"]), (wk[:, :], w["L0_attn_w_k"]),
                   (wv1T[:, :], w["L0_wv1T"]), (wv2[:, :], w["L0_attn_w_v2"]),
                   (wint[0][:, :], w["L0_wgT"]), (wint[1][:, :], w["L0_wuT"]),
                   (wint[2][:, :].rearrange("p (c d) -> p c d", d=D), w["L0_wdT"].rearrange("(c p) d -> p c d", p=P))]
        with nc.Block() as block:
            @block.sync
            def _(sp):
                for dst, src in weights:
                    sp.dma_start(dst, src).then_inc(loaded, 16)
                sp.wait_ge(loaded, 16 * len(weights))
                with sp.Fori(0, B) as i:
                    sp.wait_ge(*finished.at(i, 0))
                    sp.nop()
                    sp.dma_start(x[:, :, :], rows(x_in, i)).then_inc(x_read, 16)

            @block.gpsimd
            def _(pool):
                pool.memset(half[:, :], -0.5).then_inc(pool_set, 1)
                pool.memset(eps[:, :], EPS).then_inc(pool_set, 1)
                pool.sem_inc(stored.sem, 1)
                pool.wait_ge(pool_set, 2)
                with pool.Fori(0, B) as i:
                    pool.wait_ge(*centred.at(i, 1))
                    pool.tensor_tensor(rstd[:, :], mv[:, :, 1], eps[:, :], ALU.add).then_inc(rstd_made.sem, 1)
                    pool.wait_ge(*rstd_made.at(i, 1))
                    pool.tensor_tensor(rstd[:, :], rstd[:, :], half[:, :], ALU.pow).then_inc(rstd_made.sem, 1)
                    pool.wait_ge(*finished.at(i, 1))
                    pool.dma_start(rows(x_out, i), x_new[:, :, :]).then_inc(x_sent, 16)
                    pool.wait_ge(x_sent, i * 16 + 16)
                    pool.sem_inc(stored.sem, 1)

            @block.vector
            def _(dve):
                dve.wait_ge(loaded, 16 * len(weights))
                for src, dst in zip(wint, (wg, wu, wd)):
                    dve.tensor_scalar(dst[:, :], src[:, :], float(np.float32(1.0 / 127.0)), None, ALU.mult)
                dve.wait_ge(wv_made, 1)
                dve.tensor_copy(wv[:, :], pV[:, 0:D]).then_inc(dve_set, 1)
                dve.sem_inc(finished.sem, 1)
                with dve.Fori(0, B) as i:
                    link = Chain(dve, chain, i)
                    dve.wait_ge(x_read, i * 16 + 16)
                    for t in range(NT):
                        last = dve.bn_stats(stat[:, t, :], x[:, t, :])
                    link.then(last)
                    dve.memset(spare[:, :], 0.0)
                    for t in range(NT):
                        last = dve.bn_aggr(mv[:, t, :], stat[:, t, :])
                    last.then_inc(centred.sem, 1)
                    dve.wait_ge(*rstd_made.at(i, 2))
                    for t in range(NT):
                        last = dve.tensor_scalar(xn[:, t, :], x[:, t, :], mv[:, t, 0:1], rstd[:, t:t + 1], ALU.subtract, ALU.mult)
                    last.then_inc(xn_made.sem, 1)
                    dve.wait_ge(*qkv_ready.at(i, 2))
                    dve.tensor_scalar(kT[:, :], pK[0:KD, :], -float(KD) ** -0.5, None, ALU.mult).then_inc(kv_kept.sem, 1)
                    dve.wait_ge(*qkv_ready.at(i, 3))
                    dve.tensor_copy(v[:, :, :], pV[:, :].rearrange("p (t d) -> p t d", t=NT)).then_inc(kv_kept.sem, 1)

                    def hidden(c):
                        dve.wait_ge(*gate_tanh.at(i, c + 1))
                        link.then(dve.scalar_tensor_tensor(act_in[:, :], th[:, c % 2, :], 1.0, pG[:, :], ALU.add, ALU.mult))
                        dve.scalar_tensor_tensor(hT[:, c, :], act_in[:, :], 0.5, pU[:, :], ALU.mult, ALU.mult).then_inc(h_made.sem, 1)

                    def lowest(t):
                        dve.wait_ge(*scored.at(i, t + 1))
                        dve.tensor_reduce(low[:, t:t + 1], pS[:, t % 2, 0:(t + 1) * P], AX.X, ALU.min).then_inc(low_made.sem, 1)

                    def keep_probT(t):
                        dve.wait_ge(*probT_ready.at(i, t + 1))
                        dve.tensor_copy(probT[:, t % 2, 0:(t + 1) * P], pP[:, t % 2, 0:(t + 1) * P]).then_inc(probT_kept.sem, 1)

                    hidden(0)
                    lowest(0)
                    lowest(1)
                    hidden(1)
                    keep_probT(0)
                    lowest(2)
                    hidden(2)
                    keep_probT(1)
                    lowest(3)
                    keep_probT(2)
                    keep_probT(3)
                    dve.wait_ge(*exp_made.at(i, NT))
                    link.then(dve.reciprocal(inv[:, :], total[:, :]))
                    dve.wait_ge(*attended.at(i, NT))
                    link.then(dve.tensor_tensor(s_out[:, :, :], pY[:, :].rearrange("p (t d) -> p t d", t=NT),
                                                inv[:, :].unsqueeze(2).to_broadcast([P, NT, D]), ALU.mult))
                    dve.wait_ge(*ffn_tanh.at(i, 1))
                    link.then(dve.scalar_tensor_tensor(g_a[:, :, :], g_th[:, :, :], 1.0,
                                                       pF[:, :].rearrange("p (t d) -> p t d", t=NT), ALU.add, ALU.mult))
                    link.then(dve.scalar_tensor_tensor(g_a[:, :, :], g_a[:, :, :], 0.5, s_out[:, :, :], ALU.mult, ALU.mult))
                    dve.wait_ge(*stored.at(i, 0))
                    link.then(dve.tensor_tensor(x_new[:, :, :], g_a[:, :, :], x[:, :, :], ALU.add))
                    dve.sem_inc(finished.sem, 1)
                    link.done()

            @block.scalar
            def _(act):
                with act.Fori(0, B) as i:
                    act.wait_ge(*xT_ready.at(i, 1))
                    act.copy(xnT[:, :], pX[:, :]).then_inc(xT_kept.sem, 1)
                    act.wait_ge(*qkv_ready.at(i, 1))
                    act.copy(qT[:, :], pQ[0:KD, :]).then_inc(q_kept.sem, 1)

                    def gate(c):
                        act.wait_ge(*gu_ready.at(i, c + 1))
                        act.activation(th[:, c % 2, :], pG[:, :], ACT.Tanh, scale=0.5).then_inc(gate_tanh.sem, 1)

                    def exps(t):
                        act.wait_ge(*low_made.at(i, t + 1))
                        if t >= 2:
                            act.wait_ge(*probT_ready.at(i, t - 1))
                        n = (t + 1) * P
                        act.activation(prob[:, t % 2, 0:n], pS[:, t % 2, 0:n], ACT.Exp, bias=low[:, t:t + 1], scale=-1.0,
                                       accum_out=total[:, t:t + 1]).then_inc(exp_made.sem, 1)

                    gate(0)
                    exps(0)
                    exps(1)
                    gate(1)
                    exps(2)
                    gate(2)
                    exps(3)
                    act.wait_ge(*ffn_ready.at(i, 1))
                    act.activation(g_th[:, :, :], pF[:, :].rearrange("p (t d) -> p t d", t=NT), ACT.Tanh, scale=0.5).then_inc(ffn_tanh.sem, 1)

            @block.tensor
            def _(pe):
                pe.wait_ge(loaded, 16 * len(weights))
                pe.matmul(pV[:, 0:D], wv1T[:, :], wv2[:, :], start=True, stop=True).then_inc(wv_made, 1)
                pe.wait_ge(dve_set, 1)
                with pe.Fori(0, B) as i:
                    pe.wait_ge(*xn_made.at(i, 1))
                    pe.wait_ge(*finished.at(i, 0))
                    for t in range(NT):
                        last = pe.transpose(pX[:, t * P:(t + 1) * P], xn[:, t, :], ident[:, :])
                    last.then_inc(xT_ready.sem, 1)
                    pe.wait_ge(*xT_kept.at(i, 1))
                    pe.matmul(pQ[0:KD, :], wq[:, :], xnT[:, :], start=True, stop=True).then_inc(qkv_ready.sem, 1)
                    pe.matmul(pK[0:KD, :], wk[:, :], xnT[:, :], start=True, stop=True).then_inc(qkv_ready.sem, 1)
                    for t in range(NT):
                        last = pe.matmul(pV[:, t * P:(t + 1) * P], xnT[:, t * P:(t + 1) * P], wv[:, :], start=True, stop=True)
                    last.then_inc(qkv_ready.sem, 1)

                    def gate_up(c):
                        if c == 0:
                            pe.wait_ge(*kv_kept.at(i, 2))
                        else:
                            pe.wait_ge(*h_made.at(i, c))
                        pe.matmul(pG[:, :], wg[:, c * P:(c + 1) * P], xnT[:, :], start=True, stop=True)
                        pe.matmul(pU[:, :], wu[:, c * P:(c + 1) * P], xnT[:, :], start=True, stop=True).then_inc(gu_ready.sem, 1)

                    def scores(t):
                        if t == 0:
                            pe.wait_ge(*q_kept.at(i, 1))
                        if t >= 2:
                            pe.wait_ge(*exp_made.at(i, t - 1))
                        n = (t + 1) * P
                        pe.matmul(pS[:, t % 2, 0:n], qT[:, t * P:n], kT[:, 0:n], start=True, stop=True)
                        pe.matmul(pS[:, t % 2, t * P:n], identb[:, :], maskb[:, :], start=False, stop=True,
                                  skip_group_check=True).then_inc(scored.sem, 1)

                    def turn(t):
                        pe.wait_ge(*exp_made.at(i, t + 1))
                        if t >= 2:
                            pe.wait_ge(*probT_kept.at(i, t - 1))
                        for u in range(t + 1):
                            last = pe.transpose(pP[:, t % 2, u * P:(u + 1) * P], prob[:, t % 2, u * P:(u + 1) * P], ident[:, :])
                        last.then_inc(probT_ready.sem, 1)

                    def attend(t):
                        pe.wait_ge(*probT_kept.at(i, t + 1))
                        for u in range(t + 1):
                            last = pe.matmul(pY[:, t * P:(t + 1) * P], probT[:, t % 2, u * P:(u + 1) * P], v[:, u, :],
                                             start=(u == 0), stop=(u == t))
                        last.then_inc(attended.sem, 1)

                    gate_up(0)
                    scores(0)
                    scores(1)
                    turn(0)
                    gate_up(1)
                    scores(2)
                    attend(0)
                    turn(1)
                    gate_up(2)
                    scores(3)
                    attend(1)
                    turn(2)
                    attend(2)
                    turn(3)
                    attend(3)
                    pe.wait_ge(*h_made.at(i, HC))
                    for t in range(NT):
                        for c in range(HC):
                            last = pe.matmul(pF[:, t * P:(t + 1) * P], hT[:, c, t * P:(t + 1) * P], wd[:, c * D:(c + 1) * D],
                                             start=(c == 0), stop=(c == HC - 1))
                    last.then_inc(ffn_ready.sem, 1)


HID4 = 352
HID4P = 384
HC4 = HID4P // P


def layer1(nc, w, x_in, x_out):
    H, F = 8, 128
    BB = 16
    G = NT
    C = float(np.float32(1 / np.sqrt(D)))
    KR = B * B + BB
    with ExitStack() as stack:
        m = Scope(nc, stack, "b_")
        ident, ones, bout = m.sb("ident", [P, P]), m.sb("ones", [1, P]), m.sb("bout", [1, D])
        wq, wqT = m.sb("wq", [P, H * F]), m.sb("wqT", [P, H, D])
        wr = m.sb("wr", [P, H * F])
        wvT, wout, wvo = m.sb("wvT", [P, H, D]), m.sb("wout", [P, H, D]), m.sb("wvo", [P, H * D])
        peT = m.sb("peT", [P, B])
        uT, vT, gammaT, betaT = m.sb("uT", [P, H]), m.sb("vT", [P, H]), m.sb("gammaT", [P, 1]), m.sb("betaT", [P, 1])
        rel, gpos, gbias = m.sb("rel", [P, H, B, B]), m.sb("gpos", [P, H, B * B]), m.sb("gbias", [B * B, H])
        gnext, is_own, is_next = m.sb("gnext", [P, H, B * B]), m.sb("is_own", [P, B * B]), m.sb("is_next", [P, B * B])
        late = m.sb("late", [B * B, H, P])
        own_i, place = m.sb("own_i", [B * B, S]), m.sb("place", [KR, P])
        wnat, wqd = m.sb("wnat", [P, 2 * HID4P + HID4]), m.sb("wqd", [P, 2 * HID4P + HID4])
        wg, wu, wd = m.sb("wg", [P, HID4P]), m.sb("wu", [P, HID4P]), m.sb("wd", [P, HC4, D])
        half, eps, spare = m.sb("half", [P, NT]), m.sb("eps", [P, NT]), m.sb("spare", [P, 1])
        q4 = QuantBuffers(m, G * HID4)
        x, stat, mv, rstd = m.sb("x", [P, G, D]), m.sb("stat", [P, G, 6]), m.sb("mv", [P, G, 2]), m.sb("rstd", [P, G])
        xn, hh, hT = m.sb("xn", [P, G * D]), m.sb("hh", [P, G, D]), m.sb("hT", [P, S])
        xq, xqT, vo = m.sb("xq", [P, G * D]), m.sb("xqT", [P, S]), m.sb("vo", [P, G, H * D])
        qu, kT, pos = m.sb("qu", [P, 2, S]), m.sb("kT", [P, 2, S]), m.sb("pos", [KR, 2, S])
        top, total, inv = [m.sb(n, [P, 2, G]) for n in ("top", "total", "inv")]
        prob, probT = m.sb("prob", [P, 2, S]), m.sb("probT", [P, 2, S])
        th, act_in = m.sb("th", [P, 2, HID4]), m.sb("act_in", [P, HID4])
        hid, hidT = m.sb("hid", [P, G * HID4]), m.sb("hidT", [P, HC4, S])
        g_th, g_a, x_new = m.sb("g_th", [P, S]), m.sb("g_a", [P, S]), m.sb("x_new", [P, G, D])
        pA, pB, pQ, pR, pT, pO = [m.ps(n, [P, S]) for n in ("pA", "pB", "pQ", "pR", "pT", "pO")]
        pS = m.ps("pS", [P, 2, S])
        loaded, dve_set, pool_set, pe_set, x_read, x_sent = [m.sem(n) for n in ("loaded", "dve_set", "pool_set", "pe_set", "x_read", "x_sent")]
        late_read = m.sem("late_read")
        made_weights = m.ev("made_weights", QUANTISE_STEPS)
        centred, rstd_made = m.ev("centred", 2), m.ev("rstd_made", 4)
        hh_made, xq_made = m.ev("hh_made", 1), m.ev("xq_made", 1)
        turned_in = m.ev("turned_in", 2)
        xqT_kept, hT_kept = m.ev("xqT_kept", 1), m.ev("hT_kept", 1)
        gu_ready, gate_tanh, hid_made = m.ev("gu_ready", G), m.ev("gate_tanh", G), m.ev("hid_made", G)
        vo_ready, vo_kept = m.ev("vo_ready", 2 * G), m.ev("vo_kept", 2 * G)
        q_ready, pos_ready = m.ev("q_ready", H), m.ev("pos_ready", H)
        k_kept, qu_made, pos_made = m.ev("k_kept", H), m.ev("qu_made", H), m.ev("pos_made", H)
        scored, top_made, exp_made = m.ev("scored", H), m.ev("top_made", H), m.ev("exp_made", H)
        own_made = m.ev("own_made", H)
        inv_made, normed = m.ev("inv_made", H), m.ev("normed", H)
        probT_ready, probT_kept, attended = m.ev("probT_ready", H), m.ev("probT_kept", H), m.ev("attended", H)
        hid_quantised = m.ev("hid_quantised", 1)
        hidT_ready, hidT_kept = m.ev("hidT_ready", HC4), m.ev("hidT_kept", HC4)
        ffn_ready, ffn_tanh = m.ev("ffn_ready", 1), m.ev("ffn_tanh", 1)
        finished = m.ev("finished", 1, credit=True)
        stored = m.ev("stored", 1, credit=True)
        chain = m.ev("chain", 2 + 1 + 2 * QUANTISE_STEPS + G + 3)
        of_batch = lambda t, c, a: t.rearrange("(a c g b) d -> c a b g d", a=B, c=B, g=G)[c, a, :, :, :]
        heads = lambda t: t.rearrange("(h f) d -> f h d", f=F)
        weights = [(ident[:, :], w["ident"]), (ones[:, :], w["ones_row"]), (bout[:, :], w["L1_bout"]), (wq[:, :], w["L1_attn_Wq"]),
                   (wqT[:, :, :], heads(w["L1_WqT"])), (wr[:, :], w["L1_attn_Wr"]), (wvT[:, :, :], heads(w["L1_WvT"])),
                   (wout[:, :, :], heads(w["L1_attn_Wout"])), (peT[:, :], w["L1_peT"]), (uT[:, :], w["L1_uT"]),
                   (vT[:, :], w["L1_vT"]), (gammaT[:, :], w["L1_gammaT"]), (betaT[:, :], w["L1_betaT"]),
                   (own_i[:, :], w["L1_own_i"]), (is_own[:, :], w["L1_is_own"]), (is_next[:, :], w["L1_is_next"]), (place[:, :], w["L1_place"]),
                   (pos[B * B:KR, 0, :], w["L1_own_b"]), (pos[B * B:KR, 1, :], w["L1_own_b"]),
                   (wnat[:, 0:HID4P].rearrange("p (c d) -> p c d", c=HC4), w["L1_wg"].rearrange("(c p) d -> p c d", p=P)),
                   (wnat[:, HID4P:2 * HID4P].rearrange("p (c d) -> p c d", c=HC4), w["L1_wu"].rearrange("(c p) d -> p c d", p=P)),
                   (wnat[:, 2 * HID4P:], w["L1_ffn_w_down"])]
        SETS = 8
        with nc.Block() as block:
            @block.sync
            def _(sp):
                for dst, src in weights:
                    sp.dma_start(dst, src).then_inc(loaded, 16)
                with sp.Fori(0, B) as i:
                    sp.wait_ge(*finished.at(i, 0))
                    sp.nop()
                    for a in range(B):
                        sp.dma_start(x[a * BB:(a + 1) * BB, :, :], of_batch(x_in, i, a)).then_inc(x_read, 16)
                    sp.dma_start(late[:, :, :].rearrange("p h t -> p (h t)"), w["L1_late"][i, :].partition_broadcast(B * B)).then_inc(late_read, 16)

            @block.gpsimd
            def _(pool):
                pool.memset(half[:, :], -0.5).then_inc(pool_set, 1)
                pool.memset(eps[:, :], EPS).then_inc(pool_set, 1)
                pool.memset(q4.half_step[:, :], 0x1FFFFF).then_inc(pool_set, 1)
                pool.sem_inc(stored.sem, 1)
                pool.wait_ge(pool_set, 3)
                with pool.Fori(0, B) as i:
                    for k in range(2):
                        pool.wait_ge(*centred.at(i, k + 1))
                        pool.tensor_tensor(rstd[:, :], mv[:, :, 1], eps[:, :], ALU.add).then_inc(rstd_made.sem, 1)
                        pool.wait_ge(*rstd_made.at(i, 2 * k + 1))
                        pool.tensor_tensor(rstd[:, :], rstd[:, :], half[:, :], ALU.pow).then_inc(rstd_made.sem, 1)
                    for n in range(H):
                        pool.wait_ge(*inv_made.at(i, n + 1))
                        z = prob[:, n % 2, :].rearrange("p (g j) -> p g j", g=G)
                        pool.tensor_tensor(z, z, inv[:, n % 2, :].unsqueeze(2).to_broadcast([P, G, P]), ALU.mult).then_inc(normed.sem, 1)
                    pool.wait_ge(*finished.at(i, 1))
                    for a in range(B):
                        pool.dma_start(of_batch(x_out, i, a), x_new[a * BB:(a + 1) * BB, :, :]).then_inc(x_sent, 16)
                    pool.wait_ge(x_sent, i * 16 * B + 16 * B)
                    pool.sem_inc(stored.sem, 1)

            @block.vector
            def _(dve):
                dve.wait_ge(loaded, 16 * len(weights))
                dve.wait_ge(pool_set, 3)
                for _ in quantise(dve, Chain(dve, made_weights, 0), q4, wnat[:, :], wqd[:, :], 2 * HID4P + HID4):
                    pass
                dve.sem_inc(dve_set, 1)
                dve.wait_ge(pe_set, 1)
                dve.tensor_copy(rel[:, :, :, :], pA[:, 0:H * B].rearrange("p (h j) -> p h j", h=H).unsqueeze(2).to_broadcast([P, H, B, B])).then_inc(dve_set, 1)
                dve.wait_ge(pe_set, 2)
                for n in range(H):
                    for dst, part in ((gpos, is_own), (gnext, is_next)):
                        dve.tensor_tensor(dst[:, n, :].rearrange("p (a j) -> p a j", a=B),
                                          pB[:, n * B:(n + 1) * B].unsqueeze(1).to_broadcast([P, B, B]),
                                          part[:, :].rearrange("p (a j) -> p a j", a=B), ALU.mult)
                dve.tensor_copy(gbias[:, :], pQ[0:B * B, 0:H])
                dve.tensor_copy(wvo[:, 0:S], pS[:, 0, :])
                dve.tensor_copy(wvo[:, S:2 * S], pS[:, 1, :])
                dve.tensor_copy(wg[:, :], pR[:, 0:HID4P])
                dve.tensor_copy(wu[:, :], pT[:, 0:HID4P])
                dve.tensor_copy(wd[:, 0:2, :], pO[:, 0:2 * D].rearrange("p (c d) -> p c d", c=2))
                dve.tensor_copy(wd[0:HID4 - 2 * P, 2, :], pO[0:HID4 - 2 * P, 2 * D:3 * D]).then_inc(dve_set, 1)
                dve.sem_inc(finished.sem, 1)
                with dve.Fori(0, B) as i:
                    link = Chain(dve, chain, i)

                    def stats(k, src, dst):
                        for t in range(G):
                            last = dve.bn_stats(stat[:, t, :], src(t))
                        link.then(last)
                        dve.memset(spare[:, :], 0.0)
                        for t in range(G):
                            last = dve.bn_aggr(mv[:, t, :], stat[:, t, :])
                        last.then_inc(centred.sem, 1)
                        dve.wait_ge(*rstd_made.at(i, 2 * k + 2))
                        for t in range(G):
                            last = dve.tensor_scalar(dst(t), src(t), mv[:, t, 0:1], rstd[:, t:t + 1], ALU.subtract, ALU.mult)
                        return last

                    dve.wait_ge(x_read, i * 16 * B + 16 * B)
                    link.then(stats(0, lambda t: x[:, t, :], lambda t: xn[:, t * D:(t + 1) * D]))
                    stats(1, lambda t: xn[:, t * D:(t + 1) * D], lambda t: hh[:, t, :]).then_inc(hh_made.sem, 1)
                    for _ in quantise(dve, link, q4, xn[:, :], xq[:, :], G * D):
                        pass
                    dve.sem_inc(xq_made.sem, 1)
                    dve.wait_ge(*turned_in.at(i, 2))
                    dve.tensor_scalar(hT[:, :], pB[:, :], gammaT[:, :], betaT[:, :], ALU.mult, ALU.add).then_inc(hT_kept.sem, 1)
                    for g in range(G):
                        dve.wait_ge(*gate_tanh.at(i, g + 1))
                        link.then(dve.scalar_tensor_tensor(act_in[:, :], th[:, g % 2, :], 1.0, pA[:, 0:HID4], ALU.add, ALU.mult))
                        dve.scalar_tensor_tensor(hid[:, g * HID4:(g + 1) * HID4], act_in[:, :], 0.5, pB[:, 0:HID4], ALU.mult, ALU.mult).then_inc(hid_made.sem, 1)
                    dve.wait_ge(*hid_made.at(i, G))
                    steps = quantise(dve, link, q4, hid[:, :], hid[:, :], G * HID4)

                    def operands(n):
                        dve.wait_ge(*k_kept.at(i, n + 1))
                        if n >= 2:
                            dve.wait_ge(*scored.at(i, n - 1))
                        dve.tensor_scalar(qu[:, n % 2, :], kT[:, n % 2, :], uT[:, n:n + 1], C, ALU.add, ALU.mult).then_inc(qu_made.sem, 1)
                        dve.wait_ge(*pos_ready.at(i, n + 1))
                        dve.scalar_tensor_tensor(pos[0:B * B, n % 2, :], pR[0:B * B, :], gbias[:, n:n + 1], own_i[:, :], ALU.add, ALU.mult).then_inc(own_made.sem, 1)
                        dve.wait_ge(*own_made.at(i, n + 1))
                        first = pos[0:B * B, n % 2, 0:P]
                        dve.tensor_tensor(first, first, late[:, n, :], ALU.mult).then_inc(pos_made.sem, 1)

                    dve.wait_ge(late_read, i * 16 + 16)

                    def highest(n):
                        dve.wait_ge(*scored.at(i, n + 1))
                        dve.tensor_reduce(top[:, n % 2, :], pS[:, n % 2, :].rearrange("p (g j) -> p g j", g=G), AX.X, ALU.max, negate=True).then_inc(top_made.sem, 1)

                    def inverse(n):
                        dve.wait_ge(*exp_made.at(i, n + 1))
                        dve.reciprocal(inv[:, n % 2, :], total[:, n % 2, :]).then_inc(inv_made.sem, 1)

                    for k in range(H + 2):
                        if k < H:
                            operands(k)
                        if 0 <= k - 1 < H:
                            highest(k - 1)
                        next(steps, None)
                        if 0 <= k - 2 < H:
                            inverse(k - 2)
                    for _ in steps:
                        pass
                    dve.sem_inc(hid_quantised.sem, 1)
                    dve.wait_ge(*ffn_tanh.at(i, 1))
                    link.then(dve.scalar_tensor_tensor(g_a[:, :], g_th[:, :], 1.0, pR[:, :], ALU.add, ALU.mult))
                    dve.wait_ge(*attended.at(i, H))
                    link.then(dve.scalar_tensor_tensor(g_a[:, :], g_a[:, :], 0.5, pO[:, :], ALU.mult, ALU.mult))
                    dve.wait_ge(*stored.at(i, 0))
                    link.then(dve.tensor_tensor(x_new[:, :, :], g_a[:, :].rearrange("p (g d) -> p g d", g=G), x[:, :, :], ALU.add))
                    dve.sem_inc(finished.sem, 1)
                    link.done()

            @block.scalar
            def _(act):
                with act.Fori(0, B) as i:
                    act.wait_ge(*turned_in.at(i, 1))
                    act.copy(xqT[:, :], pA[:, :]).then_inc(xqT_kept.sem, 1)
                    for g in range(G):
                        act.wait_ge(*gu_ready.at(i, g + 1))
                        act.activation(th[:, g % 2, :], pA[:, 0:HID4], ACT.Tanh, scale=0.5).then_inc(gate_tanh.sem, 1)
                        for n in range(2 * g, 2 * g + 2):
                            act.wait_ge(*vo_ready.at(i, n + 1))
                            act.copy(vo[:, g, (n % 2) * S:(n % 2 + 1) * S], pS[:, n % 2, :]).then_inc(vo_kept.sem, 1)

                    def keep_k(n):
                        act.wait_ge(*q_ready.at(i, n + 1))
                        if n >= 2:
                            act.wait_ge(*scored.at(i, n - 1))
                        act.copy(kT[:, n % 2, :], pQ[:, :]).then_inc(k_kept.sem, 1)

                    def exps(n):
                        act.wait_ge(*top_made.at(i, n + 1))
                        if n >= 2:
                            act.wait_ge(*probT_ready.at(i, n - 1))
                        for g in range(G):
                            cut = slice(g * P, (g + 1) * P)
                            last = act.activation(prob[:, n % 2, cut], pS[:, n % 2, cut], ACT.Exp, bias=top[:, n % 2, g:g + 1],
                                                  accum_out=total[:, n % 2, g:g + 1])
                        last.then_inc(exp_made.sem, 1)

                    def keep_probT(n):
                        act.wait_ge(*probT_ready.at(i, n + 1))
                        if n >= 2:
                            act.wait_ge(*attended.at(i, n - 1))
                        act.copy(probT[:, n % 2, :], pT[:, :]).then_inc(probT_kept.sem, 1)

                    for k in range(H + 3):
                        if k < H:
                            keep_k(k)
                        if 0 <= k - 1 < H:
                            exps(k - 1)
                        if 0 <= k - 2 < H:
                            keep_probT(k - 2)
                    for c in range(HC4):
                        act.wait_ge(*hidT_ready.at(i, c + 1))
                        rows_of = min(P, HID4 - c * P)
                        act.copy(hidT[0:rows_of, c, :], (pA, pB, pQ)[c][0:rows_of, :]).then_inc(hidT_kept.sem, 1)
                    act.wait_ge(*ffn_ready.at(i, 1))
                    act.activation(g_th[:, :], pR[:, :], ACT.Tanh, scale=0.5).then_inc(ffn_tanh.sem, 1)

            @block.tensor
            def _(pe):
                pe.wait_ge(loaded, 16 * len(weights))
                for n in range(H):
                    last = pe.matmul(pA[:, n * B:(n + 1) * B], wr[:, n * F:(n + 1) * F], peT[:, :], start=True, stop=True)
                last.then_inc(pe_set, 1)
                pe.wait_ge(dve_set, 2)
                for n in range(H):
                    pe.matmul(pB[:, n * B:(n + 1) * B], wqT[:, n, :], rel[:, n, 0, :], start=True, stop=True)
                    pe.matmul(pQ[0:B * B, n:n + 1], rel[:, n, :, :].rearrange("p a j -> p (a j)"), vT[:, n:n + 1], start=True, stop=True)
                    pe.matmul(pS[:, n // 4, (n % 4) * D:(n % 4 + 1) * D], wvT[:, n, :], wout[:, n, :], start=True, stop=True)
                for c in range(HC4):
                    pe.transpose(pR[:, c * P:(c + 1) * P], wqd[:, c * P:(c + 1) * P], ident[:, :])
                    pe.transpose(pT[:, c * P:(c + 1) * P], wqd[:, HID4P + c * P:HID4P + (c + 1) * P], ident[:, :])
                    rows_of = min(P, HID4 - c * P)
                    last = pe.transpose(pO[0:rows_of, c * D:(c + 1) * D], wqd[:, 2 * HID4P + c * P:2 * HID4P + c * P + rows_of], ident[:, :])
                last.then_inc(pe_set, 1)
                pe.wait_ge(dve_set, 3)
                with pe.Fori(0, B) as i:
                    pe.wait_ge(*hh_made.at(i, 1))
                    pe.wait_ge(*finished.at(i, 0))
                    pe.wait_ge(*xq_made.at(i, 1))
                    for t in range(G):
                        last = pe.transpose(pA[:, t * P:(t + 1) * P], xq[:, t * D:(t + 1) * D], ident[:, :])
                    last.then_inc(turned_in.sem, 1)
                    for t in range(G):
                        last = pe.transpose(pB[:, t * P:(t + 1) * P], hh[:, t, :], ident[:, :])
                    last.then_inc(turned_in.sem, 1)
                    pe.wait_ge(*xqT_kept.at(i, 1))
                    pe.wait_ge(*hT_kept.at(i, 1))

                    def gate_up(g):
                        if g:
                            pe.wait_ge(*hid_made.at(i, g))
                        pe.matmul(pA[:, 0:HID4], xqT[:, g * P:(g + 1) * P], wg[:, 0:HID4], start=True, stop=True)
                        pe.matmul(pB[:, 0:HID4], xqT[:, g * P:(g + 1) * P], wu[:, 0:HID4], start=True, stop=True).then_inc(gu_ready.sem, 1)

                    def value(n):
                        if n >= 2:
                            pe.wait_ge(*vo_kept.at(i, n - 1))
                        pe.matmul(pS[:, n % 2, :], hT[:, (n // 2) * P:(n // 2 + 1) * P], wvo[:, (n % 2) * S:(n % 2 + 1) * S],
                                  start=True, stop=True).then_inc(vo_ready.sem, 1)

                    for g in range(G):
                        gate_up(g)
                        value(2 * g)
                        value(2 * g + 1)

                    def queries(n):
                        if n:
                            pe.wait_ge(*k_kept.at(i, n))
                        pe.matmul(pQ[:, :], wq[:, n * F:(n + 1) * F], hT[:, :], start=True, stop=True).then_inc(q_ready.sem, 1)
                        if n:
                            pe.wait_ge(*pos_made.at(i, n))
                        pe.matmul(pR[0:B * B, :], gpos[:, n, :], hT[:, :], start=True, stop=True)
                        pe.matmul(pR[0:B * B, :].rearrange("p (g t) -> p g t", g=G)[:, :, 0:P - BB], gnext[:, n, :],
                                  hT[:, :].rearrange("p (g t) -> p g t", g=G)[:, :, BB:P], start=False, stop=True,
                                  skip_group_check=True).then_inc(pos_ready.sem, 1)

                    def scores(n):
                        pe.wait_ge(*k_kept.at(i, n + 1))
                        pe.wait_ge(*pos_made.at(i, n + 1))
                        if n >= 2:
                            pe.wait_ge(*exp_made.at(i, n - 1))
                        else:
                            pe.wait_ge(*vo_kept.at(i, 2 * G))
                        for g in range(G):
                            cut = slice(g * P, (g + 1) * P)
                            pe.matmul(pS[:, n % 2, cut], qu[:, n % 2, cut], kT[:, n % 2, cut], start=True, stop=False)
                            last = pe.matmul(pS[:, n % 2, cut], pos[:, n % 2, cut], place[:, :], start=False, stop=True)
                        last.then_inc(scored.sem, 1)

                    def turn(n):
                        pe.wait_ge(*normed.at(i, n + 1))
                        if n:
                            pe.wait_ge(*probT_kept.at(i, n))
                        for g in range(G):
                            last = pe.transpose(pT[:, g * P:(g + 1) * P], prob[:, n % 2, g * P:(g + 1) * P], ident[:, :])
                        last.then_inc(probT_ready.sem, 1)

                    def attend(n):
                        pe.wait_ge(*probT_kept.at(i, n + 1))
                        for g in range(G):
                            if n == 0:
                                pe.matmul(pO[:, g * D:(g + 1) * D], ones[:, :], bout[:, :], start=(g == 0), stop=False, skip_group_check=True)
                            last = pe.matmul(pO[:, g * D:(g + 1) * D], probT[:, n % 2, g * P:(g + 1) * P], vo[:, g, n * D:(n + 1) * D],
                                             start=False, stop=(n == H - 1), skip_group_check=True)
                        last.then_inc(attended.sem, 1)

                    for k in range(H + 4):
                        if k < H:
                            queries(k)
                        if 0 <= k - 1 < H:
                            scores(k - 1)
                        if 0 <= k - 3 < H:
                            turn(k - 3)
                        if 0 <= k - 4 < H:
                            attend(k - 4)
                    pe.wait_ge(*hid_quantised.at(i, 1))
                    for c in range(HC4):
                        rows_of = min(P, HID4 - c * P)
                        for g in range(G):
                            last = pe.transpose((pA, pB, pQ)[c][0:rows_of, g * P:(g + 1) * P],
                                                hid[:, g * HID4 + c * P:g * HID4 + c * P + rows_of], ident[:, :])
                        last.then_inc(hidT_ready.sem, 1)
                    pe.wait_ge(*hidT_kept.at(i, HC4))
                    for g in range(G):
                        for c in range(HC4):
                            rows_of = min(P, HID4 - c * P)
                            last = pe.matmul(pR[:, g * D:(g + 1) * D], hidT[0:rows_of, c, g * P:(g + 1) * P], wd[0:rows_of, c, :],
                                             start=(c == 0), stop=(c == HC4 - 1))
                    last.then_inc(ffn_ready.sem, 1)


def layer2(nc, w, x_in, x_out):
    TB = 3
    R = P
    W = 2 * P
    SLOTS = 4
    STEP = S + P
    with ExitStack() as stack:
        m = Scope(nc, stack, "c_")
        ident, identb, maskb = m.sb("ident", [P, P]), m.sb("identb", [P, P], BF16), m.sb("maskb", [P, P], BF16)
        wqkv = m.sb("wqkv", [P, 3 * D])
        last_k, minus_last = m.sb("last_k", [P, 1]), m.sb("minus_last", [P, 1])
        place_k, place_last, place_rest = m.sb("place_k", [HD, R]), m.sb("place_last", [HD, 1]), m.sb("place_rest", [HD, R])
        place_p = [m.sb(f"place_p{j}", [HD, R], BF16) for j in range(3)]
        places = m.sb("places", [KR6, R], BF16)
        vz = m.sb("vz", [P, NT, HN, P // 2])
        place_vz = m.sb("place_vz", [R, HN, P // 2])
        no_b, spread_t = m.sb("no_b", [P, P], BF16), m.sb("spread_t", [P, NT, P])
        last_v, place_v, every_last_v = m.sb("last_v", [1, D]), m.sb("place_v", [R, HD]), m.sb("every_last_v", [R, HD])
        rel = m.sb("rel", [P, 3, NT, W])
        before = rel[:, :, :, :].rearrange("p a t c -> p (a t c)")
        wide = 2 * HID4P + HID4
        wnat, wqd = before[:, 0:wide], before[:, wide:2 * wide]
        wg, wu, wd = m.sb("wg", [P, HID4P]), m.sb("wu", [P, HID4P]), m.sb("wd", [P, HC4, D])
        q4 = QuantBuffers(m, NT * HID4)
        wc = m.sb("wc", [P, D])
        ones = m.sb("ones", [1, P])
        half, eps, spare = m.sb("half", [P, NT]), m.sb("eps", [P, NT]), m.sb("spare", [P, 1])
        x, stat, mv, rstd = m.sb("x", [P, NT, D]), m.sb("stat", [P, NT, 6]), m.sb("mv", [P, NT, 2]), m.sb("rstd", [P, NT])
        xn, xnT = m.sb("xn", [P, NT, D]), m.sb("xnT", [P, S])
        qf, kf, rest_q, rest_k = [m.sb(n, [P, S]) for n in ("qf", "kf", "rest_q", "rest_k")]
        qp, kp = [[m.sb(f"{n}{j}", [P, S], BF16) for j in range(3)] for n in ("qp", "kp")]
        qs, ks = m.sb("qs", [KR6, HN, S], BF16), m.sb("ks", [KR6, HN, S], BF16)
        low, total, inv, invT = m.sb("low", [P, ITEMS]), m.sb("total", [P, P]), m.sb("inv", [P, P]), m.sb("invT", [P, P])
        prob, probT = m.sb("prob", [P, 3, (NT - 1) * STEP + W]), m.sb("probT", [P, 3, S])
        far = m.sb("far", [P, 2])
        by_place = m.sb("by_place", [P, 2, NT, R])
        band, bandT = m.sb("band", [P, 3, NT, R]), m.sb("bandT", [P, 2, S])
        y_kept, yT = m.sb("y_kept", [P, S]), m.sb("yT", [P, S])
        x_again = m.sb("x_again", [P, NT, D])
        xq, xqT = m.sb("xq", [P, NT * D]), m.sb("xqT", [P, S])
        th, act_in = m.sb("th", [P, 2, HID4]), m.sb("act_in", [P, HID4])
        hid, hidT = m.sb("hid", [P, NT * HID4]), m.sb("hidT", [P, HC4, S])
        g_th, g_a, x_new = m.sb("g_th", [P, NT, D]), m.sb("g_a", [P, NT, D]), m.sb("x_new", [P, NT, D])
        pS, pT = m.ps("pS", [P, SB, S]), m.ps("pT", [P, TB, S])
        pY, pA = m.ps("pY", [P, S]), m.ps("pA", [P, S])
        gate_bank = lambda t: (pS[:, 0, :], pT[:, 0, :])[t % 2]
        up_bank = lambda t: (pS[:, 1, :], pT[:, 1, :])[t % 2]
        total_at = lambda n: n % NT * 32 + n // NT
        q_dram = [nc.dram_tensor(f"c_q{j}", (P, S), BF16).ap() for j in range(3)]
        k_dram = [nc.dram_tensor(f"c_k{j}", (P, S), BF16).ap() for j in range(3)]

        rel_dram = nc.dram_tensor("c_rel_dram", (SLOTS, NT * P * W), F32).ap()
        band_dram = nc.dram_tensor("c_band_dram", (SLOTS, NT * P * W), F32).ap()

        def straight(dram, h):
            return dram[h % SLOTS, :].rearrange("(t p c) -> p t c", t=NT, c=W)

        def skewed(dram, h):
            whole = straight(dram, h)
            return bass.AP(whole.tensor, whole.offset + 1, [[W + 1, P], [P * W, NT], [1, R]])

        loaded, pool_set, pe_set, dve_set, x_read, x_sent = [m.sem(n) for n in ("loaded", "pool_set", "pe_set", "dve_set", "x_read", "x_sent")]
        cleared, spread = m.sem("cleared"), m.sem("spread")
        past_sp, past_pool, past_dve = m.sem("past_sp"), m.sem("past_pool"), m.sem("past_dve")
        parts_sent, terms_read = m.sem("parts_sent"), m.sem("terms_read")
        by_slot = lambda n: [m.ev16(f"{n}{slot}", HN // SLOTS) for slot in range(SLOTS)]
        rel_sent, rel_read = by_slot("rel_sent"), by_slot("rel_read")
        band_sent, band_read = by_slot("band_sent"), by_slot("band_read")
        of_head = lambda events, i, h: events[h % SLOTS].at(i, h // SLOTS + 1)
        made_weights, made_places = m.ev("made_weights", QUANTISE_STEPS), m.ev("made_places", 6)
        stats_made, x_again_read = m.ev("stats_made", 1), m.sem("x_again_read")
        quantising = m.ev("quantising", QUANTISE_STEPS)
        centred, rstd_made, xn_made = m.ev("centred", 1), m.ev("rstd_made", 2), m.ev("xn_made", 1)
        xT_ready, xT_kept = m.ev("xT_ready", 1), m.ev("xT_kept", 1)
        proj_ready = m.ev("proj_ready", 3)
        q_split, k_split = m.ev("q_split", 1), m.ev("k_split", 1)
        v_kept = m.ev("v_kept", 1)
        xq_made, xqT_ready, xqT_kept = m.ev("xq_made", 1), m.ev("xqT_ready", 1), m.ev("xqT_kept", 1)
        gu_ready, gate_tanh, hid_made = m.ev("gu_ready", NT), m.ev("gate_tanh", NT), m.ev("hid_made", NT)
        hid_quantised, hidT_ready, hidT_kept = m.ev("hid_quantised", 1), m.ev("hidT_ready", HC4), m.ev("hidT_kept", HC4)
        ffn_ready, g_tanh = m.ev("ffn_ready", 1), m.ev("g_tanh", 1)
        places_ready, places_kept = m.ev("places_ready", HN), m.ev("places_kept", HN)
        scored, low_made, exp_made = m.ev("scored", ITEMS), m.ev("low_made", ITEMS), m.ev("exp_made", ITEMS)
        far_made = m.ev("far_made", ITEMS // 2)
        probT_ready, attended = m.ev("probT_ready", ITEMS), m.ev("attended", ITEMS)
        probT_kept_act, probT_kept_dve = m.ev("probT_kept_act", ITEMS // 2), m.ev("probT_kept_dve", ITEMS // 2)
        bandT_ready, bandT_kept, band_attended = m.ev("bandT_ready", HN), m.ev("bandT_kept", HN), m.ev("band_attended", HN)
        inv_made, invT_ready, invT_kept = m.ev("inv_made", 1), m.ev("invT_ready", 1), m.ev("invT_kept", 1)
        inv_spread, y_copied, yT_made, s_ready = m.ev("inv_spread", 1), m.ev("y_copied", 1), m.ev("yT_made", 1), m.ev("s_ready", 1)
        finished, stored = m.ev("finished", 1, credit=True), m.ev("stored", 1, credit=True)
        chain = m.ev("chain", 5 + 5 + QUANTISE_STEPS + NT + 3)

        HH = HN // 2
        half_rows = lambda h: slice(h // HH * HH * HD, (h // HH + 1) * HH * HD)

        def columns(whole, half_of, tiles):
            return bass.AP(whole.tensor, whole.offset + half_of * HH * HH * HD,
                           [list(whole.ap[0]), [HN * HH * HD, tiles], [HH * HD + HD, HH], [1, HD]])

        k_of = lambda n: (n % NT + 1) * P
        kept_by_act = lambda n: n % NT < 2
        at_prob = lambda n: n % NT * S + P

        def kept_wait(eng, i, n):
            kept, nth = (probT_kept_act, n % NT) if kept_by_act(n) else (probT_kept_dve, n % NT - 2)
            eng.wait_ge(*kept.at(i, 2 * (n // NT) + nth + 1))

        NORM_AT = 8
        LEAD, LAG = 2, 3
        turns = []
        for n in range(ITEMS + NT * LAG + 1):
            if 0 <= n - 2 < ITEMS:
                turns.append(("item", n - 2))
            if n % NT == 3 and 0 <= n // NT - LAG < HN:
                turns.append(("band", n // NT - LAG))
        bank_of = {one: r % TB for r, one in enumerate(turns)}

        def bank_free(eng, i, one):
            r = turns.index(one)
            if r >= TB:
                kind, n = turns[r - TB]
                if kind == "item":
                    kept_wait(eng, i, n)
                else:
                    eng.wait_ge(*bandT_kept.at(i, n + 1))

        weights = [(ident[:, :], w["ident"]), (identb[:, :], w["identb"]), (maskb[:, :], w["maskb"]), (spread_t[:, :, :], w["spread_t"]),
                   (wqkv[:, :], w["L2_attn_w_attn"]), (wc[:, :], w["L2_attn_w_proj"]), (ones[:, :], w["ones_row"]),
                   (last_k[:, :], w["L2_last_k"]), (place_k[:, :], w["L2_place_k"]), (place_last[:, :], w["L2_place_last"]),
                   (last_v[:, :], w["L2_last_v"]), (place_v[:, :], w["L2_place_v"]),
                   (every_last_v[:, :], w["L2_last_v"][0, 0:HD].partition_broadcast(R)),
                   (wnat[:, 0:HID4P].rearrange("p (c d) -> p c d", c=HC4), w["L2_wg"].rearrange("(c p) d -> p c d", p=P)),
                   (wnat[:, HID4P:2 * HID4P].rearrange("p (c d) -> p c d", c=HC4), w["L2_wu"].rearrange("(c p) d -> p c d", p=P)),
                   (wnat[:, 2 * HID4P:], w["L2_ffn_w_down"])]
        with nc.Block() as block:
            @block.sync
            def _(sp):
                for dst, src in weights:
                    sp.dma_start(dst, src).then_inc(loaded, 16)
                sp.wait_ge(pool_set, 7)
                for slot in range(SLOTS):
                    for dram in (rel_dram, band_dram):
                        sp.dma_start(straight(dram, slot), vz[:, 0, :, :].rearrange("p h c -> p (h c)").rearrange("p (t c) -> p t c", t=NT)).then_inc(cleared, 16)
                sp.wait_ge(*made_places.at(0, 6))
                sp.sem_inc(past_sp, 1)
                for n, (_, j) in enumerate(TERMS):
                    sp.dma_start(places[n * HD:(n + 1) * HD, :], place_p[j][:, :]).then_inc(spread, 16)
                sp.wait_ge(cleared, 16 * 2 * SLOTS)
                sp.sem_inc(past_sp, 1)
                sp.dma_start(x[:, :, :], rows(x_in, 0)).then_inc(x_read, 16)
                with sp.Fori(0, B) as i:
                    sp.wait_ge(*xn_made.at(i, 1))
                    sp.sem_inc(past_sp, 1)
                    sp.dma_start(x[:, :, :], rows(x_in, (i + 1) % B)).then_inc(x_read, 16)
                    sp.wait_ge(*finished.at(i, 0))
                    sp.sem_inc(past_sp, 1)
                    sp.dma_start(x_again[:, :, :], rows(x_in, i)).then_inc(x_again_read, 16)
                    sp.wait_ge(*q_split.at(i, 1))
                    sp.sem_inc(past_sp, 1)
                    for j in range(3):
                        sp.dma_start(q_dram[j], qp[j][:, :]).then_inc(parts_sent, 16)
                    sp.wait_ge(*k_split.at(i, 1))
                    sp.sem_inc(past_sp, 1)
                    for j in range(3):
                        sp.dma_start(k_dram[j], kp[j][:, :]).then_inc(parts_sent, 16)
                    sp.wait_ge(parts_sent, i * 96 + 96)
                    sp.sem_inc(past_sp, 1)
                    by_head = lambda z: z.rearrange("(h d) t -> d h t", d=HD)
                    for n, (a, b) in enumerate(TERMS):
                        sp.dma_start(qs[n * HD:(n + 1) * HD, :, :], by_head(q_dram[a])).then_inc(terms_read, 16)
                        sp.dma_start(ks[n * HD:(n + 1) * HD, :, :], by_head(k_dram[b])).then_inc(terms_read, 16)
                    for k in range(HN + 1):
                        if k < HN:
                            if k >= SLOTS:
                                sp.wait_ge(*of_head(rel_read, i, k - SLOTS))
                                sp.sem_inc(past_sp, 1)
                            sp.wait_ge(*places_kept.at(i, k + 1))
                            sp.sem_inc(past_sp, 1)
                            sp.dma_start(skewed(rel_dram, k), by_place[:, k % 2, :, :]).then_inc(rel_sent[k % SLOTS].sem, 16)
                        if k >= 1:
                            h = k - 1
                            sp.wait_ge(*of_head(rel_sent, i, h))
                            sp.sem_inc(past_sp, 1)
                            if h >= 3:
                                sp.wait_ge(*low_made.at(i, NT * (h - 2)))
                                sp.sem_inc(past_sp, 1)
                            sp.dma_start(rel[:, h % 3, :, :], straight(rel_dram, h)).then_inc(rel_read[h % SLOTS].sem, 16)

            @block.gpsimd
            def _(pool):
                pool.memset(half[:, :], -0.5).then_inc(pool_set, 1)
                pool.memset(eps[:, :], EPS).then_inc(pool_set, 1)
                pool.memset(q4.half_step[:, :], 0x1FFFFF).then_inc(pool_set, 1)
                pool.memset(vz[:, :, :, :], 0.0).then_inc(pool_set, 1)
                pool.memset(prob[:, :, 0:P], 0.0).then_inc(pool_set, 1)
                pool.memset(total[:, :], 1.0).then_inc(pool_set, 1)
                pool.memset(no_b[:, :], 0.0).then_inc(pool_set, 1)
                pool.sem_inc(stored.sem, 1)
                pool.wait_ge(pool_set, 7)
                pool.wait_ge(cleared, 16 * 2 * SLOTS)

                def roots(n):
                    pool.wait_ge(*centred.at(n, 1))
                    pool.tensor_tensor(rstd[:, :], mv[:, :, 1], eps[:, :], ALU.add).then_inc(rstd_made.sem, 1)
                    pool.wait_ge(*rstd_made.at(n, 1))
                    pool.tensor_tensor(rstd[:, :], rstd[:, :], half[:, :], ALU.pow).then_inc(rstd_made.sem, 1)

                roots(0)
                with pool.Fori(0, B) as i:
                    for k in range(HN + 1):
                        if k < HN:
                            if k >= SLOTS:
                                pool.wait_ge(*of_head(band_read, i, k - SLOTS))
                            pool.wait_ge(*exp_made.at(i, NT * (k + 1)))
                            pool.sem_inc(past_pool, 1)
                            whole = prob[:, k % 3, :]
                            band_of_prob = bass.AP(whole.tensor, whole.offset, [list(whole.ap[0]), [STEP, NT], [1, W]])
                            pool.dma_start(straight(band_dram, k), band_of_prob).then_inc(band_sent[k % SLOTS].sem, 16)
                        if k >= 1:
                            h = k - 1
                            pool.wait_ge(*of_head(band_sent, i, h))
                            pool.sem_inc(past_pool, 1)
                            if h >= 3:
                                pool.wait_ge(*bandT_ready.at(i, h - 2))
                                pool.sem_inc(past_pool, 1)
                            pool.dma_start(band[:, h % 3, :, :], skewed(band_dram, h)).then_inc(band_read[h % SLOTS].sem, 16)
                        if k == NORM_AT:
                            roots(i + 1)
                    pool.wait_ge(*finished.at(i, 1))
                    pool.sem_inc(past_pool, 1)
                    pool.dma_start(rows(x_out, i), x_new[:, :, :]).then_inc(x_sent, 16)
                    pool.wait_ge(x_sent, i * 16 + 16)
                    pool.sem_inc(past_pool, 1)
                    pool.sem_inc(stored.sem, 1)

            @block.vector
            def _(dve):
                dve.wait_ge(loaded, 16 * len(weights))
                dve.wait_ge(pool_set, 7)
                link = Chain(dve, made_places, 0)
                dve.tensor_scalar(minus_last[:, :], last_k[:, :], -1.0, None, ALU.mult)
                link.then(dve.tensor_scalar(place_k[:, :], place_k[:, :], place_last[:, :], -1.0, ALU.subtract, ALU.mult))
                link.then(dve.tensor_tensor(place_v[:, :], place_v[:, :], every_last_v[:, :], ALU.subtract))
                split3(dve, link, place_k[:, :], [z[:, :] for z in place_p], place_rest[:, :])
                link.done()
                for _ in quantise(dve, Chain(dve, made_weights, 0), q4, wnat[:, :], wqd[:, :], 2 * HID4P + HID4):
                    pass
                dve.sem_inc(dve_set, 1)
                dve.wait_ge(pe_set, 1)
                dve.tensor_copy(wg[:, :], pS[:, 0, 0:HID4P])
                dve.tensor_copy(wu[:, :], pS[:, 1, 0:HID4P])
                dve.tensor_copy(wd[:, 0:2, :], pS[:, 2, 0:2 * D].rearrange("p (c d) -> p c d", c=2))
                dve.tensor_copy(wd[0:HID4 - 2 * P, 2, :], pS[0:HID4 - 2 * P, 2, 2 * D:3 * D]).then_inc(dve_set, 1)
                dve.memset(place_vz[:, :, :], 0.0).then_inc(dve_set, 1)
                dve.wait_ge(dve_set, 3)
                for half_of in range(2):
                    last = dve.tensor_copy(columns(place_vz[:, :, :], half_of, 1)[:, 0, :, :], place_v[:, :].unsqueeze(1).to_broadcast([R, HH, HD]))
                last.then_inc(dve_set, 1)
                dve.sem_inc(finished.sem, 1)

                def normalise(n):
                    dve.wait_ge(x_read, n * 16 + 16)
                    for t in range(NT):
                        last = dve.bn_stats(stat[:, t, :], x[:, t, :])
                    last.then_inc(stats_made.sem, 1)
                    dve.wait_ge(*stats_made.at(n, 1))
                    dve.memset(spare[:, :], 0.0)
                    for t in range(NT):
                        last = dve.bn_aggr(mv[:, t, :], stat[:, t, :])
                    last.then_inc(centred.sem, 1)
                    yield
                    dve.wait_ge(*rstd_made.at(n, 2))
                    for t in range(NT):
                        last = dve.tensor_scalar(xn[:, t, :], x[:, t, :], mv[:, t, 0:1], rstd[:, t:t + 1], ALU.subtract, ALU.mult)
                    last.then_inc(xn_made.sem, 1)
                    dve.wait_ge(*xn_made.at(n, 1))
                    yield
                    for _ in quantise(dve, Chain(dve, quantising, n), q4, xn[:, :, :].rearrange("p t d -> p (t d)"), xq[:, :], NT * D):
                        yield
                    dve.sem_inc(xq_made.sem, 1)

                for _ in normalise(0):
                    pass
                with dve.Fori(0, B) as i:
                    link = Chain(dve, chain, i)
                    dve.wait_ge(*proj_ready.at(i, 1))
                    link.then(dve.tensor_copy(qf[:, :], pA[:, :]))
                    split3(dve, link, qf[:, :], [z[:, :] for z in qp], rest_q[:, :])
                    dve.sem_inc(q_split.sem, 1)
                    dve.wait_ge(*proj_ready.at(i, 2))
                    link.then(dve.tensor_scalar(kf[:, :], pS[:, 2, :], -float(np.float32(HD ** -0.5)), minus_last[:, :], ALU.mult, ALU.add))
                    split3(dve, link, kf[:, :], [z[:, :] for z in kp], rest_k[:, :])
                    dve.sem_inc(k_split.sem, 1)
                    for t in range(NT):
                        if t:
                            dve.wait_ge(*hid_made.at(i, t))
                        dve.wait_ge(*gate_tanh.at(i, t + 1))
                        link.then(dve.scalar_tensor_tensor(act_in[:, :], th[:, t % 2, :], 1.0, gate_bank(t)[:, 0:HID4], ALU.add, ALU.mult))
                        dve.scalar_tensor_tensor(hid[:, t * HID4:(t + 1) * HID4], act_in[:, :], 0.5, up_bank(t)[:, 0:HID4], ALU.mult, ALU.mult).then_inc(hid_made.sem, 1)
                    dve.wait_ge(*hid_made.at(i, NT))
                    steps = quantise(dve, link, q4, hid[:, :], hid[:, :], NT * HID4)

                    def lowest(n):
                        h, t, k = n // NT, n % NT, k_of(n)
                        dve.wait_ge(*scored.at(i, n + 1))
                        near = max(0, t - 1) * P
                        start = 3e38
                        if t >= 2:
                            start = far[:, t % 2:t % 2 + 1]
                            dve.tensor_reduce(start, pS[:, n % SB, 0:near], AX.X, ALU.min).then_inc(far_made.sem, 1)
                            dve.wait_ge(*far_made.at(i, 2 * h + t - 1))
                        if t == 0:
                            dve.wait_ge(*of_head(rel_read, i, h))
                        dve.sem_inc(past_dve, 1)
                        near_s = pS[:, n % SB, near:k]
                        dve.tensor_tensor_reduce(near_s, near_s, rel[:, h % 3, t, W - (k - near):W], 1.0, start, ALU.add, ALU.min,
                                                 low[:, n:n + 1]).then_inc(low_made.sem, 1)

                    def keep(n):
                        dve.wait_ge(*probT_ready.at(i, n + 1))
                        if n >= 3:
                            dve.wait_ge(*attended.at(i, n - 2))
                        dve.tensor_copy(probT[:, n % 3, 0:k_of(n)], pT[:, bank_of["item", n], 0:k_of(n)]).then_inc(probT_kept_dve.sem, 1)

                    for n in range(ITEMS + 2):
                        if n < ITEMS:
                            lowest(n)
                        if n >= 2 and not kept_by_act(n - 2):
                            keep(n - 2)
                        if n % 2 == 0 and n < 2 * QUANTISE_STEPS + 2:
                            next(steps, None)
                        if n == NORM_AT * NT:
                            dve.sem_inc(hid_quantised.sem, 1)
                            steps = normalise(i + 1)
                            next(steps)
                        if n >= NORM_AT * NT + 2 * NT:
                            next(steps, None)
                    for _ in steps:
                        pass
                    dve.wait_ge(*exp_made.at(i, ITEMS))
                    dve.reciprocal(inv[:, :], total[:, :]).then_inc(inv_made.sem, 1)
                    dve.wait_ge(*invT_ready.at(i, 1))
                    dve.tensor_copy(invT[:, :], pT[:, 0, 0:P]).then_inc(invT_kept.sem, 1)
                    dve.wait_ge(*y_copied.at(i, 1))
                    dve.wait_ge(*inv_spread.at(i, 1))
                    dve.tensor_tensor(yT[:, :], y_kept[:, :], pT[:, 1, :], ALU.mult).then_inc(yT_made.sem, 1)
                    dve.wait_ge(*g_tanh.at(i, 1))
                    out_of = lambda z: z.rearrange("p (t d) -> p t d", t=NT)
                    link.then(dve.scalar_tensor_tensor(g_a[:, :, :], g_th[:, :, :], 1.0, out_of(pT[:, 2, :]), ALU.add, ALU.mult))
                    dve.wait_ge(*s_ready.at(i, 1))
                    link.then(dve.scalar_tensor_tensor(g_a[:, :, :], g_a[:, :, :], 0.5, out_of(pA[:, :]), ALU.mult, ALU.mult))
                    dve.wait_ge(*stored.at(i, 0))
                    dve.wait_ge(x_again_read, i * 16 + 16)
                    link.then(dve.tensor_tensor(x_new[:, :, :], g_a[:, :, :], x_again[:, :, :], ALU.add))
                    dve.sem_inc(finished.sem, 1)
                    link.done()

            @block.scalar
            def _(act):
                act.wait_ge(pool_set, 7)
                act.wait_ge(dve_set, 4)
                act.wait_ge(cleared, 16 * 2 * SLOTS)
                with act.Fori(0, B) as i:
                    act.wait_ge(*xT_ready.at(i, 1))
                    act.copy(xnT[:, :], pS[:, 0, :]).then_inc(xT_kept.sem, 1)
                    act.wait_ge(*xqT_ready.at(i, 1))
                    act.copy(xqT[:, :], pS[:, 1, :]).then_inc(xqT_kept.sem, 1)
                    act.wait_ge(*proj_ready.at(i, 3))
                    for half_of in range(2):
                        last = act.copy(columns(vz[:, :, :, :], half_of, NT), pT[:, 0, :].rearrange("p (t g h d) -> p t g h d", t=NT, g=2, d=HD)[:, :, half_of, :, :])
                    last.then_inc(v_kept.sem, 1)
                    for t in range(NT):
                        act.wait_ge(*gu_ready.at(i, t + 1))
                        act.activation(th[:, t % 2, :], gate_bank(t)[:, 0:HID4], ACT.Tanh, scale=0.5).then_inc(gate_tanh.sem, 1)

                    def exps(n):
                        h = n // NT
                        act.wait_ge(*low_made.at(i, n + 1))
                        if h >= 3 and n % NT == 0:
                            act.wait_ge(*probT_ready.at(i, NT * (h - 2)))
                            act.wait_ge(*of_head(band_sent, i, h - 3))
                        act.activation(prob[:, h % 3, at_prob(n):at_prob(n) + k_of(n)], pS[:, n % SB, 0:k_of(n)], ACT.Exp, bias=low[:, n:n + 1], scale=-1.0,
                                       accum_out=total[:, total_at(n):total_at(n) + 1]).then_inc(exp_made.sem, 1)

                    def keep(n):
                        act.wait_ge(*probT_ready.at(i, n + 1))
                        if n >= 3:
                            act.wait_ge(*attended.at(i, n - 2))
                        act.copy(probT[:, n % 3, 0:k_of(n)], pT[:, bank_of["item", n], 0:k_of(n)]).then_inc(probT_kept_act.sem, 1)

                    def keep_places(h):
                        act.wait_ge(*places_ready.at(i, h + 1))
                        if h >= 2:
                            act.wait_ge(*of_head(rel_sent, i, h - 2))
                        act.copy(by_place[:, h % 2, :, :], pA[:, :].rearrange("p (t r) -> p t r", t=NT)).then_inc(places_kept.sem, 1)

                    def keep_band(h):
                        act.wait_ge(*bandT_ready.at(i, h + 1))
                        if h >= 2:
                            act.wait_ge(*band_attended.at(i, h - 1))
                        act.copy(bandT[:, h % 2, :], pT[:, bank_of["band", h], :]).then_inc(bandT_kept.sem, 1)

                    for h in range(LEAD):
                        keep_places(h)
                    for n in range(ITEMS + NT * LAG + 1):
                        if n % NT == 0 and n // NT + LEAD < HN:
                            keep_places(n // NT + LEAD)
                        if n < ITEMS:
                            exps(n)
                        if 0 <= n - 2 < ITEMS and kept_by_act(n - 2):
                            keep(n - 2)
                        if n % NT == 3 and 0 <= n // NT - LAG < HN:
                            keep_band(n // NT - LAG)
                    act.wait_ge(*band_attended.at(i, HN))
                    act.copy(y_kept[:, :], pY[:, :]).then_inc(y_copied.sem, 1)
                    for c in range(HC4):
                        act.wait_ge(*hidT_ready.at(i, c + 1))
                        rows_of = min(P, HID4 - c * P)
                        act.copy(hidT[0:rows_of, c, :], pS[0:rows_of, c, :]).then_inc(hidT_kept.sem, 1)
                    act.wait_ge(*ffn_ready.at(i, 1))
                    act.activation(g_th[:, :, :], pT[:, 2, :].rearrange("p (t d) -> p t d", t=NT), ACT.Tanh, scale=0.5).then_inc(g_tanh.sem, 1)

            @block.tensor
            def _(pe):
                pe.wait_ge(loaded, 16 * len(weights))
                pe.wait_ge(dve_set, 1)
                for c in range(HC4):
                    pe.transpose(pS[:, 0, c * P:(c + 1) * P], wqd[:, c * P:(c + 1) * P], ident[:, :])
                    pe.transpose(pS[:, 1, c * P:(c + 1) * P], wqd[:, HID4P + c * P:HID4P + (c + 1) * P], ident[:, :])
                    rows_of = min(P, HID4 - c * P)
                    last = pe.transpose(pS[0:rows_of, 2, c * D:(c + 1) * D], wqd[:, 2 * HID4P + c * P:2 * HID4P + c * P + rows_of], ident[:, :])
                last.then_inc(pe_set, 1)
                pe.wait_ge(dve_set, 4)
                pe.wait_ge(pool_set, 7)
                pe.wait_ge(spread, 16 * len(TERMS))
                with pe.Fori(0, B) as i:
                    pe.wait_ge(*xn_made.at(i, 1))
                    for t in range(NT):
                        last = pe.transpose(pS[:, 0, t * P:(t + 1) * P], xn[:, t, :], ident[:, :])
                    last.then_inc(xT_ready.sem, 1)
                    pe.wait_ge(*xq_made.at(i, 1))
                    for t in range(NT):
                        last = pe.transpose(pS[:, 1, t * P:(t + 1) * P], xq[:, t * D:(t + 1) * D], ident[:, :])
                    last.then_inc(xqT_ready.sem, 1)
                    pe.wait_ge(*xT_kept.at(i, 1))
                    pe.wait_ge(*finished.at(i, 0))
                    pe.matmul(pA[:, :], wqkv[:, 0:D], xnT[:, :], start=True, stop=True).then_inc(proj_ready.sem, 1)
                    pe.matmul(pS[:, 2, :], wqkv[:, D:2 * D], xnT[:, :], start=True, stop=True).then_inc(proj_ready.sem, 1)
                    for t in range(NT):
                        out = pT[:, 0, t * P:(t + 1) * P]
                        pe.matmul(out, xnT[:, t * P:(t + 1) * P], wqkv[:, 2 * D:3 * D], start=True, stop=False)
                        last = pe.matmul(out, ones[:, :], last_v[:, :], start=False, stop=True)
                    last.then_inc(proj_ready.sem, 1)
                    pe.wait_ge(*xqT_kept.at(i, 1))
                    for t in range(NT):
                        if t == 1:
                            pe.wait_ge(*v_kept.at(i, 1))
                        if t >= 2:
                            pe.wait_ge(*hid_made.at(i, t - 1))
                        pe.matmul(gate_bank(t)[:, 0:HID4], xqT[:, t * P:(t + 1) * P], wg[:, 0:HID4], start=True, stop=True)
                        pe.matmul(up_bank(t)[:, 0:HID4], xqT[:, t * P:(t + 1) * P], wu[:, 0:HID4], start=True, stop=True).then_inc(gu_ready.sem, 1)
                    for t in range(NT):
                        pe.matmul(pY[:, t * P:(t + 1) * P], no_b[:, :], identb[:, :], start=True, stop=True)

                    def by_places(h):
                        if h:
                            pe.wait_ge(*places_kept.at(i, h))
                        for t in range(NT):
                            last = pe.matmul(pA[:, t * P:(t + 1) * P], qs[:, h, t * P:(t + 1) * P], places[:, :], start=True, stop=True)
                        last.then_inc(places_ready.sem, 1)

                    def scores(n):
                        h, t, k = n // NT, n % NT, k_of(n)
                        if n >= SB:
                            pe.wait_ge(*exp_made.at(i, n - SB + 1))
                        elif n == 0:
                            pe.wait_ge(*hid_made.at(i, NT))
                        pe.matmul(pS[:, n % SB, 0:k], qs[:, h, t * P:k], ks[:, h, 0:k], start=True, stop=True)
                        pe.matmul(pS[:, n % SB, t * P:k], identb[:, :], maskb[:, :], start=False, stop=True,
                                  skip_group_check=True).then_inc(scored.sem, 1)

                    def turn(n):
                        pe.wait_ge(*exp_made.at(i, n + 1))
                        bank_free(pe, i, ("item", n))
                        for u in range(n % NT + 1):
                            last = pe.transpose(pT[:, bank_of["item", n], u * P:(u + 1) * P],
                                                prob[:, n // NT % 3, at_prob(n) + u * P:at_prob(n) + (u + 1) * P], ident[:, :])
                        last.then_inc(probT_ready.sem, 1)

                    def attend(n):
                        h, t = n // NT, n % NT
                        kept_wait(pe, i, n)
                        for u in range(t + 1):
                            last = pe.matmul(pY[half_rows(h), t * P:(t + 1) * P], vz[:, u, h, :], probT[:, n % 3, u * P:(u + 1) * P],
                                             start=False, stop=True, skip_group_check=True)
                        last.then_inc(attended.sem, 1)

                    def turn_band(h):
                        pe.wait_ge(*of_head(band_read, i, h))
                        bank_free(pe, i, ("band", h))
                        for t in range(NT):
                            last = pe.transpose(pT[:, bank_of["band", h], t * P:(t + 1) * P], band[:, h % 3, t, :], ident[:, :])
                        last.then_inc(bandT_ready.sem, 1)

                    def attend_band(h):
                        pe.wait_ge(*bandT_kept.at(i, h + 1))
                        pe.matmul(pY[half_rows(h), :], place_vz[:, h, :], bandT[:, h % 2, :], start=False, stop=True,
                                  skip_group_check=True).then_inc(band_attended.sem, 1)

                    pe.wait_ge(terms_read, i * 16 * 2 * len(TERMS) + 16 * 2 * len(TERMS))
                    pe.wait_ge(*v_kept.at(i, 1))
                    for h in range(LEAD):
                        by_places(h)
                    for n in range(ITEMS + NT * LAG + 3):
                        if n % NT == 0 and n // NT + LEAD < HN:
                            by_places(n // NT + LEAD)
                        if n < ITEMS:
                            scores(n)
                        if 0 <= n - 2 < ITEMS:
                            turn(n - 2)
                        if n % NT == 3 and 0 <= n // NT - LAG < HN:
                            turn_band(n // NT - LAG)
                        if 0 <= n - 4 < ITEMS:
                            attend(n - 4)
                        if (n - 2) % NT == 3 and 0 <= (n - 2) // NT - LAG < HN:
                            attend_band((n - 2) // NT - LAG)
                    pe.wait_ge(*hid_quantised.at(i, 1))
                    for c in range(HC4):
                        rows_of = min(P, HID4 - c * P)
                        for t in range(NT):
                            last = pe.transpose(pS[0:rows_of, c, t * P:(t + 1) * P],
                                                hid[:, t * HID4 + c * P:t * HID4 + c * P + rows_of], ident[:, :])
                        last.then_inc(hidT_ready.sem, 1)
                    pe.wait_ge(*inv_made.at(i, 1))
                    pe.transpose(pT[:, 0, 0:P], inv[:, :], ident[:, :]).then_inc(invT_ready.sem, 1)
                    pe.wait_ge(*hidT_kept.at(i, HC4))
                    for t in range(NT):
                        for c in range(HC4):
                            rows_of = min(P, HID4 - c * P)
                            last = pe.matmul(pT[:, 2, t * D:(t + 1) * D], hidT[0:rows_of, c, t * P:(t + 1) * P], wd[0:rows_of, c, :],
                                             start=(c == 0), stop=(c == HC4 - 1))
                    last.then_inc(ffn_ready.sem, 1)
                    pe.wait_ge(*invT_kept.at(i, 1))
                    for t in range(NT):
                        last = pe.matmul(pT[:, 1, t * P:(t + 1) * P], spread_t[:, t, :], invT[:, :], start=True, stop=True)
                    last.then_inc(inv_spread.sem, 1)
                    pe.wait_ge(*yT_made.at(i, 1))
                    for t in range(NT):
                        last = pe.matmul(pA[:, t * P:(t + 1) * P], yT[:, t * P:(t + 1) * P], wc[:, :], start=True, stop=True)
                    last.then_inc(s_ready.sem, 1)


def layer3(nc, w, x_in, x_out):
    L = 64
    E, FF = 8, 512
    FC = FF // P
    with ExitStack() as stack:
        m = Scope(nc, stack, "d_")
        ident, identb, maskb = m.sb("ident", [P, P]), m.sb("identb", [P, P], BF16), m.sb("maskb", [P, P], BF16)
        HH = HN // 2
        vz = m.sb("vz", [P, NT * 2 * HH * P])
        wdn = vz[0:L, 0:3 * HN * D].rearrange("l (n h d) -> l n h d", n=3, h=HN)
        gather = m.sb("gather", [P, P])
        v_at = lambda u, h: vz[:, (u * HN + h) * P:(u * HN + h + 1) * P]
        ups = m.sb("ups", [L, 5, HD])
        weff = m.sb("weff", [P, 5, P])
        wc = m.sb("wc", [P, D])
        cosq, sinq, cosk, sink = [m.sb(n, [P, S]) for n in ("cosq", "sinq", "cosk", "sink")]
        rw, rb, lg_sum = m.sb("rw", [P, E]), m.sb("rb", [P, E]), m.sb("lg_sum", [P, NT, E])
        earlier = m.sb("earlier", [P, E, E])
        wup, wdown = m.sb("wup", [P, E, FF]), m.sb("wdown", [P, E * FC, D])
        half, eps, spare = m.sb("half", [P, NT]), m.sb("eps", [P, NT]), m.sb("spare", [P, 1])
        x, stat, mv, rstd = m.sb("x", [P, NT, D]), m.sb("stat", [P, NT, 6]), m.sb("mv", [P, NT, 2]), m.sb("rstd", [P, NT])
        xn, xnT = m.sb("xn", [P, NT, D]), m.sb("xnT", [P, S])
        rot_a, rot_b, qf, kf, rest_q, rest_k = [m.sb(n, [P, S]) for n in ("rot_a", "rot_b", "qf", "kf", "rest_q", "rest_k")]
        qp, kp = [[m.sb(f"{n}{j}", [P, S], BF16) for j in range(3)] for n in ("qp", "kp")]
        qs, ks = m.sb("qs", [KR9, HN, S], BF16), m.sb("ks", [KR9, HN, S], BF16)
        sums = m.sb("sums", [P, S])
        low, rest_low = m.sb("low", [P, P]), m.sb("rest_low", [ITEMS, P])
        lowp = [m.sb(f"lowp{j}", [ITEMS, P], BF16) for j in range(3)]
        probT = m.sb("probT", [P, 3, 3 * S])
        x_again = m.sb("x_again", [P, NT, D])
        y_kept, yT = m.sb("y_kept", [P, S]), m.sb("yT", [P, S])
        lg, pr, comb = [m.sb(n, [P, NT, E]) for n in ("lg", "pr", "comb")]
        ltop, lsum, linv = m.sb("ltop", [P, NT]), m.sb("lsum", [P, NT]), m.sb("linv", [P, NT])
        more, same, rank = m.sb("more", [P, NT, E, E]), m.sb("same", [P, NT, E, E]), m.sb("rank", [P, NT, E])
        hid = m.sb("hid", [P, 2, FC, S])
        acc, g_th, g_a, x_new = m.sb("acc", [P, NT, D]), m.sb("g_th", [P, NT, D]), m.sb("g_a", [P, NT, D]), m.sb("x_new", [P, NT, D])
        pX, pY = m.ps("pX", [P, 6, S]), m.ps("pY", [P, 2, S])
        X = [pX[:, n, :] for n in range(6)]
        up_bank = lambda n: X[n % 3]
        down_bank = lambda e: X[3 + e % 2]
        score_bank = lambda n: (X[5], pY[:, 0, :], pY[:, 1, :])[n % 3]
        q_dram = [nc.dram_tensor(f"d_q{j}", (P, S), BF16).ap() for j in range(3)]
        k_dram = [nc.dram_tensor(f"d_k{j}", (P, S), BF16).ap() for j in range(3)]

        loaded, pool_set, pe_set, dve_set, x_read, x_sent = [m.sem(n) for n in ("loaded", "pool_set", "pe_set", "dve_set", "x_read", "x_sent")]
        parts_sent, terms_read = m.sem("parts_sent"), m.sem("terms_read")
        stats_made = m.ev("stats_made", 1)
        centred, rstd_made, xn_made = m.ev("centred", 1), m.ev("rstd_made", 2), m.ev("xn_made", 1)
        xT_ready, xT_kept = m.ev("xT_ready", 1), m.ev("xT_kept", 1)
        proj_ready = m.ev("proj_ready", 5)
        turned = m.ev("turned", 2)
        q_split, k_split = m.ev("q_split", 1), m.ev("k_split", 1)
        v_kept = m.ev("v_kept", 1)
        scored, low_made = m.ev("scored", ITEMS), m.ev("low_made", ITEMS)
        lowT_ready, low_split, low_sent = m.ev("lowT_ready", 1), m.ev("low_split", 1), m.sem("low_sent")
        scored_by_key, exp_made, attended = m.ev("scored_by_key", PIECES * HN), m.ev("exp_made", PIECES * HN), m.ev("attended", HN)
        x_again_read = m.sem("x_again_read")
        past_pool = m.sem("past_pool")
        halves_kept = m.ev("halves_kept", 2)
        sums_made, sums_spread, yT_made, s_ready = m.ev("sums_made", 1), m.ev("sums_spread", 1), m.ev("yT_made", 1), m.ev("s_ready", 1)
        lg_ready, lg_top, lg_exp, comb_made = m.ev("lg_ready", 1), m.ev("lg_top", 1), m.ev("lg_exp", 1), m.ev("comb_made", 1)
        up_ready, hid_made = m.ev("up_ready", E * FC), m.ev("hid_made", E * FC)
        down_ready, added = m.ev("down_ready", E), m.ev("added", E)
        summed, g_tanh = m.ev("summed", 1), m.ev("g_tanh", 1)
        finished, stored = m.ev("finished", 1, credit=True), m.ev("stored", 1, credit=True)
        chain = m.ev("chain", 25)

        def v_columns(half_of, width, column, step):
            whole = vz[:, :]
            return bass.AP(whole.tensor, whole.offset + half_of * HH * P + column,
                           [list(whole.ap[0]), [2 * HH * P, NT], [P + step, HH], [1, width]])

        k_of = lambda n: (n % NT + 1) * P

        moe = [("up", e, c) for e in range(2) for c in range(FC)] + [("down", 0, t) for t in range(NT)]
        for e in range(2, E):
            moe += [("up", e, c) for c in range(FC)] + [("down", e - 1, t) for t in range(NT)]
        first, last_of = 6 * FC, len(moe) - 2 * FC
        plan = [("route", 0, 0)] + moe[:first]
        for n in range(ITEMS):
            plan.append(("score", n, 0))
            plan += moe[first + (last_of - first) * n // ITEMS:first + (last_of - first) * (n + 1) // ITEMS]
        plan += [("turn_low", 0, 0)] + moe[last_of:]

        weights = [(ident[:, :], w["ident"]), (identb[:, :], w["identb"]), (maskb[:, :], w["maskb"]),
                   (wdn[:, 0, :, :], w["L3_WqT"]), (wdn[:, 1, :, :], w["L3_WkT"]), (wdn[:, 2, :, :], w["L3_WvT"]),
                   (ups[:, 0, 0:4], w["L3_attn_Wq_up_c"]), (ups[:, 0, 4:8], w["L3_attn_Wq_up_e"]),
                   (ups[:, 2, 0:4], w["L3_attn_Wk_up_c"]), (ups[:, 2, 4:8], w["L3_attn_Wk_up_e"]),
                   (ups[:, 4, :], w["L3_attn_Wv_up"]), (wc[:, :], w["L3_attn_Wc"]),
                   (cosq[:, :], w["L3_cosq"]), (sinq[:, :], w["L3_sinq"]), (cosk[:, :], w["L3_cosk"]), (sink[:, :], w["L3_sink"]),
                   (rw[:, :], w["L3_ffn_router_w"]), (rb[:, :], w["L3_rb"][0, :].partition_broadcast(P)), (earlier[:, :, :], w["L3_earlier"]), (gather[:, :], w["gather"]),
                   (ks[KR6:KR9, :, :], w["L3_minus"].rearrange("a (h t) -> a h t", t=S)),
                   (wup[:, :, :], w["L3_upT"]), (wdown[:, :, :], w["L3_downT"])]
        with nc.Block() as block:
            @block.sync
            def _(sp):
                for dst, src in weights:
                    sp.dma_start(dst, src).then_inc(loaded, 16)
                sp.dma_start(x[:, :, :], rows(x_in, 0)).then_inc(x_read, 16)
                with sp.Fori(0, B) as i:
                    sp.wait_ge(*xn_made.at(i, 1))
                    sp.nop()
                    sp.dma_start(x[:, :, :], rows(x_in, (i + 1) % B)).then_inc(x_read, 16)
                    sp.wait_ge(*q_split.at(i, 1))
                    for j in range(3):
                        sp.dma_start(q_dram[j], qp[j][:, :]).then_inc(parts_sent, 16)
                    sp.wait_ge(*k_split.at(i, 1))
                    for j in range(3):
                        sp.dma_start(k_dram[j], kp[j][:, :]).then_inc(parts_sent, 16)
                    sp.wait_ge(parts_sent, i * 96 + 96)
                    by_head = lambda z: z.rearrange("(h d) t -> d h t", d=HD)
                    for n, (a, b) in enumerate(TERMS):
                        sp.dma_start(qs[n * HD:(n + 1) * HD, :, :], by_head(q_dram[a])).then_inc(terms_read, 16)
                        sp.dma_start(ks[n * HD:(n + 1) * HD, :, :], by_head(k_dram[b])).then_inc(terms_read, 16)
                    sp.wait_ge(*low_split.at(i, 1))
                    for j in range(3):
                        sp.dma_start(qs[KR6 + j:KR6 + j + 1, :, :], lowp[j][:, :]).then_inc(low_sent, 16)
                    sp.wait_ge(*finished.at(i, 0))
                    sp.dma_start(x_again[:, :, :], rows(x_in, i)).then_inc(x_again_read, 16)

            @block.gpsimd
            def _(pool):
                pool.memset(half[:, :], -0.5).then_inc(pool_set, 1)
                pool.memset(eps[:, :], EPS).then_inc(pool_set, 1)
                pool.memset(low[:, ITEMS:], 0.0).then_inc(pool_set, 1)
                pool.memset(sums[:, :], 0.0).then_inc(pool_set, 1)
                pool.sem_inc(stored.sem, 1)
                pool.wait_ge(pool_set, 4)

                def roots(n):
                    pool.wait_ge(*centred.at(n, 1))
                    pool.tensor_tensor(rstd[:, :], mv[:, :, 1], eps[:, :], ALU.add).then_inc(rstd_made.sem, 1)
                    pool.wait_ge(*rstd_made.at(n, 1))
                    pool.tensor_tensor(rstd[:, :], rstd[:, :], half[:, :], ALU.pow).then_inc(rstd_made.sem, 1)

                roots(0)
                with pool.Fori(0, B) as i:
                    roots(i + 1)
                    pool.wait_ge(*finished.at(i, 1))
                    pool.sem_inc(past_pool, 1)
                    pool.dma_start(rows(x_out, i), x_new[:, :, :]).then_inc(x_sent, 16)
                    pool.wait_ge(x_sent, i * 16 + 16)
                    pool.sem_inc(stored.sem, 1)

            @block.vector
            def _(dve):
                dve.wait_ge(loaded, 16 * len(weights))
                dve.wait_ge(pool_set, 4)
                for one in (0, 2):
                    dve.memset(ups[:, one + 1, 0:4], 0.0)
                    pair = lambda z: z.rearrange("p (a b) -> p a b", b=2)
                    dve.tensor_scalar(pair(ups[:, one + 1, 4:8])[:, :, 0], pair(ups[:, one, 4:8])[:, :, 1], -1.0, None, ALU.mult)
                    last = dve.tensor_copy(pair(ups[:, one + 1, 4:8])[:, :, 1], pair(ups[:, one, 4:8])[:, :, 0])
                last.then_inc(dve_set, 1)
                dve.wait_ge(pe_set, 1)
                for n in range(5):
                    last = dve.tensor_copy(weff[:, n, :], X[n][:, 0:P])
                last.then_inc(dve_set, 1)
                dve.memset(vz[:, :], 0.0).then_inc(dve_set, 1)
                dve.wait_ge(dve_set, 3)
                for half_of in range(2):
                    ones_of = v_columns(half_of, 1, HH * HD if half_of == 0 else 0, 1)
                    last = dve.memset(ones_of, 1.0)
                last.then_inc(dve_set, 1)
                dve.sem_inc(finished.sem, 1)

                def normalise(n):
                    dve.wait_ge(x_read, n * 16 + 16)
                    for t in range(NT):
                        last = dve.bn_stats(stat[:, t, :], x[:, t, :])
                    last.then_inc(stats_made.sem, 1)
                    dve.wait_ge(*stats_made.at(n, 1))
                    dve.memset(spare[:, :], 0.0)
                    for t in range(NT):
                        last = dve.bn_aggr(mv[:, t, :], stat[:, t, :])
                    last.then_inc(centred.sem, 1)
                    dve.wait_ge(*rstd_made.at(n, 2))
                    for t in range(NT):
                        last = dve.tensor_scalar(xn[:, t, :], x[:, t, :], mv[:, t, 0:1], rstd[:, t:t + 1], ALU.subtract, ALU.mult)
                    last.then_inc(xn_made.sem, 1)

                normalise(0)
                with dve.Fori(0, B) as i:
                    link = Chain(dve, chain, i)
                    dve.wait_ge(*lg_ready.at(i, 1))
                    link.then(dve.tensor_tensor(lg_sum[:, :, :], pY[:, 0, 0:NT * E].rearrange("p (t e) -> p t e", t=NT), rb[:, :].unsqueeze(1).to_broadcast([P, NT, E]), ALU.add))
                    dve.tensor_reduce(ltop[:, :], lg_sum[:, :, :], AX.X, ALU.max, negate=True).then_inc(lg_top.sem, 1)
                    for one, (cos, sin, full) in enumerate(((cosq, sinq, qf), (cosk, sink, kf))):
                        dve.wait_ge(*proj_ready.at(i, 2 * one + 2))
                        straight, crossed = ((X[0], X[1]), (X[3], X[2]))[one]
                        dve.tensor_tensor(rot_a[:, :], straight, cos[:, :], ALU.mult)
                        dve.tensor_tensor(rot_b[:, :], crossed, sin[:, :], ALU.mult).then_inc(turned.sem, 1)
                        dve.wait_ge(*turned.at(i, one + 1))
                        link.then(dve.tensor_tensor(full[:, :], rot_a[:, :], rot_b[:, :], ALU.add))
                    for one, full in enumerate((qf, kf)):
                        split3(dve, link, full[:, :], [z[:, :] for z in (qp, kp)[one]], (rest_q, rest_k)[one][:, :])
                        dve.sem_inc((q_split, k_split)[one].sem, 1)

                    def route():
                        dve.wait_ge(*lg_exp.at(i, 1))
                        link.then(dve.reciprocal(linv[:, :], lsum[:, :]))
                        link.then(dve.tensor_tensor(pr[:, :, :], lg[:, :, :], linv[:, :].unsqueeze(2).to_broadcast([P, NT, E]), ALU.mult))
                        for t in range(NT):
                            other = pr[:, t, :].unsqueeze(1).to_broadcast([P, E, E])
                            own = pr[:, t, :].unsqueeze(2).to_broadcast([P, E, E])
                            dve.tensor_tensor(more[:, t, :, :], other, own, ALU.is_gt)
                            last = dve.tensor_tensor(same[:, t, :, :], other, own, ALU.is_equal)
                        link.then(last)
                        for t in range(NT):
                            last = dve.tensor_tensor(same[:, t, :, :], same[:, t, :, :], earlier[:, :, :], ALU.mult)
                        link.then(last)
                        link.then(dve.tensor_tensor(more[:, :, :, :], more[:, :, :, :], same[:, :, :, :], ALU.add))
                        link.then(dve.tensor_reduce(rank[:, :, :], more[:, :, :, :], AX.X, ALU.add))
                        link.then(dve.scalar_tensor_tensor(comb[:, :, :], rank[:, :, :], 1.5, pr[:, :, :], ALU.is_lt, ALU.mult))

                    def add_expert(e):
                        dve.wait_ge(*down_ready.at(i, e + 1))
                        if e:
                            dve.wait_ge(*added.at(i, e))
                        for t in range(NT):
                            part, share = down_bank(e)[:, t * D:(t + 1) * D], comb[:, t, e:e + 1]
                            if e == 0:
                                last = dve.tensor_scalar(acc[:, t, :], part, share, None, ALU.mult)
                            else:
                                last = dve.scalar_tensor_tensor(acc[:, t, :], part, share, acc[:, t, :], ALU.mult, ALU.add)
                        last.then_inc(added.sem, 1)

                    for kind, n, part in plan:
                        if kind == "route":
                            route()
                        if kind == "score":
                            dve.wait_ge(*scored.at(i, n + 1))
                            dve.tensor_reduce(low[:, n:n + 1], score_bank(n)[:, 0:k_of(n)], AX.X, ALU.min).then_inc(low_made.sem, 1)
                        if kind == "turn_low":
                            dve.wait_ge(*lowT_ready.at(i, 1))
                            split3(dve, link, X[5][0:ITEMS, 0:P], [z[:, :] for z in lowp], rest_low[:, :])
                            dve.sem_inc(low_split.sem, 1)
                        if kind == "down" and part == NT - 1:
                            add_expert(n)
                    normalise(i + 1)
                    dve.wait_ge(*attended.at(i, HH))
                    dve.reciprocal(sums[HH * HD:HH * HD + HH, :], pY[HH * HD:HH * HD + HH, 0, :])
                    dve.wait_ge(*attended.at(i, HN))
                    dve.reciprocal(sums[0:HH, :], pY[0:HH, 1, :]).then_inc(sums_made.sem, 1)
                    dve.wait_ge(*sums_spread.at(i, 1))
                    dve.wait_ge(*halves_kept.at(i, 2))
                    for half_of in range(2):
                        mine = slice(half_of * HH * HD, (half_of + 1) * HH * HD)
                        last = dve.tensor_tensor(yT[mine, :], y_kept[mine, :], X[0][mine, :], ALU.mult)
                    last.then_inc(yT_made.sem, 1)
                    add_expert(E - 1)
                    dve.wait_ge(*g_tanh.at(i, 1))
                    link.then(dve.scalar_tensor_tensor(g_a[:, :, :], g_th[:, :, :], 1.0, acc[:, :, :], ALU.add, ALU.mult))
                    dve.wait_ge(*s_ready.at(i, 1))
                    link.then(dve.scalar_tensor_tensor(g_a[:, :, :], g_a[:, :, :], 0.5, pY[:, 1, :].rearrange("p (t d) -> p t d", t=NT), ALU.mult, ALU.mult))
                    dve.wait_ge(*stored.at(i, 0))
                    dve.wait_ge(x_again_read, i * 16 + 16)
                    link.then(dve.tensor_tensor(x_new[:, :, :], g_a[:, :, :], x_again[:, :, :], ALU.add))
                    dve.sem_inc(finished.sem, 1)
                    link.done()

            @block.scalar
            def _(act):
                act.wait_ge(dve_set, 4)
                with act.Fori(0, B) as i:
                    act.wait_ge(*xT_ready.at(i, 1))
                    act.copy(xnT[:, :], X[2]).then_inc(xT_kept.sem, 1)
                    act.wait_ge(*lg_top.at(i, 1))
                    for t in range(NT):
                        last = act.activation(lg[:, t, :], lg_sum[:, t, :], ACT.Exp, bias=ltop[:, t:t + 1], accum_out=lsum[:, t:t + 1])
                    last.then_inc(lg_exp.sem, 1)
                    act.wait_ge(*proj_ready.at(i, 5))
                    for half_of in range(2):
                        last = act.copy(v_columns(half_of, HD, half_of * HH * HD, HD), X[5].rearrange("p (t g h d) -> p t g h d", t=NT, g=2, d=HD)[:, :, half_of, :, :])
                    last.then_inc(v_kept.sem, 1)
                    for n in range(E * FC):
                        e, c = n // FC, n % FC
                        act.wait_ge(*up_ready.at(i, n + 1))
                        if e >= 2 and c == 0:
                            act.wait_ge(*down_ready.at(i, e - 1))
                        act.activation(hid[:, e % 2, c, :], up_bank(n), ACT.Gelu).then_inc(hid_made.sem, 1)

                    def keep_half(half_of):
                        mine = slice(half_of * HH * HD, (half_of + 1) * HH * HD)
                        act.wait_ge(*attended.at(i, HH * (half_of + 1)))
                        act.copy(y_kept[mine, :], pY[mine, half_of, :]).then_inc(halves_kept.sem, 1)

                    for h in range(HN):
                        if h == HH + 2:
                            keep_half(0)
                        if h >= 3:
                            act.wait_ge(*attended.at(i, h - 2))
                        for piece in range(PIECES):
                            act.wait_ge(*scored_by_key.at(i, PIECES * h + piece + 1))
                            width = S if piece < 2 else 2 * P
                            act.activation(probT[:, h % 3, piece * S:piece * S + width], X[h % 2 * PIECES + piece][:, 0:width], ACT.Exp, scale=-1.0).then_inc(exp_made.sem, 1)
                    keep_half(1)
                    act.wait_ge(*added.at(i, E))
                    act.activation(g_th[:, :, :], acc[:, :, :], ACT.Tanh, scale=0.5).then_inc(g_tanh.sem, 1)

            @block.tensor
            def _(pe):
                pe.wait_ge(loaded, 16 * len(weights))
                pe.wait_ge(dve_set, 1)
                for n in range(5):
                    for h in range(HN):
                        last = pe.matmul(X[n][:, h * HD:(h + 1) * HD], wdn[:, n // 2, h, :], ups[:, n, :], start=True, stop=True)
                last.then_inc(pe_set, 1)
                pe.wait_ge(dve_set, 4)
                with pe.Fori(0, B) as i:
                    pe.wait_ge(*xn_made.at(i, 1))
                    for t in range(NT):
                        last = pe.transpose(X[2][:, t * P:(t + 1) * P], xn[:, t, :], ident[:, :])
                    last.then_inc(xT_ready.sem, 1)
                    pe.wait_ge(*xT_kept.at(i, 1))
                    for t in range(NT):
                        last = pe.matmul(pY[:, 0, t * E:(t + 1) * E], xnT[:, t * P:(t + 1) * P], rw[:, :], start=True, stop=True)
                    last.then_inc(lg_ready.sem, 1)
                    for n, bank in enumerate((0, 1, 3, 2)):
                        pe.matmul(X[bank], weff[:, n, :], xnT[:, :], start=True, stop=True).then_inc(proj_ready.sem, 1)
                    for t in range(NT):
                        last = pe.matmul(X[5][:, t * P:(t + 1) * P], xnT[:, t * P:(t + 1) * P], weff[:, 4, :], start=True, stop=True)
                    last.then_inc(proj_ready.sem, 1)

                    def scores(n):
                        h, t, k = n // NT, n % NT, k_of(n)
                        if n >= 3:
                            pe.wait_ge(*low_made.at(i, n - 2))
                        elif n == 0:
                            pe.wait_ge(terms_read, i * 16 * 2 * len(TERMS) + 16 * 2 * len(TERMS))
                            pe.wait_ge(*v_kept.at(i, 1))
                        elif n == 1:
                            pe.wait_ge(*lg_top.at(i, 1))
                        else:
                            pe.wait_ge(*finished.at(i, 0))
                        pe.matmul(score_bank(n)[:, 0:k], qs[0:KR6, h, t * P:k], ks[0:KR6, h, 0:k], start=True, stop=True)
                        pe.matmul(score_bank(n)[:, t * P:k], identb[:, :], maskb[:, :], start=False, stop=True,
                                  skip_group_check=True).then_inc(scored.sem, 1)

                    def up(e, c):
                        n = e * FC + c
                        if n >= 3:
                            pe.wait_ge(*hid_made.at(i, n - 2))
                        elif n == 0:
                            pe.wait_ge(*turned.at(i, 1))
                        elif n == 2:
                            pe.wait_ge(*turned.at(i, 2))
                        pe.matmul(up_bank(n), wup[:, e, c * P:(c + 1) * P], xnT[:, :], start=True, stop=True).then_inc(up_ready.sem, 1)

                    def down(e, t):
                        if t == 0:
                            pe.wait_ge(*hid_made.at(i, (e + 1) * FC))
                            if e >= 2:
                                pe.wait_ge(*added.at(i, e - 1))
                        for c in range(FC):
                            last = pe.matmul(down_bank(e)[:, t * D:(t + 1) * D], hid[:, e % 2, c, t * P:(t + 1) * P], wdown[:, e * FC + c, :],
                                             start=(c == 0), stop=(c == FC - 1))
                        if t == NT - 1:
                            last.then_inc(down_ready.sem, 1)

                    def turn_low():
                        pe.wait_ge(*low_made.at(i, ITEMS))
                        pe.transpose(X[5][:, 0:P], low[:, :], ident[:, :]).then_inc(lowT_ready.sem, 1)

                    for kind, n, part in plan:
                        if kind == "score":
                            scores(n)
                        if kind == "up":
                            up(n, part)
                        if kind == "down":
                            down(n, part)
                        if kind == "turn_low":
                            turn_low()

                    place_of = (0, S, 2 * S, S + 3 * P)

                    def scores_by_key(h):
                        for piece, tiles in enumerate(((0,), (1, 3), (2,))):
                            if h >= 2:
                                pe.wait_ge(*exp_made.at(i, PIECES * (h - 2) + piece + 1))
                            for u in tiles:
                                at = place_of[u] - piece * S
                                bank = X[h % 2 * PIECES + piece]
                                pe.matmul(bank[:, at:at + S - u * P], ks[:, h, u * P:(u + 1) * P], qs[:, h, u * P:S], start=True, stop=True)
                                last = pe.matmul(bank[:, at:at + P], maskb[:, :], identb[:, :], start=False, stop=True, skip_group_check=True)
                            last.then_inc(scored_by_key.sem, 1)

                    def attend(h):
                        pe.wait_ge(*exp_made.at(i, PIECES * (h + 1)))
                        for u in range(NT):
                            at = place_of[u]
                            last = pe.matmul(pY[:, h // HH, u * P:S], v_at(u, h), probT[:, h % 3, at:at + S - u * P],
                                             start=(h % HH == 0 and u == 0), stop=(h % HH == HH - 1 and u == NT - 1),
                                             skip_group_check=True)
                        last.then_inc(attended.sem, 1)

                    pe.wait_ge(*hid_made.at(i, E * FC))
                    pe.wait_ge(*added.at(i, E - 1))
                    pe.wait_ge(low_sent, i * 48 + 48)
                    for h in range(HN + 1):
                        if h < HN:
                            scores_by_key(h)
                        if h:
                            attend(h - 1)
                    for t in range(NT):
                        down(E - 1, t)
                    pe.wait_ge(*sums_made.at(i, 1))
                    pe.matmul(X[0], gather[:, :], sums[:, :], start=True, stop=True).then_inc(sums_spread.sem, 1)
                    pe.wait_ge(*yT_made.at(i, 1))
                    for t in range(NT):
                        last = pe.matmul(pY[:, 1, t * P:(t + 1) * P], yT[:, t * P:(t + 1) * P], wc[:, :], start=True, stop=True)
                    last.then_inc(s_ready.sem, 1)


def host_arrays(inputs):
    a = {k: np.ascontiguousarray(v) for k, v in inputs.items()}
    out = {}
    keep = lambda *names: out.update({n: a[n] for n in names})
    t = lambda z: np.ascontiguousarray(z.T)
    out["x0"] = a["L0_attn_x"].reshape(B * S, D)
    keep("L0_attn_w_q", "L0_attn_w_k", "L0_attn_w_v2")
    out["L0_wv1T"] = t(a["L0_attn_w_v1"])
    out["L0_wgT"], out["L0_wuT"], out["L0_wdT"] = t(a["L0_ffn_w_gate"]), t(a["L0_ffn_w_up"]), t(a["L0_ffn_w_down"])
    out["ident"] = np.eye(P, dtype=np.float32)
    out["identb"] = np.eye(P).astype(mybir.dt.np(BF16))
    out["maskb"] = (BIG * (np.arange(P)[None, :] > np.arange(P)[:, None])).astype(mybir.dt.np(BF16))
    t = lambda z: np.ascontiguousarray(z.T)
    pad = lambda z: np.concatenate([z, np.zeros((HID4P - HID4, D), z.dtype)])
    for n in ("L1_attn_Wq", "L1_attn_Wr", "L1_attn_Wout", "L1_ffn_w_down"):
        out[n] = a[n]
    out["L1_WqT"], out["L1_WvT"] = t(a["L1_attn_Wq"]), t(a["L1_attn_Wv"])
    out["L1_uT"], out["L1_vT"] = t(a["L1_attn_u_bias"]), t(a["L1_attn_v_bias"])
    out["L1_gammaT"], out["L1_betaT"] = a["L1_attn_gamma"].reshape(D, 1), a["L1_attn_beta"].reshape(D, 1)
    out["L1_bout"] = a["L1_attn_bout"].reshape(1, D)
    out["L1_wg"], out["L1_wu"] = pad(a["L1_ffn_w_gate"]), pad(a["L1_ffn_w_up"])
    out["ones_row"] = np.ones((1, P), np.float32)
    place = np.arange(B, dtype=np.float32)[:, None]
    div = np.exp(np.arange(0, D, 2, dtype=np.float32) * np.float32(-np.log(10000.0) / D)).astype(np.float32)
    ang = (place * div).astype(np.float32)
    pe = np.stack([np.sin(ang), np.cos(ang)], axis=-1).reshape(B, D).astype(np.float32)
    out["L1_peT"] = t(pe[::-1])
    tok = np.arange(P)
    r = np.arange(B * B)
    c = np.float32(1 / np.sqrt(D))
    own_i = (r[:, None] // B == tok[None, :] // 16).astype(np.float32) * c
    out["L1_own_i"] = np.ascontiguousarray(np.tile(own_i, (1, NT)))
    own_b = (np.arange(16)[:, None] == tok[None, :] % 16).astype(np.float32)
    out["L1_own_b"] = np.ascontiguousarray(np.tile(own_b, (1, NT)))
    i, jj, j = r[:, None] // B, r[:, None] % B, tok[None, :] // 16
    put = (((jj == 7 + j - i) & (j <= i)) | ((jj == j - i - 2) & (j >= i + 2))).astype(np.float32)
    out["L1_is_own"] = np.ascontiguousarray(np.broadcast_to((r % B >= 7 - r // B), (P, B * B))).astype(np.float32)
    out["L1_is_next"] = np.ascontiguousarray(np.broadcast_to((r % B <= 5 - r // B), (P, B * B))).astype(np.float32)
    late = np.ones((B, B, P), np.float32)
    late[0] = np.arange(B)[:, None] <= tok[None, :] % 16
    out["L1_late"] = late.reshape(B, B * P)
    out["L1_place"] = np.concatenate([put, np.float32(-BIG) * (1 - own_b)]).astype(np.float32)
    t = lambda z: np.ascontiguousarray(z.T)
    for n in ("q", "k", "v"):
        out[f"L3_W{n}T"] = np.ascontiguousarray(a[f"L3_attn_W{n}_down"].reshape(D, 16, 64).transpose(2, 1, 0))
    for n in ("Wq_up_c", "Wq_up_e", "Wk_up_c", "Wk_up_e", "Wv_up", "Wc"):
        out[f"L3_attn_{n}"] = a[f"L3_attn_{n}"]
    inv_freq = (1.0 / np.float32(10000.0) ** (np.arange(0, 4, 2, dtype=np.float32) / np.float32(4))).astype(np.float32)
    ang = (np.arange(S, dtype=np.float32)[:, None] * inv_freq[None, :]).astype(np.float32)
    ang = np.concatenate([ang, ang], axis=-1)
    cos, sin = np.ones((S, HD), np.float32), np.zeros((S, HD), np.float32)
    cos[:, 4:], sin[:, 4:] = np.cos(ang), np.sin(ang)
    cos, sin = np.tile(cos.T, (HN, 1)), np.tile(sin.T, (HN, 1))
    neg = np.float32(-1 / np.sqrt(HD))
    out["L3_cosq"], out["L3_sinq"] = np.ascontiguousarray(cos), np.ascontiguousarray(sin)
    out["L3_cosk"], out["L3_sink"] = np.ascontiguousarray(cos * neg), np.ascontiguousarray(sin * neg)
    out["L3_ffn_router_w"] = a["L3_ffn_router_w"]
    out["L3_rb"] = a["L3_ffn_router_b"].reshape(1, 8)
    out["L3_earlier"] = np.ascontiguousarray(np.broadcast_to(np.tril(np.ones((8, 8), np.float32), -1), (P, 8, 8)))
    out["L3_upT"] = np.ascontiguousarray(a["L3_ffn_expert_up"].transpose(2, 0, 1))
    out["L3_downT"] = np.ascontiguousarray(a["L3_ffn_expert_down"].transpose(2, 0, 1).reshape(4, P, 8, D).transpose(1, 2, 0, 3).reshape(P, 32, D))
    out["L3_minus"] = np.full((3, HN * S), -1, mybir.dt.np(BF16))
    r, c = np.arange(P)[:, None], np.arange(P)[None, :]
    out["gather"] = (((r < 8) & (c >= 64) & ((c - 64) // HD == r)) | ((r >= 64) & (c < 64) & (c // HD == r - 64))).astype(np.float32)
    pad = lambda z: np.concatenate([z, np.zeros((HID4P - HID4, D), z.dtype)])
    for n in ("L2_attn_w_attn", "L2_attn_w_proj", "L2_ffn_w_down"):
        out[n] = a[n]
    ek, ev = a["L2_attn_embk"], a["L2_attn_embv"]
    out["L2_last_k"] = np.tile(ek[-1], HN).reshape(D, 1)
    out["L2_place_k"] = np.ascontiguousarray(ek[::-1].T)
    out["L2_place_last"] = ek[-1].reshape(HD, 1)
    out["L2_last_v"] = np.tile(ev[-1], HN).reshape(1, D)
    out["L2_place_v"] = np.ascontiguousarray(ev[::-1])
    out["L2_wg"], out["L2_wu"] = pad(a["L2_ffn_w_gate"]), pad(a["L2_ffn_w_up"])
    row, tile, c = np.arange(P)[:, None, None], np.arange(NT)[None, :, None], np.arange(P)[None, None, :]
    out["spread_t"] = (row == tile * 32 + c // HD).astype(np.float32)
    return out


def build(nc, w, result):
    x1, x2, x3 = [nc.dram_tensor(f"x_after_{n}", (B * S, D), F32).ap() for n in range(3)]
    layer0(nc, w, w["x0"], x1)
    layer1(nc, w, x1, x2)
    layer2(nc, w, x2, x3)
    layer3(nc, w, x3, result)


def kernel(**inputs):
    import concourse.bacc as bacc
    from concourse.bass_utils import run_bass_kernel_spmd

    nc = bacc.Bacc("TRN2", target_bir_lowering=False, num_devices=1)
    arrays = host_arrays(inputs)
    w = {name: nc.dram_tensor(name, a.shape, mybir.dt.from_np(a.dtype), kind="ExternalInput").ap() for name, a in arrays.items()}
    result = nc.dram_tensor("result", (B * S, D), F32, kind="ExternalOutput").ap()
    build(nc, w, result)
    r = run_bass_kernel_spmd(nc, [arrays], core_ids=[0])
    return r.results[0]["result"].reshape(B, S, D)
```

```python
from contextlib import ExitStack, contextmanager

import numpy as np

import concourse.bass as bass
from concourse import mybir

F32 = mybir.dt.float32
BF16 = mybir.dt.bfloat16
I32 = mybir.dt.int32
ALU = mybir.AluOpType
ACT = mybir.ActivationFunctionType
AX = mybir.AxisListType

P = 128
D = 128
B, S = 8, 512
NT = S // P
EPS = 1e-5
BIG = 1e30


class Event:

    def __init__(self, scope, name, per, credit=False, step=1):
        self.sem = scope.sem(name)
        self.per, self.step = per * step, step
        self.base = self.per if credit else 0

    def at(self, i, n):
        return self.sem, i * self.per + self.base + n * self.step


class Chain:

    def __init__(self, eng, event, i):
        self.eng, self.event, self.i, self.n = eng, event, i, 0

    def then(self, instruction):
        self.n += 1
        instruction.then_inc(self.event.sem, 1)
        self.eng.wait_ge(*self.event.at(self.i, self.n))

    def done(self):
        assert self.n == self.event.per, f"chain of {self.n} steps"


class Scope:

    def __init__(self, nc, stack, prefix):
        self.nc, self.stack, self.prefix = nc, stack, prefix
        self.semaphores = []
        stack.callback(self.clear)

    def clear(self):
        self.nc.clear_and_free_semaphores(self.semaphores)
        self.nc.all_engine_barrier()

    def sb(self, name, shape, dt=F32):
        return self.stack.enter_context(self.nc.sbuf_tensor(self.prefix + name, shape, dt))

    def ps(self, name, shape, dt=F32):
        return self.stack.enter_context(self.nc.psum_tensor(self.prefix + name, shape, dt))

    def sem(self, name):
        self.semaphores.append(self.nc.alloc_semaphore(name=self.prefix + name))
        return self.semaphores[-1]

    def ev(self, name, per, credit=False):
        return Event(self, name, per, credit)

    def ev16(self, name, per):
        return Event(self, name, per, step=16)


def rows(x, i):
    return x.rearrange("(b t p) d -> b p t d", b=B, p=P)[i, :, :, :]


def quantise(dve, link, q, src, dst, n):
    nb = n // 16
    blocks = lambda z: z.rearrange("p (b k) -> p b k", k=16)
    each = lambda z: z[:, 0:nb].unsqueeze(2).to_broadcast([P, nb, 16])
    norm, mag, grid, low = q.norm[:, 0:n], q.mag[:, 0:n], q.grid[:, 0:n], q.low[:, 0:n]
    link.then(dve.tensor_reduce(q.peak[:, 0:nb], blocks(src), AX.X, ALU.max, apply_absolute_value=True))
    yield
    link.then(dve.tensor_scalar(q.scale[:, 0:nb], q.peak[:, 0:nb], float(np.float32(1 / 6)), 1e-12, ALU.mult, ALU.max))
    yield
    link.then(dve.reciprocal(q.rscale[:, 0:nb], q.scale[:, 0:nb]))
    yield
    link.then(dve.tensor_tensor(blocks(norm), blocks(src), each(q.rscale), ALU.mult))
    yield
    link.then(dve.tensor_scalar(mag.bitcast(I32), norm.bitcast(I32), 0x7FFFFFFF, None, ALU.bitwise_and))
    yield
    link.then(dve.tensor_scalar(grid, mag, 1.0, None, ALU.max))
    yield
    dve.tensor_scalar(low, mag, 0.25, 0.5, ALU.is_gt, ALU.mult)
    link.then(dve.tensor_tensor(grid.bitcast(I32), grid.bitcast(I32), q.half_step[:, 0:n], ALU.add))
    yield
    link.then(dve.tensor_scalar(grid.bitcast(I32), grid.bitcast(I32), -0x400000, None, ALU.bitwise_and))
    yield
    link.then(dve.scalar_tensor_tensor(grid, mag, 0.75, grid, ALU.is_gt, ALU.mult))
    yield
    link.then(dve.tensor_tensor(grid, grid, low, ALU.max))
    yield
    link.then(dve.scalar_tensor_tensor(grid.bitcast(I32), norm.bitcast(I32), -0x80000000, grid.bitcast(I32), ALU.bitwise_and, ALU.bitwise_or))
    yield
    link.then(dve.tensor_tensor(blocks(dst), blocks(grid), each(q.scale), ALU.mult))
    yield


QUANTISE_STEPS = 12


class QuantBuffers:
    def __init__(self, m, n):
        self.norm, self.mag, self.grid, self.low = [m.sb("q_" + s, [P, n]) for s in ("norm", "mag", "grid", "low")]
        self.half_step = m.sb("q_half_step", [P, n], I32)
        self.peak, self.scale, self.rscale = [m.sb("q_" + s, [P, n // 16]) for s in ("peak", "scale", "rscale")]


HN, HD = 16, 8
ITEMS = HN * NT
TERMS = ((0, 0), (0, 1), (0, 2), (1, 0), (1, 1), (2, 0))
KR6 = len(TERMS) * HD
KR9 = KR6 + 3
PIECES = 3
SB, TB = 3, 2


def split3_steps(eng, link, src, parts, rest):
    link.then(eng.tensor_copy(parts[0], src))
    yield
    link.then(eng.tensor_tensor(rest, src, parts[0], ALU.subtract))
    yield
    link.then(eng.tensor_copy(parts[1], rest))
    yield
    link.then(eng.tensor_tensor(parts[2], rest, parts[1], ALU.subtract))


def split3(eng, link, src, parts, rest):
    for _ in split3_steps(eng, link, src, parts, rest):
        pass


def send_parts(eng, dram, parts, sem):
    whole = dram[0, :, :]
    for j in range(3):
        dst = bass.AP(whole.tensor, whole.offset + j * HD * HN * S, [[S, HN], [HN * S, HD], [1, S]])
        eng.dma_start(dst, parts[:, j, :]).then_inc(sem, 16)


def load_terms(eng, dst, dram, groups, sem):
    whole = dram[0, :, :]
    for n, part, step, count in groups:
        src = bass.AP(whole.tensor, whole.offset + part * HD * HN * S, [[step * HD * HN * S, count], [HN * S, HD], [1, HN * S]])
        eng.dma_start(dst[n * HD:(n + count) * HD, :, :].rearrange("r h t -> r (h t)"), src).then_inc(sem, 16)


Q_GROUPS = ((0, 0, 0, 3), (3, 1, 0, 2), (5, 2, 0, 1))
K_GROUPS = ((0, 0, 1, 3), (3, 0, 1, 2), (5, 0, 0, 1))


def layer0(nc, w, x_in, x_out):
    KD, HID = 64, 384
    HC = HID // P
    with ExitStack() as stack:
        m = Scope(nc, stack, "a_")
        ident, maskb, identb = m.sb("ident", [P, P]), m.sb("maskb", [P, P], BF16), m.sb("identb", [P, P], BF16)
        wq, wk = m.sb("wq", [P, KD]), m.sb("wk", [P, KD])
        wv1T, wv2, wv = m.sb("wv1T", [KD, P]), m.sb("wv2", [KD, P]), m.sb("wv", [P, P])
        wint = [m.sb(f"wint{n}", [P, HID], I32) for n in range(3)]
        wg, wu, wd = [m.sb(n, [P, HID]) for n in ("wg", "wu", "wd")]
        half, eps = m.sb("half", [P, NT]), m.sb("eps", [P, NT])
        x, spare = m.sb("x", [P, NT, D]), m.sb("spare", [P, 1])
        stat, mv, rstd = m.sb("stat", [P, NT, 6]), m.sb("mv", [P, NT, 2]), m.sb("rstd", [P, NT])
        xn, xnT = m.sb("xn", [P, NT, D]), m.sb("xnT", [P, S])
        qT, kT, v = m.sb("qT", [KD, S]), m.sb("kT", [KD, S]), m.sb("v", [P, NT, D])
        th, act_in, hT = m.sb("th", [P, 2, S]), m.sb("act_in", [P, S]), m.sb("hT", [P, HC, S])
        low, total, inv = m.sb("low", [P, NT]), m.sb("total", [P, NT]), m.sb("inv", [P, NT])
        prob, probT = m.sb("prob", [P, 2, S]), m.sb("probT", [P, 2, S])
        s_out, g_a, x_new = m.sb("s_out", [P, NT, D]), m.sb("g_a", [P, NT, D]), m.sb("x_new", [P, NT, D])
        g_th, x_again = m.sb("g_th", [P, NT, D]), m.sb("x_again", [P, NT, D])
        pY, pF, pG, pU = [m.ps(n, [P, S]) for n in ("pY", "pF", "pG", "pU")]
        pS, pP = m.ps("pS", [P, 2, S]), m.ps("pP", [P, 2, S])
        pX, pQ, pK, pV = pS[:, 0, :], pS[:, 1, :], pP[:, 0, :], pP[:, 1, :]

        loaded, pool_set, dve_set = m.sem("loaded"), m.sem("pool_set"), m.sem("dve_set")
        wv_made, x_read, x_sent = m.sem("wv_made"), m.sem("x_read"), m.sem("x_sent")
        x_again_read, stats_made = m.sem("x_again_read"), m.ev("stats_made", 1)
        past_sp, past_pool = m.sem("past_sp"), m.sem("past_pool")
        centred = m.ev("centred", 1)
        rstd_made = m.ev("rstd_made", 2)
        xn_made = m.ev("xn_made", 1)
        xT_ready = m.ev("xT_ready", 1)
        xT_kept = m.ev("xT_kept", 1)
        qkv_ready = m.ev("qkv_ready", 3)
        q_kept = m.ev("q_kept", 1)
        kv_kept = m.ev("kv_kept", 2)
        gu_ready = m.ev("gu_ready", HC)
        gate_tanh = m.ev("gate_tanh", HC)
        h_made = m.ev("h_made", HC)
        scored = m.ev("scored", NT)
        low_made = m.ev("low_made", NT)
        exp_made = m.ev("exp_made", NT)
        probT_ready = m.ev("probT_ready", NT)
        probT_kept = m.ev("probT_kept", NT)
        attended = m.ev("attended", NT)
        ffn_ready = m.ev("ffn_ready", 1)
        ffn_tanh = m.ev("ffn_tanh", 1)
        finished = m.ev("finished", 1, credit=True)
        chain = m.ev("chain", 8)
        stored = m.ev("stored", 1, credit=True)
        weights = [(ident[:, :], w["ident"]), (identb[:, :], w["identb"]), (maskb[:, :], w["maskb"]),
                   (wq[:, :], w["L0_attn_w_q"]), (wk[:, :], w["L0_attn_w_k"]),
                   (wv1T[:, :], w["L0_wv1T"]), (wv2[:, :], w["L0_attn_w_v2"]),
                   (wint[0][:, :], w["L0_wgT"]), (wint[1][:, :], w["L0_wuT"]),
                   (wint[2][:, :].rearrange("p (c d) -> p c d", d=D), w["L0_wdT"].rearrange("(c p) d -> p c d", p=P))]
        with nc.Block() as block:
            @block.sync
            def _(sp):
                for dst, src in weights:
                    sp.dma_start(dst, src).then_inc(loaded, 16)
                sp.wait_ge(loaded, 16 * len(weights))
                sp.dma_start(x[:, :, :], rows(x_in, 0)).then_inc(x_read, 16)
                with sp.Fori(0, B) as i:
                    sp.wait_ge(*xn_made.at(i, 1))
                    sp.sem_inc(past_sp, 1)
                    sp.dma_start(x[:, :, :], rows(x_in, (i + 1) % B)).then_inc(x_read, 16)
                    sp.wait_ge(*finished.at(i, 0))
                    sp.sem_inc(past_sp, 1)
                    sp.dma_start(x_again[:, :, :], rows(x_in, i)).then_inc(x_again_read, 16)

            @block.gpsimd
            def _(pool):
                pool.memset(half[:, :], -0.5).then_inc(pool_set, 1)
                pool.memset(eps[:, :], EPS).then_inc(pool_set, 1)
                pool.sem_inc(stored.sem, 1)
                pool.wait_ge(pool_set, 2)

                def roots(n):
                    pool.wait_ge(*centred.at(n, 1))
                    pool.tensor_tensor(rstd[:, :], mv[:, :, 1], eps[:, :], ALU.add).then_inc(rstd_made.sem, 1)
                    pool.wait_ge(*rstd_made.at(n, 1))
                    pool.tensor_tensor(rstd[:, :], rstd[:, :], half[:, :], ALU.pow).then_inc(rstd_made.sem, 1)

                roots(0)
                with pool.Fori(0, B) as i:
                    roots(i + 1)
                    pool.wait_ge(*finished.at(i, 1))
                    pool.sem_inc(past_pool, 1)
                    pool.dma_start(rows(x_out, i), x_new[:, :, :]).then_inc(x_sent, 16)
                    pool.wait_ge(x_sent, i * 16 + 16)
                    pool.sem_inc(stored.sem, 1)

            @block.vector
            def _(dve):
                dve.wait_ge(loaded, 16 * len(weights))
                for src, dst in zip(wint, (wg, wu, wd)):
                    dve.tensor_scalar(dst[:, :], src[:, :], float(np.float32(1.0 / 127.0)), None, ALU.mult)
                dve.wait_ge(wv_made, 1)
                dve.tensor_copy(wv[:, :], pV[:, 0:D]).then_inc(dve_set, 1)
                dve.sem_inc(finished.sem, 1)

                def centre(n):
                    dve.wait_ge(x_read, n * 16 + 16)
                    for t in range(NT):
                        last = dve.bn_stats(stat[:, t, :], x[:, t, :])
                    last.then_inc(stats_made.sem, 1)
                    dve.wait_ge(*stats_made.at(n, 1))
                    dve.memset(spare[:, :], 0.0)
                    for t in range(NT):
                        last = dve.bn_aggr(mv[:, t, :], stat[:, t, :])
                    last.then_inc(centred.sem, 1)

                def normalise(n):
                    dve.wait_ge(*rstd_made.at(n, 2))
                    for t in range(NT):
                        last = dve.tensor_scalar(xn[:, t, :], x[:, t, :], mv[:, t, 0:1], rstd[:, t:t + 1], ALU.subtract, ALU.mult)
                    last.then_inc(xn_made.sem, 1)

                centre(0)
                normalise(0)
                with dve.Fori(0, B) as i:
                    link = Chain(dve, chain, i)
                    dve.wait_ge(*qkv_ready.at(i, 2))
                    dve.tensor_scalar(kT[:, :], pK[0:KD, :], -float(KD) ** -0.5, None, ALU.mult).then_inc(kv_kept.sem, 1)
                    dve.wait_ge(*qkv_ready.at(i, 3))
                    dve.tensor_copy(v[:, :, :], pV.rearrange("p (t d) -> p t d", t=NT)).then_inc(kv_kept.sem, 1)

                    def hidden(c):
                        dve.wait_ge(*gate_tanh.at(i, c + 1))
                        link.then(dve.scalar_tensor_tensor(act_in[:, :], th[:, c % 2, :], 1.0, pG[:, :], ALU.add, ALU.mult))
                        dve.scalar_tensor_tensor(hT[:, c, :], act_in[:, :], 0.5, pU[:, :], ALU.mult, ALU.mult).then_inc(h_made.sem, 1)

                    def lowest(t):
                        dve.wait_ge(*scored.at(i, t + 1))
                        dve.tensor_reduce(low[:, t:t + 1], pS[:, t % 2, 0:(t + 1) * P], AX.X, ALU.min).then_inc(low_made.sem, 1)

                    def keep_probT(t):
                        dve.wait_ge(*probT_ready.at(i, t + 1))
                        dve.tensor_copy(probT[:, t % 2, 0:(t + 1) * P], pP[:, t % 2, 0:(t + 1) * P]).then_inc(probT_kept.sem, 1)

                    hidden(0)
                    lowest(0)
                    lowest(1)
                    hidden(1)
                    keep_probT(0)
                    lowest(2)
                    hidden(2)
                    keep_probT(1)
                    lowest(3)
                    centre(i + 1)
                    keep_probT(2)
                    keep_probT(3)
                    normalise(i + 1)
                    dve.wait_ge(*exp_made.at(i, NT))
                    link.then(dve.reciprocal(inv[:, :], total[:, :]))
                    dve.wait_ge(*attended.at(i, NT))
                    link.then(dve.tensor_tensor(s_out[:, :, :], pY[:, :].rearrange("p (t d) -> p t d", t=NT),
                                                inv[:, :].unsqueeze(2).to_broadcast([P, NT, D]), ALU.mult))
                    dve.wait_ge(*ffn_tanh.at(i, 1))
                    link.then(dve.scalar_tensor_tensor(g_a[:, :, :], g_th[:, :, :], 1.0,
                                                       pF[:, :].rearrange("p (t d) -> p t d", t=NT), ALU.add, ALU.mult))
                    link.then(dve.scalar_tensor_tensor(g_a[:, :, :], g_a[:, :, :], 0.5, s_out[:, :, :], ALU.mult, ALU.mult))
                    dve.wait_ge(*stored.at(i, 0))
                    dve.wait_ge(x_again_read, i * 16 + 16)
                    link.then(dve.tensor_tensor(x_new[:, :, :], g_a[:, :, :], x_again[:, :, :], ALU.add))
                    dve.sem_inc(finished.sem, 1)
                    link.done()

            @block.scalar
            def _(act):
                with act.Fori(0, B) as i:
                    act.wait_ge(*xT_ready.at(i, 1))
                    act.copy(xnT[:, :], pX).then_inc(xT_kept.sem, 1)
                    act.wait_ge(*qkv_ready.at(i, 1))
                    act.copy(qT[:, :], pQ[0:KD, :]).then_inc(q_kept.sem, 1)

                    def gate(c):
                        act.wait_ge(*gu_ready.at(i, c + 1))
                        act.activation(th[:, c % 2, :], pG[:, :], ACT.Tanh, scale=0.5).then_inc(gate_tanh.sem, 1)

                    def exps(t):
                        act.wait_ge(*low_made.at(i, t + 1))
                        if t >= 2:
                            act.wait_ge(*probT_ready.at(i, t - 1))
                        n = (t + 1) * P
                        act.activation(prob[:, t % 2, 0:n], pS[:, t % 2, 0:n], ACT.Exp, bias=low[:, t:t + 1], scale=-1.0,
                                       accum_out=total[:, t:t + 1]).then_inc(exp_made.sem, 1)

                    gate(0)
                    exps(0)
                    exps(1)
                    gate(1)
                    exps(2)
                    gate(2)
                    exps(3)
                    act.wait_ge(*ffn_ready.at(i, 1))
                    act.activation(g_th[:, :, :], pF[:, :].rearrange("p (t d) -> p t d", t=NT), ACT.Tanh, scale=0.5).then_inc(ffn_tanh.sem, 1)

            @block.tensor
            def _(pe):
                pe.wait_ge(loaded, 16 * len(weights))
                pe.matmul(pV[:, 0:D], wv1T[:, :], wv2[:, :], start=True, stop=True).then_inc(wv_made, 1)
                pe.wait_ge(dve_set, 1)
                with pe.Fori(0, B) as i:
                    pe.wait_ge(*xn_made.at(i, 1))
                    for t in range(NT):
                        last = pe.transpose(pX[:, t * P:(t + 1) * P], xn[:, t, :], ident[:, :])
                    last.then_inc(xT_ready.sem, 1)
                    pe.wait_ge(*xT_kept.at(i, 1))
                    pe.matmul(pQ[0:KD, :], wq[:, :], xnT[:, :], start=True, stop=True).then_inc(qkv_ready.sem, 1)
                    pe.matmul(pK[0:KD, :], wk[:, :], xnT[:, :], start=True, stop=True).then_inc(qkv_ready.sem, 1)
                    for t in range(NT):
                        last = pe.matmul(pV[:, t * P:(t + 1) * P], xnT[:, t * P:(t + 1) * P], wv[:, :], start=True, stop=True)
                    last.then_inc(qkv_ready.sem, 1)

                    def gate_up(c):
                        if c == 0:
                            pe.wait_ge(*xT_kept.at(i, 1))
                        else:
                            pe.wait_ge(*h_made.at(i, c))
                        pe.matmul(pG[:, :], wg[:, c * P:(c + 1) * P], xnT[:, :], start=True, stop=True)
                        pe.matmul(pU[:, :], wu[:, c * P:(c + 1) * P], xnT[:, :], start=True, stop=True).then_inc(gu_ready.sem, 1)

                    def scores(t):
                        if t == 0:
                            pe.wait_ge(*q_kept.at(i, 1))
                            pe.wait_ge(*kv_kept.at(i, 2))
                        if t >= 2:
                            pe.wait_ge(*exp_made.at(i, t - 1))
                        n = (t + 1) * P
                        pe.matmul(pS[:, t % 2, 0:n], qT[:, t * P:n], kT[:, 0:n], start=True, stop=True)
                        pe.matmul(pS[:, t % 2, t * P:n], identb[:, :], maskb[:, :], start=False, stop=True,
                                  skip_group_check=True).then_inc(scored.sem, 1)

                    def turn(t):
                        pe.wait_ge(*exp_made.at(i, t + 1))
                        if t >= 2:
                            pe.wait_ge(*probT_kept.at(i, t - 1))
                        for u in range(t + 1):
                            last = pe.transpose(pP[:, t % 2, u * P:(u + 1) * P], prob[:, t % 2, u * P:(u + 1) * P], ident[:, :])
                        last.then_inc(probT_ready.sem, 1)

                    def attend(t):
                        pe.wait_ge(*probT_kept.at(i, t + 1))
                        if t == 0:
                            pe.wait_ge(*finished.at(i, 0))
                        for u in range(t + 1):
                            last = pe.matmul(pY[:, t * P:(t + 1) * P], probT[:, t % 2, u * P:(u + 1) * P], v[:, u, :],
                                             start=(u == 0), stop=(u == t))
                        last.then_inc(attended.sem, 1)

                    gate_up(0)
                    scores(0)
                    scores(1)
                    turn(0)
                    gate_up(1)
                    scores(2)
                    attend(0)
                    turn(1)
                    gate_up(2)
                    scores(3)
                    attend(1)
                    turn(2)
                    attend(2)
                    turn(3)
                    attend(3)
                    pe.wait_ge(*h_made.at(i, HC))
                    for t in range(NT):
                        for c in range(HC):
                            last = pe.matmul(pF[:, t * P:(t + 1) * P], hT[:, c, t * P:(t + 1) * P], wd[:, c * D:(c + 1) * D],
                                             start=(c == 0), stop=(c == HC - 1))
                    last.then_inc(ffn_ready.sem, 1)


HID4 = 352
HID4P = 384
HC4 = HID4P // P


def layer1(nc, w, x_in, x_out):
    H, F = 8, 128
    BB = 16
    G = NT
    C = float(np.float32(1 / np.sqrt(D)))
    KR = B * B + BB
    with ExitStack() as stack:
        m = Scope(nc, stack, "b_")
        ident, ones, bout = m.sb("ident", [P, P]), m.sb("ones", [1, P]), m.sb("bout", [1, D])
        wq, wqT = m.sb("wq", [P, H * F]), m.sb("wqT", [P, H, D])
        wr = m.sb("wr", [P, H * F])
        wvT, wout, wvo = m.sb("wvT", [P, H, D]), m.sb("wout", [P, H, D]), m.sb("wvo", [P, H * D])
        peT = m.sb("peT", [P, B])
        uT, vT, gammaT, betaT = m.sb("uT", [P, H]), m.sb("vT", [P, H]), m.sb("gammaT", [P, 1]), m.sb("betaT", [P, 1])
        rel, gpos, gbias = m.sb("rel", [P, H, B, B]), m.sb("gpos", [P, H, B * B]), m.sb("gbias", [B * B, H])
        gnext, is_own, is_next = m.sb("gnext", [P, H, B * B]), m.sb("is_own", [P, B * B]), m.sb("is_next", [P, B * B])
        late = m.sb("late", [B * B, H, P])
        own_i, place = m.sb("own_i", [B * B, S]), m.sb("place", [KR, P])
        wnat, wqd = m.sb("wnat", [P, 2 * HID4P + HID4]), m.sb("wqd", [P, 2 * HID4P + HID4])
        wg, wu, wd = m.sb("wg", [P, HID4P]), m.sb("wu", [P, HID4P]), m.sb("wd", [P, HC4, D])
        half, eps, spare = m.sb("half", [P, NT]), m.sb("eps", [P, NT]), m.sb("spare", [P, 1])
        q4 = QuantBuffers(m, G * HID4)
        x, stat, mv, rstd = m.sb("x", [P, G, D]), m.sb("stat", [P, G, 6]), m.sb("mv", [P, G, 2]), m.sb("rstd", [P, G])
        xn, hh, hT = m.sb("xn", [P, G * D]), m.sb("hh", [P, G, D]), m.sb("hT", [P, S])
        xq, xqT, vo = m.sb("xq", [P, G * D]), m.sb("xqT", [P, S]), m.sb("vo", [P, G, H * D])
        qu, kT, pos = m.sb("qu", [P, 2, S]), m.sb("kT", [P, 2, S]), m.sb("pos", [KR, 2, S])
        top, total, inv = [m.sb(n, [P, 2, G]) for n in ("top", "total", "inv")]
        prob, probT = m.sb("prob", [P, 2, S]), m.sb("probT", [P, 2, S])
        th, act_in = m.sb("th", [P, 2, HID4]), m.sb("act_in", [P, HID4])
        hid, hidT = m.sb("hid", [P, G * HID4]), m.sb("hidT", [P, HC4, S])
        x_again = m.sb("x_again", [P, G, D])
        g_th, g_a, x_new = m.sb("g_th", [P, S]), m.sb("g_a", [P, S]), m.sb("x_new", [P, G, D])
        pA, pB, pQ, pR, pT, pO = [m.ps(n, [P, S]) for n in ("pA", "pB", "pQ", "pR", "pT", "pO")]
        pS = m.ps("pS", [P, 2, S])
        pos_bank = lambda n: (pR, pA)[n % 2]
        gate_bank, up_bank = lambda g: (pA, pQ)[g % 2], lambda g: (pB, pR)[g % 2]
        past_sp, past_pool = m.sem("past_sp"), m.sem("past_pool")
        loaded, dve_set, pool_set, pe_set, x_read, x_sent = [m.sem(n) for n in ("loaded", "dve_set", "pool_set", "pe_set", "x_read", "x_sent")]
        late_read, x_again_read = m.sem("late_read"), m.sem("x_again_read")
        preparing = m.ev("preparing", 3 + QUANTISE_STEPS)
        made_weights = m.ev("made_weights", QUANTISE_STEPS)
        centred, rstd_made = m.ev("centred", 2), m.ev("rstd_made", 4)
        hh_made, xq_made = m.ev("hh_made", 1), m.ev("xq_made", 1)
        turned_in = m.ev("turned_in", 2)
        xqT_kept, hT_kept = m.ev("xqT_kept", 1), m.ev("hT_kept", 1)
        gu_ready, gate_tanh, hid_made = m.ev("gu_ready", G), m.ev("gate_tanh", G), m.ev("hid_made", G)
        vo_ready, vo_kept = m.ev("vo_ready", 2 * G), m.ev("vo_kept", 2 * G)
        q_ready, pos_ready = m.ev("q_ready", H), m.ev("pos_ready", H)
        k_kept, qu_made, pos_made = m.ev("k_kept", H), m.ev("qu_made", H), m.ev("pos_made", H)
        scored, top_made, exp_made = m.ev("scored", H), m.ev("top_made", H), m.ev("exp_made", H)
        own_made = m.ev("own_made", H)
        inv_made, normed = m.ev("inv_made", H), m.ev("normed", H)
        probT_ready, probT_kept, attended = m.ev("probT_ready", H), m.ev("probT_kept", H), m.ev("attended", H)
        hid_quantised = m.ev("hid_quantised", 1)
        hidT_ready, hidT_kept = m.ev("hidT_ready", HC4), m.ev("hidT_kept", HC4)
        ffn_ready, ffn_tanh = m.ev("ffn_ready", 1), m.ev("ffn_tanh", 1)
        gated = m.ev("gated", 1, credit=True)
        finished = m.ev("finished", 1, credit=True)
        stored = m.ev("stored", 1, credit=True)
        chain = m.ev("chain", QUANTISE_STEPS + G + 2)
        of_batch = lambda t, c, a: t.rearrange("(a c g b) d -> c a b g d", a=B, c=B, g=G)[c, a, :, :, :]
        heads = lambda t: t.rearrange("(h f) d -> f h d", f=F)
        weights = [(ident[:, :], w["ident"]), (ones[:, :], w["ones_row"]), (bout[:, :], w["L1_bout"]), (wq[:, :], w["L1_attn_Wq"]),
                   (wqT[:, :, :], heads(w["L1_WqT"])), (wr[:, :], w["L1_attn_Wr"]), (wvT[:, :, :], heads(w["L1_WvT"])),
                   (wout[:, :, :], heads(w["L1_attn_Wout"])), (peT[:, :], w["L1_peT"]), (uT[:, :], w["L1_uT"]),
                   (vT[:, :], w["L1_vT"]), (gammaT[:, :], w["L1_gammaT"]), (betaT[:, :], w["L1_betaT"]),
                   (own_i[:, :], w["L1_own_i"]), (is_own[:, :], w["L1_is_own"]), (is_next[:, :], w["L1_is_next"]), (place[:, :], w["L1_place"]),
                   (pos[B * B:KR, 0, :], w["L1_own_b"]), (pos[B * B:KR, 1, :], w["L1_own_b"]),
                   (wnat[:, 0:HID4P].rearrange("p (c d) -> p c d", c=HC4), w["L1_wg"].rearrange("(c p) d -> p c d", p=P)),
                   (wnat[:, HID4P:2 * HID4P].rearrange("p (c d) -> p c d", c=HC4), w["L1_wu"].rearrange("(c p) d -> p c d", p=P)),
                   (wnat[:, 2 * HID4P:], w["L1_ffn_w_down"])]
        SETS = 8
        with nc.Block() as block:
            @block.sync
            def _(sp):
                for a in range(B):
                    sp.dma_start(x[a * BB:(a + 1) * BB, :, :], of_batch(x_in, 0, a)).then_inc(x_read, 16)
                for dst, src in weights:
                    sp.dma_start(dst, src).then_inc(loaded, 16)
                with sp.Fori(0, B) as i:
                    sp.wait_ge(*hh_made.at(i, 1))
                    sp.sem_inc(past_sp, 1)
                    for a in range(B):
                        sp.dma_start(x[a * BB:(a + 1) * BB, :, :], of_batch(x_in, (i + 1) % B, a)).then_inc(x_read, 16)
                    sp.wait_ge(*finished.at(i, 0))
                    sp.sem_inc(past_sp, 1)
                    for a in range(B):
                        sp.dma_start(x_again[a * BB:(a + 1) * BB, :, :], of_batch(x_in, i, a)).then_inc(x_again_read, 16)
                    sp.dma_start(late[:, :, :].rearrange("p h t -> p (h t)"), w["L1_late"][i, :].partition_broadcast(B * B)).then_inc(late_read, 16)

            @block.gpsimd
            def _(pool):
                pool.memset(half[:, :], -0.5).then_inc(pool_set, 1)
                pool.memset(eps[:, :], EPS).then_inc(pool_set, 1)
                pool.memset(q4.half_step[:, :], 0x1FFFFF).then_inc(pool_set, 1)
                pool.sem_inc(stored.sem, 1)
                pool.wait_ge(pool_set, 3)

                def roots(n, k):
                    pool.wait_ge(*centred.at(n, k + 1))
                    pool.tensor_tensor(rstd[:, :], mv[:, :, 1], eps[:, :], ALU.add).then_inc(rstd_made.sem, 1)
                    pool.wait_ge(*rstd_made.at(n, 2 * k + 1))
                    pool.tensor_tensor(rstd[:, :], rstd[:, :], half[:, :], ALU.pow).then_inc(rstd_made.sem, 1)

                roots(0, 0)
                roots(0, 1)
                with pool.Fori(0, B) as i:
                    for n in range(H):
                        pool.wait_ge(*inv_made.at(i, n + 1))
                        z = prob[:, n % 2, :].rearrange("p (g j) -> p g j", g=G)
                        pool.tensor_tensor(z, z, inv[:, n % 2, :].unsqueeze(2).to_broadcast([P, G, P]), ALU.mult).then_inc(normed.sem, 1)
                        if n in (3, 4):
                            roots(i + 1, n - 3)
                    pool.wait_ge(*finished.at(i, 1))
                    pool.sem_inc(past_pool, 1)
                    for a in range(B):
                        pool.dma_start(of_batch(x_out, i, a), x_new[a * BB:(a + 1) * BB, :, :]).then_inc(x_sent, 16)
                    pool.wait_ge(x_sent, i * 16 * B + 16 * B)
                    pool.sem_inc(stored.sem, 1)

            @block.vector
            def _(dve):
                dve.wait_ge(pool_set, 3)

                def prepare(n):
                    link = Chain(dve, preparing, n)

                    def stats(src):
                        for t in range(G):
                            last = dve.bn_stats(stat[:, t, :], src(t))
                        link.then(last)
                        dve.memset(spare[:, :], 0.0)
                        for t in range(G):
                            last = dve.bn_aggr(mv[:, t, :], stat[:, t, :])
                        last.then_inc(centred.sem, 1)

                    def scale(k, src, dst):
                        dve.wait_ge(*rstd_made.at(n, 2 * k + 2))
                        for t in range(G):
                            last = dve.tensor_scalar(dst(t), src(t), mv[:, t, 0:1], rstd[:, t:t + 1], ALU.subtract, ALU.mult)
                        return last

                    dve.wait_ge(x_read, n * 16 * B + 16 * B)
                    stats(lambda t: x[:, t, :])
                    yield
                    link.then(scale(0, lambda t: x[:, t, :], lambda t: xn[:, t * D:(t + 1) * D]))
                    stats(lambda t: xn[:, t * D:(t + 1) * D])
                    yield
                    scale(1, lambda t: xn[:, t * D:(t + 1) * D], lambda t: hh[:, t, :]).then_inc(hh_made.sem, 1)
                    yield
                    for _ in quantise(dve, link, q4, xn[:, :], xq[:, :], G * D):
                        yield
                    dve.sem_inc(xq_made.sem, 1)

                for _ in prepare(0):
                    pass
                dve.wait_ge(loaded, 16 * len(weights))
                for _ in quantise(dve, Chain(dve, made_weights, 0), q4, wnat[:, :], wqd[:, :], 2 * HID4P + HID4):
                    pass
                dve.sem_inc(dve_set, 1)
                dve.wait_ge(pe_set, 1)
                dve.tensor_copy(rel[:, :, :, :], pA[:, 0:H * B].rearrange("p (h j) -> p h j", h=H).unsqueeze(2).to_broadcast([P, H, B, B])).then_inc(dve_set, 1)
                dve.wait_ge(pe_set, 2)
                for n in range(H):
                    for dst, part in ((gpos, is_own), (gnext, is_next)):
                        dve.tensor_tensor(dst[:, n, :].rearrange("p (a j) -> p a j", a=B),
                                          pB[:, n * B:(n + 1) * B].unsqueeze(1).to_broadcast([P, B, B]),
                                          part[:, :].rearrange("p (a j) -> p a j", a=B), ALU.mult)
                dve.tensor_copy(gbias[:, :], pQ[0:B * B, 0:H])
                dve.tensor_copy(wvo[:, 0:S], pS[:, 0, :])
                dve.tensor_copy(wvo[:, S:2 * S], pS[:, 1, :])
                dve.tensor_copy(wg[:, :], pR[:, 0:HID4P])
                dve.tensor_copy(wu[:, :], pT[:, 0:HID4P])
                dve.tensor_copy(wd[:, 0:2, :], pO[:, 0:2 * D].rearrange("p (c d) -> p c d", c=2))
                dve.tensor_copy(wd[0:HID4 - 2 * P, 2, :], pO[0:HID4 - 2 * P, 2 * D:3 * D]).then_inc(dve_set, 1)
                dve.sem_inc(finished.sem, 1)
                dve.sem_inc(gated.sem, 1)

                with dve.Fori(0, B) as i:
                    link = Chain(dve, chain, i)
                    dve.wait_ge(*turned_in.at(i, 2))
                    dve.tensor_scalar(hT[:, :], pB[:, :], gammaT[:, :], betaT[:, :], ALU.mult, ALU.add).then_inc(hT_kept.sem, 1)
                    for g in range(G):
                        if g:
                            dve.wait_ge(*hid_made.at(i, g))
                        dve.wait_ge(*gate_tanh.at(i, g + 1))
                        link.then(dve.scalar_tensor_tensor(act_in[:, :], th[:, g % 2, :], 1.0, gate_bank(g)[:, 0:HID4], ALU.add, ALU.mult))
                        dve.scalar_tensor_tensor(hid[:, g * HID4:(g + 1) * HID4], act_in[:, :], 0.5, up_bank(g)[:, 0:HID4], ALU.mult, ALU.mult).then_inc(hid_made.sem, 1)
                    dve.wait_ge(*hid_made.at(i, G))
                    steps = quantise(dve, link, q4, hid[:, :], hid[:, :], G * HID4)

                    def operands(n):
                        dve.wait_ge(*k_kept.at(i, n + 1))
                        if n >= 2:
                            dve.wait_ge(*scored.at(i, n - 1))
                        dve.tensor_scalar(qu[:, n % 2, :], kT[:, n % 2, :], uT[:, n:n + 1], C, ALU.add, ALU.mult).then_inc(qu_made.sem, 1)
                        dve.wait_ge(*pos_ready.at(i, n + 1))
                        dve.scalar_tensor_tensor(pos[0:B * B, n % 2, :], pos_bank(n)[0:B * B, :], gbias[:, n:n + 1], own_i[:, :], ALU.add, ALU.mult).then_inc(own_made.sem, 1)
                        dve.wait_ge(*own_made.at(i, n + 1))
                        first = pos[0:B * B, n % 2, 0:P]
                        dve.tensor_tensor(first, first, late[:, n, :], ALU.mult).then_inc(pos_made.sem, 1)

                    dve.wait_ge(late_read, i * 16 + 16)

                    def highest(n):
                        dve.wait_ge(*scored.at(i, n + 1))
                        dve.tensor_reduce(top[:, n % 2, :], pS[:, n % 2, :].rearrange("p (g j) -> p g j", g=G), AX.X, ALU.max, negate=True).then_inc(top_made.sem, 1)

                    def inverse(n):
                        dve.wait_ge(*exp_made.at(i, n + 1))
                        dve.reciprocal(inv[:, n % 2, :], total[:, n % 2, :]).then_inc(inv_made.sem, 1)

                    for k in range(H + 2):
                        if k < H:
                            operands(k)
                        if 0 <= k - 1 < H:
                            highest(k - 1)
                        if k < 6:
                            for _ in range(QUANTISE_STEPS // 6):
                                next(steps)
                        if k == 5:
                            dve.sem_inc(hid_quantised.sem, 1)
                            steps = prepare(i + 1)
                        if 5 <= k <= 7:
                            next(steps)
                        if k >= 7:
                            for _ in range(4):
                                next(steps, None)
                        if 0 <= k - 2 < H:
                            inverse(k - 2)
                    for _ in steps:
                        pass
                    dve.wait_ge(*ffn_tanh.at(i, 1))
                    dve.scalar_tensor_tensor(g_a[:, :], g_th[:, :], 1.0, pB[:, :], ALU.add, ALU.mult).then_inc(gated.sem, 1)
                    dve.wait_ge(*gated.at(i, 1))
                    dve.wait_ge(*attended.at(i, H))
                    link.then(dve.scalar_tensor_tensor(g_a[:, :], g_a[:, :], 0.5, pO[:, :], ALU.mult, ALU.mult))
                    dve.wait_ge(*stored.at(i, 0))
                    dve.wait_ge(x_again_read, i * 16 * B + 16 * B)
                    link.then(dve.tensor_tensor(x_new[:, :, :], g_a[:, :].rearrange("p (g d) -> p g d", g=G), x_again[:, :, :], ALU.add))
                    dve.sem_inc(finished.sem, 1)
                    link.done()

            @block.scalar
            def _(act):
                with act.Fori(0, B) as i:
                    act.wait_ge(*turned_in.at(i, 1))
                    act.copy(xqT[:, :], pA[:, :]).then_inc(xqT_kept.sem, 1)
                    for g in range(G):
                        act.wait_ge(*gu_ready.at(i, g + 1))
                        act.activation(th[:, g % 2, :], gate_bank(g)[:, 0:HID4], ACT.Tanh, scale=0.5).then_inc(gate_tanh.sem, 1)
                        for n in range(2 * g, 2 * g + 2):
                            act.wait_ge(*vo_ready.at(i, n + 1))
                            act.copy(vo[:, g, (n % 2) * S:(n % 2 + 1) * S], pS[:, n % 2, :]).then_inc(vo_kept.sem, 1)

                    def keep_k(n):
                        act.wait_ge(*q_ready.at(i, n + 1))
                        if n >= 2:
                            act.wait_ge(*scored.at(i, n - 1))
                        act.copy(kT[:, n % 2, :], pQ[:, :]).then_inc(k_kept.sem, 1)

                    def exps(n):
                        act.wait_ge(*top_made.at(i, n + 1))
                        if n >= 2:
                            act.wait_ge(*probT_ready.at(i, n - 1))
                        for g in range(G):
                            cut = slice(g * P, (g + 1) * P)
                            last = act.activation(prob[:, n % 2, cut], pS[:, n % 2, cut], ACT.Exp, bias=top[:, n % 2, g:g + 1],
                                                  accum_out=total[:, n % 2, g:g + 1])
                        last.then_inc(exp_made.sem, 1)

                    def keep_probT(n):
                        act.wait_ge(*probT_ready.at(i, n + 1))
                        if n >= 2:
                            act.wait_ge(*attended.at(i, n - 1))
                        act.copy(probT[:, n % 2, :], pT[:, :]).then_inc(probT_kept.sem, 1)

                    def keep_hidT(c):
                        act.wait_ge(*hidT_ready.at(i, c + 1))
                        rows_of = min(P, HID4 - c * P)
                        act.copy(hidT[0:rows_of, c, :], pB[0:rows_of, :]).then_inc(hidT_kept.sem, 1)

                    for k in range(H + 3):
                        if k < H:
                            keep_k(k)
                        if 7 <= k < 7 + HC4:
                            keep_hidT(k - 7)
                        if 0 <= k - 1 < H:
                            exps(k - 1)
                        if 0 <= k - 3 < H:
                            keep_probT(k - 3)
                    act.wait_ge(*ffn_ready.at(i, 1))
                    act.activation(g_th[:, :], pB[:, :], ACT.Tanh, scale=0.5).then_inc(ffn_tanh.sem, 1)
            @block.tensor
            def _(pe):
                pe.wait_ge(loaded, 16 * len(weights))
                for n in range(H):
                    last = pe.matmul(pA[:, n * B:(n + 1) * B], wr[:, n * F:(n + 1) * F], peT[:, :], start=True, stop=True)
                last.then_inc(pe_set, 1)
                pe.wait_ge(dve_set, 2)
                for n in range(H):
                    pe.matmul(pB[:, n * B:(n + 1) * B], wqT[:, n, :], rel[:, n, 0, :], start=True, stop=True)
                    pe.matmul(pQ[0:B * B, n:n + 1], rel[:, n, :, :].rearrange("p a j -> p (a j)"), vT[:, n:n + 1], start=True, stop=True)
                    pe.matmul(pS[:, n // 4, (n % 4) * D:(n % 4 + 1) * D], wvT[:, n, :], wout[:, n, :], start=True, stop=True)
                for c in range(HC4):
                    pe.transpose(pR[:, c * P:(c + 1) * P], wqd[:, c * P:(c + 1) * P], ident[:, :])
                    pe.transpose(pT[:, c * P:(c + 1) * P], wqd[:, HID4P + c * P:HID4P + (c + 1) * P], ident[:, :])
                    rows_of = min(P, HID4 - c * P)
                    last = pe.transpose(pO[0:rows_of, c * D:(c + 1) * D], wqd[:, 2 * HID4P + c * P:2 * HID4P + c * P + rows_of], ident[:, :])
                last.then_inc(pe_set, 1)
                pe.wait_ge(dve_set, 3)
                with pe.Fori(0, B) as i:
                    pe.wait_ge(*xq_made.at(i, 1))
                    for t in range(G):
                        last = pe.transpose(pA[:, t * P:(t + 1) * P], xq[:, t * D:(t + 1) * D], ident[:, :])
                    last.then_inc(turned_in.sem, 1)
                    pe.wait_ge(*gated.at(i, 0))
                    for t in range(G):
                        last = pe.transpose(pB[:, t * P:(t + 1) * P], hh[:, t, :], ident[:, :])
                    last.then_inc(turned_in.sem, 1)
                    pe.wait_ge(*xqT_kept.at(i, 1))
                    pe.wait_ge(*hT_kept.at(i, 1))

                    def gate_up(g):
                        if g >= 2:
                            pe.wait_ge(*hid_made.at(i, g - 1))
                        pe.matmul(gate_bank(g)[:, 0:HID4], xqT[:, g * P:(g + 1) * P], wg[:, 0:HID4], start=True, stop=True)
                        pe.matmul(up_bank(g)[:, 0:HID4], xqT[:, g * P:(g + 1) * P], wu[:, 0:HID4], start=True, stop=True).then_inc(gu_ready.sem, 1)

                    def value(n):
                        if n >= 2:
                            pe.wait_ge(*vo_kept.at(i, n - 1))
                        pe.matmul(pS[:, n % 2, :], hT[:, (n // 2) * P:(n // 2 + 1) * P], wvo[:, (n % 2) * S:(n % 2 + 1) * S],
                                  start=True, stop=True).then_inc(vo_ready.sem, 1)

                    for g in range(G):
                        gate_up(g)
                        value(2 * g)
                        value(2 * g + 1)

                    def queries(n):
                        if n:
                            pe.wait_ge(*k_kept.at(i, n))
                        else:
                            pe.wait_ge(*hid_made.at(i, G))
                        pe.matmul(pQ[:, :], wq[:, n * F:(n + 1) * F], hT[:, :], start=True, stop=True).then_inc(q_ready.sem, 1)
                        if n >= 2:
                            pe.wait_ge(*pos_made.at(i, n - 1))
                        pe.matmul(pos_bank(n)[0:B * B, :], gpos[:, n, :], hT[:, :], start=True, stop=True)
                        pe.matmul(pos_bank(n)[0:B * B, :].rearrange("p (g t) -> p g t", g=G)[:, :, 0:P - BB], gnext[:, n, :],
                                  hT[:, :].rearrange("p (g t) -> p g t", g=G)[:, :, BB:P], start=False, stop=True,
                                  skip_group_check=True).then_inc(pos_ready.sem, 1)

                    def scores(n):
                        pe.wait_ge(*k_kept.at(i, n + 1))
                        pe.wait_ge(*pos_made.at(i, n + 1))
                        if n >= 2:
                            pe.wait_ge(*exp_made.at(i, n - 1))
                        else:
                            pe.wait_ge(*vo_kept.at(i, 2 * G))
                        for g in range(G):
                            cut = slice(g * P, (g + 1) * P)
                            pe.matmul(pS[:, n % 2, cut], qu[:, n % 2, cut], kT[:, n % 2, cut], start=True, stop=False)
                            last = pe.matmul(pS[:, n % 2, cut], pos[:, n % 2, cut], place[:, :], start=False, stop=True)
                        last.then_inc(scored.sem, 1)

                    def turn(n):
                        pe.wait_ge(*normed.at(i, n + 1))
                        if n:
                            pe.wait_ge(*probT_kept.at(i, n))
                        for g in range(G):
                            last = pe.transpose(pT[:, g * P:(g + 1) * P], prob[:, n % 2, g * P:(g + 1) * P], ident[:, :])
                        last.then_inc(probT_ready.sem, 1)

                    def attend(n):
                        pe.wait_ge(*probT_kept.at(i, n + 1))
                        for g in range(G):
                            if n == 0 and g == 0:
                                pe.wait_ge(*finished.at(i, 0))
                            if n == 0:
                                pe.matmul(pO[:, g * D:(g + 1) * D], ones[:, :], bout[:, :], start=(g == 0), stop=False, skip_group_check=True)
                            last = pe.matmul(pO[:, g * D:(g + 1) * D], probT[:, n % 2, g * P:(g + 1) * P], vo[:, g, n * D:(n + 1) * D],
                                             start=False, stop=(n == H - 1), skip_group_check=True)
                        last.then_inc(attended.sem, 1)

                    def turn_hidden(c):
                        rows_of = min(P, HID4 - c * P)
                        for g in range(G):
                            last = pe.transpose(pB[0:rows_of, g * P:(g + 1) * P],
                                                hid[:, g * HID4 + c * P:g * HID4 + c * P + rows_of], ident[:, :])
                        last.then_inc(hidT_ready.sem, 1)

                    def down():
                        for g in range(G):
                            for c in range(HC4):
                                rows_of = min(P, HID4 - c * P)
                                last = pe.matmul(pB[:, g * D:(g + 1) * D], hidT[0:rows_of, c, g * P:(g + 1) * P], wd[0:rows_of, c, :],
                                                 start=(c == 0), stop=(c == HC4 - 1))
                        last.then_inc(ffn_ready.sem, 1)

                    for k in range(H + 4):
                        if k == 7:
                            pe.wait_ge(*hid_quantised.at(i, 1))
                        if 7 <= k < 7 + HC4:
                            if k > 7:
                                pe.wait_ge(*hidT_kept.at(i, k - 7))
                            turn_hidden(k - 7)
                        if k == H + 2:
                            pe.wait_ge(*hidT_kept.at(i, HC4))
                            down()
                        if k < H:
                            queries(k)
                        if 0 <= k - 1 < H:
                            scores(k - 1)
                        if 0 <= k - 3 < H:
                            turn(k - 3)
                        if 0 <= k - 4 < H:
                            attend(k - 4)


def layer2(nc, w, x_in, x_out):
    TB = 3
    LEAD, LAG = 2, 3
    BY_ACT = 3
    R = P
    W = 2 * P
    SLOTS = 4
    STEP = S + P
    with ExitStack() as stack:
        m = Scope(nc, stack, "c_")
        ident, identb, maskb = m.sb("ident", [P, P]), m.sb("identb", [P, P], BF16), m.sb("maskb", [P, P], BF16)
        wqkv = m.sb("wqkv", [P, 3 * D])
        last_k, minus_last = m.sb("last_k", [P, 1]), m.sb("minus_last", [P, 1])
        place_k, place_last, place_rest = m.sb("place_k", [HD, R]), m.sb("place_last", [HD, 1]), m.sb("place_rest", [HD, R])
        place_p = [m.sb(f"place_p{j}", [HD, R], BF16) for j in range(3)]
        places = m.sb("places", [KR6, R], BF16)
        place_wide = m.sb("place_wide", [P, LEAD, R])
        vz = m.sb("vz", [P, NT, HN, P // 2])
        place_vz = m.sb("place_vz", [R, HN, P // 2])
        no_b, spread_t = m.sb("no_b", [P, P], BF16), m.sb("spread_t", [P, NT, P])
        last_v, place_v, every_last_v = m.sb("last_v", [1, D]), m.sb("place_v", [R, HD]), m.sb("every_last_v", [R, HD])
        rel = m.sb("rel", [P, 3, NT, W])
        before = rel[:, :, :, :].rearrange("p a t c -> p (a t c)")
        wide = 2 * HID4P + HID4
        wnat, wqd = before[:, 0:wide], before[:, wide:2 * wide]
        wg, wu, wd = m.sb("wg", [P, HID4P]), m.sb("wu", [P, HID4P]), m.sb("wd", [P, HC4, D])
        q4 = QuantBuffers(m, NT * HID4)
        wc = m.sb("wc", [P, D])
        ones = m.sb("ones", [1, P])
        half, eps, spare = m.sb("half", [P, NT]), m.sb("eps", [P, NT]), m.sb("spare", [P, 1])
        x, stat, mv, rstd = m.sb("x", [P, NT, D]), m.sb("stat", [P, NT, 6]), m.sb("mv", [P, NT, 2]), m.sb("rstd", [P, NT])
        xn, xnT = m.sb("xn", [P, NT, D]), m.sb("xnT", [P, S])
        qf, kf, rest_q, rest_k = [m.sb(n, [P, S]) for n in ("qf", "kf", "rest_q", "rest_k")]
        qp, kp = m.sb("qp", [P, 3, S], BF16), m.sb("kp", [P, 3, S], BF16)
        qs, ks = m.sb("qs", [KR6, HN, S], BF16), m.sb("ks", [KR6, HN, S], BF16)
        low, total, inv, invT = m.sb("low", [P, ITEMS]), m.sb("total", [P, P]), m.sb("inv", [P, P]), m.sb("invT", [P, P])
        prob, probT = m.sb("prob", [P, 3, (NT - 1) * STEP + W]), m.sb("probT", [P, 3, S])
        far = m.sb("far", [P, 2])
        by_place = m.sb("by_place", [P, 2, NT, R])
        band, bandT = m.sb("band", [P, 3, NT, R]), m.sb("bandT", [P, 2, S])
        y_kept, yT = m.sb("y_kept", [P, S]), m.sb("yT", [P, S])
        x_again = m.sb("x_again", [P, NT, D])
        xq, xqT = m.sb("xq", [P, NT * D]), m.sb("xqT", [P, S])
        th, act_in = m.sb("th", [P, 2, HID4]), m.sb("act_in", [P, HID4])
        hid, hidT = m.sb("hid", [P, NT * HID4]), m.sb("hidT", [P, HC4, S])
        g_th, g_a, x_new = m.sb("g_th", [P, NT, D]), m.sb("g_a", [P, NT, D]), m.sb("x_new", [P, NT, D])
        pS, pT = m.ps("pS", [P, SB, S]), m.ps("pT", [P, TB, S])
        pY, pA = m.ps("pY", [P, S]), m.ps("pA", [P, S])
        gate_bank = lambda t: (pS[:, 0, :], pT[:, 0, :])[t % 2]
        up_bank = lambda t: (pS[:, 1, :], pT[:, 1, :])[t % 2]
        total_at = lambda n: n % NT * 32 + n // NT
        q_dram, k_dram = [nc.dram_tensor(f"c_{n}", (3, HD, HN * S), BF16).ap() for n in ("q_parts", "k_parts")]

        rel_dram = nc.dram_tensor("c_rel_dram", (SLOTS, NT * P * W), F32).ap()
        band_dram = nc.dram_tensor("c_band_dram", (SLOTS, NT * P * W), F32).ap()

        def straight(dram, h):
            return dram[h % SLOTS, :].rearrange("(t p c) -> p t c", t=NT, c=W)

        def skewed(dram, h):
            whole = straight(dram, h)
            return bass.AP(whole.tensor, whole.offset + 1, [[W + 1, P], [P * W, NT], [1, R]])

        loaded, pool_set, pe_set, dve_set, x_read, x_sent = [m.sem(n) for n in ("loaded", "pool_set", "pe_set", "dve_set", "x_read", "x_sent")]
        cleared, spread = m.sem("cleared"), m.sem("spread")
        past_sp, past_pool, past_dve = m.sem("past_sp"), m.sem("past_pool"), m.sem("past_dve")
        q_sent, k_sent, terms_read = m.sem("q_sent"), m.sem("k_sent"), m.sem("terms_read")
        by_slot = lambda n: [m.ev16(f"{n}{slot}", HN // SLOTS) for slot in range(SLOTS)]
        rel_sent, rel_read = by_slot("rel_sent"), by_slot("rel_read")
        band_sent, band_read = by_slot("band_sent"), by_slot("band_read")
        of_head = lambda events, i, h: events[h % SLOTS].at(i, h // SLOTS + 1)
        made_weights, made_places = m.ev("made_weights", QUANTISE_STEPS), m.ev("made_places", 6)
        stats_made, x_again_read = m.ev("stats_made", 1), m.sem("x_again_read")
        quantising = m.ev("quantising", QUANTISE_STEPS)
        centred, rstd_made, xn_made = m.ev("centred", 1), m.ev("rstd_made", 2), m.ev("xn_made", 1)
        xT_ready, xT_kept = m.ev("xT_ready", 1), m.ev("xT_kept", 1)
        proj_ready = m.ev("proj_ready", 3)
        q_kept = m.ev("q_kept", 1)
        q_split, k_split = m.ev("q_split", 1), m.ev("k_split", 1)
        v_kept = m.ev("v_kept", 1)
        xq_made, xqT_ready, xqT_kept = m.ev("xq_made", 1), m.ev("xqT_ready", 1), m.ev("xqT_kept", 1)
        gu_ready, gate_tanh, hid_made = m.ev("gu_ready", NT), m.ev("gate_tanh", NT), m.ev("hid_made", NT)
        hid_quantised, hidT_ready, hidT_kept = m.ev("hid_quantised", 1), m.ev("hidT_ready", HC4), m.ev("hidT_kept", HC4)
        ffn_ready, g_tanh = m.ev("ffn_ready", 1), m.ev("g_tanh", 1)
        places_ready, places_kept = m.ev("places_ready", HN), m.ev("places_kept", HN)
        scored, low_made, exp_made = m.ev("scored", ITEMS), m.ev("low_made", ITEMS), m.ev("exp_made", ITEMS)
        far_made = m.ev("far_made", ITEMS // 2)
        probT_ready, attended = m.ev("probT_ready", ITEMS), m.ev("attended", ITEMS)
        probT_kept_act, probT_kept_dve = m.ev("probT_kept_act", HN * BY_ACT), m.ev("probT_kept_dve", HN * (NT - BY_ACT))
        bandT_ready, bandT_kept, band_attended = m.ev("bandT_ready", HN), m.ev("bandT_kept", HN), m.ev("band_attended", HN)
        inv_made, invT_ready, invT_kept = m.ev("inv_made", 1), m.ev("invT_ready", 1), m.ev("invT_kept", 1)
        inv_spread, y_copied, yT_made, s_ready = m.ev("inv_spread", 1), m.ev("y_copied", 1), m.ev("yT_made", 1), m.ev("s_ready", 1)
        finished, stored = m.ev("finished", 1, credit=True), m.ev("stored", 1, credit=True)
        chain = m.ev("chain", 4 + 5 + 2 * QUANTISE_STEPS + NT + 3)

        HH = HN // 2
        half_rows = lambda h: slice(h // HH * HH * HD, (h // HH + 1) * HH * HD)

        def columns(whole, half_of, tiles):
            return bass.AP(whole.tensor, whole.offset + half_of * HH * HH * HD,
                           [list(whole.ap[0]), [HN * HH * HD, tiles], [HH * HD + HD, HH], [1, HD]])

        LOADS = len(Q_GROUPS) + len(K_GROUPS)
        k_of = lambda n: (n % NT + 1) * P
        kept_by_act = lambda n: n % NT < BY_ACT
        at_prob = lambda n: n % NT * S + P

        def kept_wait(eng, i, n):
            if kept_by_act(n):
                eng.wait_ge(*probT_kept_act.at(i, BY_ACT * (n // NT) + n % NT + 1))
            else:
                eng.wait_ge(*probT_kept_dve.at(i, (NT - BY_ACT) * (n // NT) + n % NT - BY_ACT + 1))

        NORM_AT = 8
        EARLY = 7
        turns = []
        for n in range(ITEMS + NT * LAG + 1):
            if 0 <= n - 3 < ITEMS:
                turns.append(("item", n - 3))
            if n % NT == 3 and 0 <= n // NT - LAG < HN:
                turns.append(("band", n // NT - LAG))
        bank_of = {one: r % TB for r, one in enumerate(turns)}

        def bank_free(eng, i, one):
            r = turns.index(one)
            if r >= TB:
                kind, n = turns[r - TB]
                if kind == "item":
                    kept_wait(eng, i, n)
                else:
                    eng.wait_ge(*bandT_kept.at(i, n + 1))

        weights = [(ident[:, :], w["ident"]), (identb[:, :], w["identb"]), (maskb[:, :], w["maskb"]), (spread_t[:, :, :], w["spread_t"]),
                   (wqkv[:, :], w["L2_attn_w_attn"]), (wc[:, :], w["L2_attn_w_proj"]), (ones[:, :], w["ones_row"]),
                   (last_k[:, :], w["L2_last_k"]), (place_k[:, :], w["L2_place_k"]), (place_last[:, :], w["L2_place_last"]),
                   (last_v[:, :], w["L2_last_v"]), (place_v[:, :], w["L2_place_v"]),
                   (every_last_v[:, :], w["L2_last_v"][0, 0:HD].partition_broadcast(R)),
                   (wnat[:, 0:HID4P].rearrange("p (c d) -> p c d", c=HC4), w["L2_wg"].rearrange("(c p) d -> p c d", p=P)),
                   (wnat[:, HID4P:2 * HID4P].rearrange("p (c d) -> p c d", c=HC4), w["L2_wu"].rearrange("(c p) d -> p c d", p=P)),
                   (wnat[:, 2 * HID4P:], w["L2_ffn_w_down"])]
        with nc.Block() as block:
            @block.sync
            def _(sp):
                sp.dma_start(x[:, :, :], rows(x_in, 0)).then_inc(x_read, 16)
                for dst, src in weights:
                    sp.dma_start(dst, src).then_inc(loaded, 16)
                sp.wait_ge(pool_set, 8)
                for slot in range(SLOTS):
                    for dram in (rel_dram, band_dram):
                        sp.dma_start(straight(dram, slot), vz[:, 0, :, :].rearrange("p h c -> p (h c)").rearrange("p (t c) -> p t c", t=NT)).then_inc(cleared, 16)
                sp.wait_ge(*made_places.at(0, 6))
                sp.sem_inc(past_sp, 1)
                for n, (_, j) in enumerate(TERMS):
                    sp.dma_start(places[n * HD:(n + 1) * HD, :], place_p[j][:, :]).then_inc(spread, 16)
                for h in range(LEAD):
                    sp.dma_start(place_wide[h * HD:(h + 1) * HD, h, :], place_k[:, :]).then_inc(spread, 16)
                sp.wait_ge(cleared, 16 * 2 * SLOTS)
                sp.sem_inc(past_sp, 1)
                with sp.Fori(0, B) as i:
                    sp.wait_ge(*xn_made.at(i, 1))
                    sp.sem_inc(past_sp, 1)
                    sp.dma_start(x[:, :, :], rows(x_in, (i + 1) % B)).then_inc(x_read, 16)
                    sp.wait_ge(*finished.at(i, 0))
                    sp.sem_inc(past_sp, 1)
                    sp.dma_start(x_again[:, :, :], rows(x_in, i)).then_inc(x_again_read, 16)

                    def send_rel(k):
                        if k >= SLOTS:
                            sp.wait_ge(*of_head(rel_read, i, k - SLOTS))
                            sp.sem_inc(past_sp, 1)
                        sp.wait_ge(*places_kept.at(i, k + 1))
                        sp.sem_inc(past_sp, 1)
                        sp.dma_start(skewed(rel_dram, k), by_place[:, k % 2, :, :]).then_inc(rel_sent[k % SLOTS].sem, 16)

                    def read_rel(h):
                        sp.wait_ge(*of_head(rel_sent, i, h))
                        sp.sem_inc(past_sp, 1)
                        if h >= 3:
                            sp.wait_ge(*low_made.at(i, NT * (h - 2)))
                            sp.sem_inc(past_sp, 1)
                        sp.dma_start(rel[:, h % 3, :, :], straight(rel_dram, h)).then_inc(rel_read[h % SLOTS].sem, 16)

                    def send_band(k):
                        if k >= SLOTS:
                            sp.wait_ge(*of_head(band_read, i, k - SLOTS))
                            sp.sem_inc(past_sp, 1)
                        sp.wait_ge(*exp_made.at(i, NT * (k + 1)))
                        sp.sem_inc(past_sp, 1)
                        whole = prob[:, k % 3, :]
                        band_of_prob = bass.AP(whole.tensor, whole.offset, [list(whole.ap[0]), [STEP, NT], [1, W]])
                        sp.dma_start(straight(band_dram, k), band_of_prob).then_inc(band_sent[k % SLOTS].sem, 16)

                    def read_band(h):
                        sp.wait_ge(*of_head(band_sent, i, h))
                        sp.sem_inc(past_sp, 1)
                        if h >= 3:
                            sp.wait_ge(*bandT_ready.at(i, h - 2))
                            sp.sem_inc(past_sp, 1)
                        sp.dma_start(band[:, h % 3, :, :], skewed(band_dram, h)).then_inc(band_read[h % SLOTS].sem, 16)

                    sp.wait_ge(*q_split.at(i, 1))
                    sp.sem_inc(past_sp, 1)
                    send_parts(sp, q_dram, qp, q_sent)
                    send_rel(0)
                    sp.wait_ge(*k_split.at(i, 1))
                    sp.sem_inc(past_sp, 1)
                    send_parts(sp, k_dram, kp, k_sent)
                    sp.wait_ge(q_sent, i * 48 + 48)
                    sp.sem_inc(past_sp, 1)
                    load_terms(sp, qs, q_dram, Q_GROUPS, terms_read)
                    read_rel(0)
                    sp.wait_ge(k_sent, i * 48 + 48)
                    sp.sem_inc(past_sp, 1)
                    load_terms(sp, ks, k_dram, K_GROUPS, terms_read)
                    send_rel(1)
                    for k in range(2, HN + LEAD + 2):
                        if k < HN:
                            send_rel(k)
                        if k <= HN:
                            read_rel(k - 1)
                        if 0 <= k - LEAD - 1 < HN:
                            send_band(k - LEAD - 1)
                        if 0 <= k - LEAD - 2 < HN:
                            read_band(k - LEAD - 2)

            @block.gpsimd
            def _(pool):
                pool.memset(half[:, :], -0.5).then_inc(pool_set, 1)
                pool.memset(eps[:, :], EPS).then_inc(pool_set, 1)
                pool.memset(q4.half_step[:, :], 0x1FFFFF).then_inc(pool_set, 1)
                pool.wait_ge(pool_set, 3)

                def roots(n):
                    pool.wait_ge(*centred.at(n, 1))
                    pool.tensor_tensor(rstd[:, :], mv[:, :, 1], eps[:, :], ALU.add).then_inc(rstd_made.sem, 1)
                    pool.wait_ge(*rstd_made.at(n, 1))
                    pool.tensor_tensor(rstd[:, :], rstd[:, :], half[:, :], ALU.pow).then_inc(rstd_made.sem, 1)

                roots(0)
                pool.memset(vz[:, :, :, :], 0.0).then_inc(pool_set, 1)
                pool.memset(prob[:, :, 0:P], 0.0).then_inc(pool_set, 1)
                pool.memset(total[:, :], 1.0).then_inc(pool_set, 1)
                pool.memset(place_wide[:, :, :], 0.0).then_inc(pool_set, 1)
                pool.memset(no_b[:, :], 0.0).then_inc(pool_set, 1)
                pool.sem_inc(stored.sem, 1)
                pool.wait_ge(pool_set, 8)
                pool.wait_ge(cleared, 16 * 2 * SLOTS)

                with pool.Fori(0, B) as i:
                    roots(i + 1)
                    pool.wait_ge(*finished.at(i, 1))
                    pool.sem_inc(past_pool, 1)
                    pool.dma_start(rows(x_out, i), x_new[:, :, :]).then_inc(x_sent, 16)
                    pool.wait_ge(x_sent, i * 16 + 16)
                    pool.sem_inc(past_pool, 1)
                    pool.sem_inc(stored.sem, 1)

            @block.vector
            def _(dve):
                dve.wait_ge(pool_set, 3)

                def normalise(n):
                    dve.wait_ge(x_read, n * 16 + 16)
                    for t in range(NT):
                        last = dve.bn_stats(stat[:, t, :], x[:, t, :])
                    last.then_inc(stats_made.sem, 1)
                    dve.wait_ge(*stats_made.at(n, 1))
                    dve.memset(spare[:, :], 0.0)
                    for t in range(NT):
                        last = dve.bn_aggr(mv[:, t, :], stat[:, t, :])
                    last.then_inc(centred.sem, 1)
                    yield
                    dve.wait_ge(*rstd_made.at(n, 2))
                    for t in range(NT):
                        last = dve.tensor_scalar(xn[:, t, :], x[:, t, :], mv[:, t, 0:1], rstd[:, t:t + 1], ALU.subtract, ALU.mult)
                    last.then_inc(xn_made.sem, 1)
                    dve.wait_ge(*xn_made.at(n, 1))
                    yield
                    for _ in quantise(dve, Chain(dve, quantising, n), q4, xn[:, :, :].rearrange("p t d -> p (t d)"), xq[:, :], NT * D):
                        yield
                    dve.sem_inc(xq_made.sem, 1)

                for _ in normalise(0):
                    pass
                dve.wait_ge(loaded, 16 * len(weights))
                dve.wait_ge(pool_set, 8)
                link = Chain(dve, made_places, 0)
                dve.tensor_scalar(minus_last[:, :], last_k[:, :], -1.0, None, ALU.mult)
                link.then(dve.tensor_scalar(place_k[:, :], place_k[:, :], place_last[:, :], -1.0, ALU.subtract, ALU.mult))
                link.then(dve.tensor_tensor(place_v[:, :], place_v[:, :], every_last_v[:, :], ALU.subtract))
                split3(dve, link, place_k[:, :], [z[:, :] for z in place_p], place_rest[:, :])
                link.done()
                for _ in quantise(dve, Chain(dve, made_weights, 0), q4, wnat[:, :], wqd[:, :], 2 * HID4P + HID4):
                    pass
                dve.sem_inc(dve_set, 1)
                dve.wait_ge(pe_set, 1)
                dve.tensor_copy(wg[:, :], pS[:, 0, 0:HID4P])
                dve.tensor_copy(wu[:, :], pS[:, 1, 0:HID4P])
                dve.tensor_copy(wd[:, 0:2, :], pS[:, 2, 0:2 * D].rearrange("p (c d) -> p c d", c=2))
                dve.tensor_copy(wd[0:HID4 - 2 * P, 2, :], pS[0:HID4 - 2 * P, 2, 2 * D:3 * D]).then_inc(dve_set, 1)
                dve.memset(place_vz[:, :, :], 0.0).then_inc(dve_set, 1)
                dve.wait_ge(dve_set, 3)
                for half_of in range(2):
                    last = dve.tensor_copy(columns(place_vz[:, :, :], half_of, 1)[:, 0, :, :], place_v[:, :].unsqueeze(1).to_broadcast([R, HH, HD]))
                last.then_inc(dve_set, 1)
                dve.sem_inc(finished.sem, 1)

                with dve.Fori(0, B) as i:
                    link = Chain(dve, chain, i)
                    dve.wait_ge(*proj_ready.at(i, 1))
                    dve.tensor_copy(qf[:, :], pA[:, :]).then_inc(q_kept.sem, 1)
                    dve.wait_ge(*q_kept.at(i, 1))
                    split3(dve, link, qf[:, :], [qp[:, j, :] for j in range(3)], rest_q[:, :])
                    dve.sem_inc(q_split.sem, 1)
                    dve.wait_ge(*proj_ready.at(i, 2))
                    link.then(dve.tensor_scalar(kf[:, :], pS[:, 2, :], -float(np.float32(HD ** -0.5)), minus_last[:, :], ALU.mult, ALU.add))
                    split3(dve, link, kf[:, :], [kp[:, j, :] for j in range(3)], rest_k[:, :])
                    dve.sem_inc(k_split.sem, 1)
                    for t in range(NT):
                        if t:
                            dve.wait_ge(*hid_made.at(i, t))
                        dve.wait_ge(*gate_tanh.at(i, t + 1))
                        link.then(dve.scalar_tensor_tensor(act_in[:, :], th[:, t % 2, :], 1.0, gate_bank(t)[:, 0:HID4], ALU.add, ALU.mult))
                        dve.scalar_tensor_tensor(hid[:, t * HID4:(t + 1) * HID4], act_in[:, :], 0.5, up_bank(t)[:, 0:HID4], ALU.mult, ALU.mult).then_inc(hid_made.sem, 1)
                    dve.wait_ge(*hid_made.at(i, NT))

                    def quantise_hidden():
                        for part in (hid[:, 0:NT * HID4 // 2], hid[:, NT * HID4 // 2:]):
                            yield from quantise(dve, link, q4, part, part, NT * HID4 // 2)

                    steps = quantise_hidden()

                    def lowest(n):
                        h, t, k = n // NT, n % NT, k_of(n)
                        dve.wait_ge(*scored.at(i, n + 1))
                        near = max(0, t - 1) * P
                        start = 3e38
                        if t >= 2:
                            start = far[:, t % 2:t % 2 + 1]
                            dve.tensor_reduce(start, pS[:, n % SB, 0:near], AX.X, ALU.min).then_inc(far_made.sem, 1)
                            dve.wait_ge(*far_made.at(i, 2 * h + t - 1))
                        if t == 0:
                            dve.wait_ge(*of_head(rel_read, i, h))
                        dve.sem_inc(past_dve, 1)
                        near_s = pS[:, n % SB, near:k]
                        dve.tensor_tensor_reduce(near_s, near_s, rel[:, h % 3, t, W - (k - near):W], 1.0, start, ALU.add, ALU.min,
                                                 low[:, n:n + 1]).then_inc(low_made.sem, 1)

                    def keep(n):
                        dve.wait_ge(*probT_ready.at(i, n + 1))
                        if n >= 3:
                            dve.wait_ge(*attended.at(i, n - 2))
                        dve.tensor_copy(probT[:, n % 3, 0:k_of(n)], pT[:, bank_of["item", n], 0:k_of(n)]).then_inc(probT_kept_dve.sem, 1)

                    for _ in range(EARLY):
                        next(steps)
                    for n in range(ITEMS + 3):
                        if n < ITEMS:
                            lowest(n)
                        if n >= 3 and not kept_by_act(n - 3):
                            keep(n - 3)
                        if n % 2 == 1 and n < NORM_AT * NT:
                            next(steps, None)
                        if n == NORM_AT * NT:
                            for _ in steps:
                                pass
                            dve.sem_inc(hid_quantised.sem, 1)
                            steps = normalise(i + 1)
                            next(steps)
                        if n >= NORM_AT * NT + 2 * NT:
                            next(steps, None)
                    for _ in steps:
                        pass
                    dve.wait_ge(*exp_made.at(i, ITEMS))
                    dve.reciprocal(inv[:, :], total[:, :]).then_inc(inv_made.sem, 1)
                    dve.wait_ge(*invT_ready.at(i, 1))
                    dve.tensor_copy(invT[:, :], pT[:, 0, 0:P]).then_inc(invT_kept.sem, 1)
                    dve.wait_ge(*y_copied.at(i, 1))
                    dve.wait_ge(*inv_spread.at(i, 1))
                    dve.tensor_tensor(yT[:, :], y_kept[:, :], pT[:, 1, :], ALU.mult).then_inc(yT_made.sem, 1)
                    dve.wait_ge(*g_tanh.at(i, 1))
                    out_of = lambda z: z.rearrange("p (t d) -> p t d", t=NT)
                    link.then(dve.scalar_tensor_tensor(g_a[:, :, :], g_th[:, :, :], 1.0, out_of(pA[:, :]), ALU.add, ALU.mult))
                    dve.wait_ge(*s_ready.at(i, 1))
                    link.then(dve.scalar_tensor_tensor(g_a[:, :, :], g_a[:, :, :], 0.5, out_of(pT[:, 2, :]), ALU.mult, ALU.mult))
                    dve.wait_ge(*stored.at(i, 0))
                    dve.wait_ge(x_again_read, i * 16 + 16)
                    link.then(dve.tensor_tensor(x_new[:, :, :], g_a[:, :, :], x_again[:, :, :], ALU.add))
                    dve.sem_inc(finished.sem, 1)
                    link.done()

            @block.scalar
            def _(act):
                act.wait_ge(pool_set, 8)
                act.wait_ge(dve_set, 4)
                act.wait_ge(cleared, 16 * 2 * SLOTS)
                with act.Fori(0, B) as i:
                    act.wait_ge(*xT_ready.at(i, 1))
                    act.copy(xnT[:, :], pS[:, 0, :]).then_inc(xT_kept.sem, 1)
                    act.wait_ge(*xqT_ready.at(i, 1))
                    act.copy(xqT[:, :], pS[:, 1, :]).then_inc(xqT_kept.sem, 1)
                    def keep_places(h):
                        act.wait_ge(*places_ready.at(i, h + 1))
                        if h >= 2:
                            act.wait_ge(*of_head(rel_sent, i, h - 2))
                        act.copy(by_place[:, h % 2, :, :], pA[:, :].rearrange("p (t r) -> p t r", t=NT)).then_inc(places_kept.sem, 1)

                    act.wait_ge(*proj_ready.at(i, 3))
                    for half_of in range(2):
                        last = act.copy(columns(vz[:, :, :, :], half_of, NT), pT[:, 0, :].rearrange("p (t g h d) -> p t g h d", t=NT, g=2, d=HD)[:, :, half_of, :, :])
                    last.then_inc(v_kept.sem, 1)
                    for t in range(NT):
                        if t < LEAD:
                            keep_places(t)
                        act.wait_ge(*gu_ready.at(i, t + 1))
                        act.activation(th[:, t % 2, :], gate_bank(t)[:, 0:HID4], ACT.Tanh, scale=0.5).then_inc(gate_tanh.sem, 1)

                    def exps(n):
                        h = n // NT
                        act.wait_ge(*low_made.at(i, n + 1))
                        if h >= 3 and n % NT == 0:
                            act.wait_ge(*probT_ready.at(i, NT * (h - 2)))
                            act.wait_ge(*of_head(band_sent, i, h - 3))
                        act.activation(prob[:, h % 3, at_prob(n):at_prob(n) + k_of(n)], pS[:, n % SB, 0:k_of(n)], ACT.Exp, bias=low[:, n:n + 1], scale=-1.0,
                                       accum_out=total[:, total_at(n):total_at(n) + 1]).then_inc(exp_made.sem, 1)

                    def keep(n):
                        act.wait_ge(*probT_ready.at(i, n + 1))
                        if n >= 3:
                            act.wait_ge(*attended.at(i, n - 2))
                        act.copy(probT[:, n % 3, 0:k_of(n)], pT[:, bank_of["item", n], 0:k_of(n)]).then_inc(probT_kept_act.sem, 1)

                    def keep_band(h):
                        act.wait_ge(*bandT_ready.at(i, h + 1))
                        if h >= 2:
                            act.wait_ge(*band_attended.at(i, h - 1))
                        act.copy(bandT[:, h % 2, :], pT[:, bank_of["band", h], :]).then_inc(bandT_kept.sem, 1)

                    def keep_hidden():
                        for c in range(HC4):
                            act.wait_ge(*hidT_ready.at(i, c + 1))
                            rows_of = min(P, HID4 - c * P)
                            act.copy(hidT[0:rows_of, c, :], pS[0:rows_of, c, :]).then_inc(hidT_kept.sem, 1)

                    def gate():
                        act.wait_ge(*ffn_ready.at(i, 1))
                        act.activation(g_th[:, :, :], pA[:, :].rearrange("p (t d) -> p t d", t=NT), ACT.Tanh, scale=0.5).then_inc(g_tanh.sem, 1)

                    for n in range(ITEMS + NT * LAG + 1):
                        if n % NT == 0 and n // NT + LEAD < HN:
                            keep_places(n // NT + LEAD)
                        if n < ITEMS:
                            exps(n)
                        if 0 <= n - 3 < ITEMS and kept_by_act(n - 3):
                            keep(n - 3)
                        if n == ITEMS + 2:
                            keep_hidden()
                        if n % NT == 3 and 0 <= n // NT - LAG < HN:
                            keep_band(n // NT - LAG)
                        if n == ITEMS + 8:
                            gate()
                    act.wait_ge(*band_attended.at(i, HN))
                    act.copy(y_kept[:, :], pY[:, :]).then_inc(y_copied.sem, 1)

            @block.tensor
            def _(pe):
                pe.wait_ge(loaded, 16 * len(weights))
                pe.wait_ge(dve_set, 1)
                for c in range(HC4):
                    pe.transpose(pS[:, 0, c * P:(c + 1) * P], wqd[:, c * P:(c + 1) * P], ident[:, :])
                    pe.transpose(pS[:, 1, c * P:(c + 1) * P], wqd[:, HID4P + c * P:HID4P + (c + 1) * P], ident[:, :])
                    rows_of = min(P, HID4 - c * P)
                    last = pe.transpose(pS[0:rows_of, 2, c * D:(c + 1) * D], wqd[:, 2 * HID4P + c * P:2 * HID4P + c * P + rows_of], ident[:, :])
                last.then_inc(pe_set, 1)
                pe.wait_ge(dve_set, 4)
                pe.wait_ge(pool_set, 8)
                pe.wait_ge(spread, 16 * (len(TERMS) + LEAD))
                with pe.Fori(0, B) as i:
                    pe.wait_ge(*xn_made.at(i, 1))
                    for t in range(NT):
                        last = pe.transpose(pS[:, 0, t * P:(t + 1) * P], xn[:, t, :], ident[:, :])
                    last.then_inc(xT_ready.sem, 1)
                    pe.wait_ge(*xq_made.at(i, 1))
                    for t in range(NT):
                        last = pe.transpose(pS[:, 1, t * P:(t + 1) * P], xq[:, t * D:(t + 1) * D], ident[:, :])
                    last.then_inc(xqT_ready.sem, 1)
                    pe.wait_ge(*xT_kept.at(i, 1))
                    pe.wait_ge(*finished.at(i, 0))
                    pe.matmul(pA[:, :], wqkv[:, 0:D], xnT[:, :], start=True, stop=True).then_inc(proj_ready.sem, 1)
                    pe.matmul(pS[:, 2, :], wqkv[:, D:2 * D], xnT[:, :], start=True, stop=True).then_inc(proj_ready.sem, 1)
                    for t in range(NT):
                        out = pT[:, 0, t * P:(t + 1) * P]
                        pe.matmul(out, xnT[:, t * P:(t + 1) * P], wqkv[:, 2 * D:3 * D], start=True, stop=False)
                        last = pe.matmul(out, ones[:, :], last_v[:, :], start=False, stop=True)
                    last.then_inc(proj_ready.sem, 1)
                    def by_places(h):
                        if h:
                            pe.wait_ge(*places_kept.at(i, h))
                        for t in range(NT):
                            cut = slice(t * P, (t + 1) * P)
                            if h < LEAD:
                                last = pe.matmul(pA[:, cut], qf[:, cut], place_wide[:, h, :], start=True, stop=True)
                            else:
                                last = pe.matmul(pA[:, cut], qs[:, h, cut], places[:, :], start=True, stop=True)
                        last.then_inc(places_ready.sem, 1)

                    pe.wait_ge(*xqT_kept.at(i, 1))
                    for t in range(NT):
                        if t == 1:
                            pe.wait_ge(*v_kept.at(i, 1))
                        if t < LEAD:
                            if t == 0:
                                pe.wait_ge(*q_kept.at(i, 1))
                            by_places(t)
                        if t >= 2:
                            pe.wait_ge(*hid_made.at(i, t - 1))
                        pe.matmul(gate_bank(t)[:, 0:HID4], xqT[:, t * P:(t + 1) * P], wg[:, 0:HID4], start=True, stop=True)
                        pe.matmul(up_bank(t)[:, 0:HID4], xqT[:, t * P:(t + 1) * P], wu[:, 0:HID4], start=True, stop=True).then_inc(gu_ready.sem, 1)
                    for t in range(NT):
                        pe.matmul(pY[:, t * P:(t + 1) * P], no_b[:, :], identb[:, :], start=True, stop=True)

                    def scores(n):
                        h, t, k = n // NT, n % NT, k_of(n)
                        if n >= SB:
                            pe.wait_ge(*exp_made.at(i, n - SB + 1))
                        elif n == 0:
                            pe.wait_ge(*hid_made.at(i, NT))
                        pe.matmul(pS[:, n % SB, 0:k], qs[:, h, t * P:k], ks[:, h, 0:k], start=True, stop=True)
                        pe.matmul(pS[:, n % SB, t * P:k], identb[:, :], maskb[:, :], start=False, stop=True,
                                  skip_group_check=True).then_inc(scored.sem, 1)

                    def turn(n):
                        pe.wait_ge(*exp_made.at(i, n + 1))
                        bank_free(pe, i, ("item", n))
                        for u in range(n % NT + 1):
                            last = pe.transpose(pT[:, bank_of["item", n], u * P:(u + 1) * P],
                                                prob[:, n // NT % 3, at_prob(n) + u * P:at_prob(n) + (u + 1) * P], ident[:, :])
                        last.then_inc(probT_ready.sem, 1)

                    def attend(n):
                        h, t = n // NT, n % NT
                        kept_wait(pe, i, n)
                        for u in range(t + 1):
                            last = pe.matmul(pY[half_rows(h), t * P:(t + 1) * P], vz[:, u, h, :], probT[:, n % 3, u * P:(u + 1) * P],
                                             start=False, stop=True, skip_group_check=True)
                        last.then_inc(attended.sem, 1)

                    def turn_band(h):
                        pe.wait_ge(*of_head(band_read, i, h))
                        bank_free(pe, i, ("band", h))
                        for t in range(NT):
                            last = pe.transpose(pT[:, bank_of["band", h], t * P:(t + 1) * P], band[:, h % 3, t, :], ident[:, :])
                        last.then_inc(bandT_ready.sem, 1)

                    def attend_band(h):
                        pe.wait_ge(*bandT_kept.at(i, h + 1))
                        pe.matmul(pY[half_rows(h), :], place_vz[:, h, :], bandT[:, h % 2, :], start=False, stop=True,
                                  skip_group_check=True).then_inc(band_attended.sem, 1)

                    def turn_hidden():
                        pe.wait_ge(*exp_made.at(i, ITEMS))
                        pe.wait_ge(*hid_quantised.at(i, 1))
                        for c in range(HC4):
                            rows_of = min(P, HID4 - c * P)
                            for t in range(NT):
                                last = pe.transpose(pS[0:rows_of, c, t * P:(t + 1) * P],
                                                    hid[:, t * HID4 + c * P:t * HID4 + c * P + rows_of], ident[:, :])
                            last.then_inc(hidT_ready.sem, 1)

                    def down():
                        pe.wait_ge(*hidT_kept.at(i, HC4))
                        for t in range(NT):
                            for c in range(HC4):
                                rows_of = min(P, HID4 - c * P)
                                last = pe.matmul(pA[:, t * D:(t + 1) * D], hidT[0:rows_of, c, t * P:(t + 1) * P], wd[0:rows_of, c, :],
                                                 start=(c == 0), stop=(c == HC4 - 1))
                        last.then_inc(ffn_ready.sem, 1)

                    pe.wait_ge(terms_read, i * 16 * LOADS + 16 * LOADS)
                    pe.wait_ge(*v_kept.at(i, 1))
                    for n in range(ITEMS + NT * LAG + 3):
                        if n % NT == 0 and n // NT + LEAD < HN:
                            by_places(n // NT + LEAD)
                        if n < ITEMS:
                            scores(n)
                        if 0 <= n - 3 < ITEMS:
                            turn(n - 3)
                        if n == ITEMS + 1:
                            turn_hidden()
                        if n == ITEMS + 5:
                            down()
                        if n % NT == 3 and 0 <= n // NT - LAG < HN:
                            turn_band(n // NT - LAG)
                        if 0 <= n - 5 < ITEMS:
                            attend(n - 5)
                        if (n - 3) % NT == 3 and 0 <= (n - 3) // NT - LAG < HN:
                            attend_band((n - 3) // NT - LAG)
                    pe.wait_ge(*inv_made.at(i, 1))
                    pe.transpose(pT[:, 0, 0:P], inv[:, :], ident[:, :]).then_inc(invT_ready.sem, 1)
                    pe.wait_ge(*invT_kept.at(i, 1))
                    for t in range(NT):
                        last = pe.matmul(pT[:, 1, t * P:(t + 1) * P], spread_t[:, t, :], invT[:, :], start=True, stop=True)
                    last.then_inc(inv_spread.sem, 1)
                    pe.wait_ge(*yT_made.at(i, 1))
                    for t in range(NT):
                        last = pe.matmul(pT[:, 2, t * P:(t + 1) * P], yT[:, t * P:(t + 1) * P], wc[:, :], start=True, stop=True)
                    last.then_inc(s_ready.sem, 1)


def layer3(nc, w, x_in, x_out):
    L = 64
    E, FF = 8, 512
    FC = FF // P
    with ExitStack() as stack:
        m = Scope(nc, stack, "d_")
        ident, identb, maskb = m.sb("ident", [P, P]), m.sb("identb", [P, P], BF16), m.sb("maskb", [P, P], BF16)
        HH = HN // 2
        vz = m.sb("vz", [P, NT * 2 * HH * P])
        wdn = vz[0:L, 0:3 * HN * D].rearrange("l (n h d) -> l n h d", n=3, h=HN)
        gather = m.sb("gather", [P, P])
        VZ_HALF = NT * HN * P // 2
        v_at = lambda u, h: vz[:, (u * HN + h) * P:(u * HN + h + 1) * P]
        ups = m.sb("ups", [L, 5, HD])
        weff = m.sb("weff", [P, 5, P])
        wc = m.sb("wc", [P, D])
        cosq, sinq, cosk, sink = [m.sb(n, [P, S]) for n in ("cosq", "sinq", "cosk", "sink")]
        rw, rb, lg_sum = m.sb("rw", [P, E]), m.sb("rb", [P, E]), m.sb("lg_sum", [P, NT, E])
        earlier = m.sb("earlier", [P, E, E])
        wup, wdown = m.sb("wup", [P, E, FF]), m.sb("wdown", [P, E * FC, D])
        half, eps, spare = m.sb("half", [P, NT]), m.sb("eps", [P, NT]), m.sb("spare", [P, 1])
        x, stat, mv, rstd = m.sb("x", [P, NT, D]), m.sb("stat", [P, NT, 6]), m.sb("mv", [P, NT, 2]), m.sb("rstd", [P, NT])
        xn, xnT = m.sb("xn", [P, NT, D]), m.sb("xnT", [P, S])
        rot_a, rot_b, qf, kf, rest_q, rest_k = [m.sb(n, [P, S]) for n in ("rot_a", "rot_b", "qf", "kf", "rest_q", "rest_k")]
        qp, kp = m.sb("qp", [P, 3, S], BF16), m.sb("kp", [P, 3, S], BF16)
        qs, ks = m.sb("qs", [KR9, HN, S], BF16), m.sb("ks", [KR9, HN, S], BF16)
        sums = m.sb("sums", [P, S])
        low, rest_low = m.sb("low", [P, P]), m.sb("rest_low", [ITEMS, P])
        lowp = [m.sb(f"lowp{j}", [ITEMS, P], BF16) for j in range(3)]
        probT = m.sb("probT", [P, 3, 3 * S])
        x_again = m.sb("x_again", [P, NT, D])
        y_kept, yT = m.sb("y_kept", [P, S]), m.sb("yT", [P, S])
        lg, pr, comb = [m.sb(n, [P, NT, E]) for n in ("lg", "pr", "comb")]
        ltop, lsum, linv = m.sb("ltop", [P, NT]), m.sb("lsum", [P, NT]), m.sb("linv", [P, NT])
        more, same, rank = m.sb("more", [P, NT, E, E]), m.sb("same", [P, NT, E, E]), m.sb("rank", [P, NT, E])
        hid = m.sb("hid", [P, 2, FC, S])
        acc, g_th, g_a, x_new = m.sb("acc", [P, NT, D]), m.sb("g_th", [P, NT, D]), m.sb("g_a", [P, NT, D]), m.sb("x_new", [P, NT, D])
        pX, pY = m.ps("pX", [P, 6, S]), m.ps("pY", [P, 2, S])
        X = [pX[:, n, :] for n in range(6)]
        up_bank = lambda n: X[n % 3]
        down_bank = lambda e: X[3 + e % 2]
        score_bank = lambda n: (X[5], pY[:, 0, :], pY[:, 1, :])[n % 3]
        q_dram, k_dram = [nc.dram_tensor(f"d_{n}", (3, HD, HN * S), BF16).ap() for n in ("q_parts", "k_parts")]

        loaded, pool_set, pe_set, dve_set, x_read, x_sent = [m.sem(n) for n in ("loaded", "pool_set", "pe_set", "dve_set", "x_read", "x_sent")]
        q_sent, k_sent, terms_read = m.sem("q_sent"), m.sem("k_sent"), m.sem("terms_read")
        stats_made = m.ev("stats_made", 1)
        centred, rstd_made, xn_made = m.ev("centred", 1), m.ev("rstd_made", 2), m.ev("xn_made", 1)
        xT_ready, xT_kept = m.ev("xT_ready", 1), m.ev("xT_kept", 1)
        proj_ready = m.ev("proj_ready", 5)
        turned = m.ev("turned", 2)
        q_split, k_split = m.ev("q_split", 1), m.ev("k_split", 1)
        v_kept = m.ev("v_kept", 1)
        scored, low_made = m.ev("scored", ITEMS), m.ev("low_made", ITEMS)
        lowT_ready, low_split, low_sent = m.ev("lowT_ready", 1), m.ev("low_split", 1), m.sem("low_sent")
        scored_by_key, exp_made, attended = m.ev("scored_by_key", PIECES * HN), m.ev("exp_made", PIECES * HN), m.ev("attended", HN)
        x_again_read = m.sem("x_again_read")
        first_loaded, moe_loaded = m.sem("first_loaded"), m.sem("moe_loaded")
        past_pool, past_sp = m.sem("past_pool"), m.sem("past_sp")
        halves_kept = m.ev("halves_kept", 2)
        sums_made, sums_spread, yT_made, s_ready = m.ev("sums_made", 1), m.ev("sums_spread", 1), m.ev("yT_made", 1), m.ev("s_ready", 1)
        lg_ready, lg_top, lg_exp, comb_made = m.ev("lg_ready", 1), m.ev("lg_top", 1), m.ev("lg_exp", 1), m.ev("comb_made", 1)
        up_ready, hid_made = m.ev("up_ready", E * FC), m.ev("hid_made", E * FC)
        down_ready, added = m.ev("down_ready", E), m.ev("added", E)
        summed, g_tanh = m.ev("summed", 1), m.ev("g_tanh", 1)
        finished, stored = m.ev("finished", 1, credit=True), m.ev("stored", 1, credit=True)
        chain = m.ev("chain", 25)

        def v_columns(half_of, width, column, step):
            whole = vz[:, :]
            return bass.AP(whole.tensor, whole.offset + half_of * HH * P + column,
                           [list(whole.ap[0]), [2 * HH * P, NT], [P + step, HH], [1, width]])

        LOADS = len(Q_GROUPS) + len(K_GROUPS)
        k_of = lambda n: (n % NT + 1) * P

        moe = [("up", e, c) for e in range(2) for c in range(FC)] + [("down", 0, t) for t in range(NT)]
        for e in range(2, E):
            moe += [("up", e, c) for c in range(FC)] + [("down", e - 1, t) for t in range(NT)]
        first, last_of = 6 * FC, len(moe) - 2 * FC
        plan = [("route", 0, 0)] + moe[:first]
        for n in range(ITEMS):
            plan.append(("score", n, 0))
            plan += moe[first + (last_of - first) * n // ITEMS:first + (last_of - first) * (n + 1) // ITEMS]
        plan += [("turn_low", 0, 0)] + moe[last_of:]

        first_weights = [(wdn[:, n, :, :], w[f"L3_W{name}T"]) for n, name in enumerate("qkv")]
        first_weights += [(ups[:, 0, 0:4], w["L3_attn_Wq_up_c"]), (ups[:, 0, 4:8], w["L3_attn_Wq_up_e"]),
                          (ups[:, 2, 0:4], w["L3_attn_Wk_up_c"]), (ups[:, 2, 4:8], w["L3_attn_Wk_up_e"]),
                          (ups[:, 4, :], w["L3_attn_Wv_up"])]
        weights = [(ident[:, :], w["ident"]), (rw[:, :], w["L3_ffn_router_w"]), (rb[:, :], w["L3_rb"][0, :].partition_broadcast(P)),
                   (cosq[:, :], w["L3_cosq"]), (sinq[:, :], w["L3_sinq"]), (cosk[:, :], w["L3_cosk"]), (sink[:, :], w["L3_sink"]),
                   (earlier[:, :, :], w["L3_earlier"]), (identb[:, :], w["identb"]), (maskb[:, :], w["maskb"]),
                   (gather[:, :], w["gather"]), (wc[:, :], w["L3_attn_Wc"]),
                   (ks[KR6:KR9, :, :], w["L3_minus"].rearrange("a (h t) -> a h t", t=S))]
        moe_weights = [(wup[:, :, :], w["L3_upT"]), (wdown[:, :, :], w["L3_downT"])]
        with nc.Block() as block:
            @block.sync
            def _(sp):
                for dst, src in first_weights:
                    sp.dma_start(dst, src).then_inc(first_loaded, 16)
                sp.dma_start(x[:, :, :], rows(x_in, 0)).then_inc(x_read, 16)
                for dst, src in weights:
                    sp.dma_start(dst, src).then_inc(loaded, 16)
                for dst, src in moe_weights:
                    sp.dma_start(dst, src).then_inc(moe_loaded, 16)
                with sp.Fori(0, B) as i:
                    sp.wait_ge(*xn_made.at(i, 1))
                    sp.nop()
                    sp.dma_start(x[:, :, :], rows(x_in, (i + 1) % B)).then_inc(x_read, 16)
                    sp.wait_ge(*q_split.at(i, 1))
                    sp.sem_inc(past_sp, 1)
                    send_parts(sp, q_dram, qp, q_sent)
                    sp.wait_ge(*k_split.at(i, 1))
                    sp.sem_inc(past_sp, 1)
                    send_parts(sp, k_dram, kp, k_sent)
                    sp.wait_ge(q_sent, i * 48 + 48)
                    sp.sem_inc(past_sp, 1)
                    load_terms(sp, qs, q_dram, Q_GROUPS, terms_read)
                    sp.wait_ge(k_sent, i * 48 + 48)
                    sp.sem_inc(past_sp, 1)
                    load_terms(sp, ks, k_dram, K_GROUPS, terms_read)
                    sp.wait_ge(*low_split.at(i, 1))
                    for j in range(3):
                        sp.dma_start(qs[KR6 + j:KR6 + j + 1, :, :], lowp[j][:, :]).then_inc(low_sent, 16)
                    sp.wait_ge(*finished.at(i, 0))
                    sp.dma_start(x_again[:, :, :], rows(x_in, i)).then_inc(x_again_read, 16)

            @block.gpsimd
            def _(pool):
                pool.memset(half[:, :], -0.5).then_inc(pool_set, 1)
                pool.memset(eps[:, :], EPS).then_inc(pool_set, 1)
                pool.memset(low[:, ITEMS:], 0.0).then_inc(pool_set, 1)
                pool.memset(sums[:, :], 0.0).then_inc(pool_set, 1)
                pool.sem_inc(stored.sem, 1)
                pool.wait_ge(pool_set, 4)

                def roots(n):
                    pool.wait_ge(*centred.at(n, 1))
                    pool.tensor_tensor(rstd[:, :], mv[:, :, 1], eps[:, :], ALU.add).then_inc(rstd_made.sem, 1)
                    pool.wait_ge(*rstd_made.at(n, 1))
                    pool.tensor_tensor(rstd[:, :], rstd[:, :], half[:, :], ALU.pow).then_inc(rstd_made.sem, 1)

                roots(0)
                pool.wait_ge(pe_set, 1)
                pool.memset(vz[:, VZ_HALF:], 0.0).then_inc(pool_set, 1)
                with pool.Fori(0, B) as i:
                    roots(i + 1)
                    pool.wait_ge(*finished.at(i, 1))
                    pool.sem_inc(past_pool, 1)
                    pool.dma_start(rows(x_out, i), x_new[:, :, :]).then_inc(x_sent, 16)
                    pool.wait_ge(x_sent, i * 16 + 16)
                    pool.sem_inc(stored.sem, 1)

            @block.vector
            def _(dve):
                dve.wait_ge(first_loaded, 16 * len(first_weights))
                dve.wait_ge(pool_set, 4)
                for one in (0, 2):
                    dve.memset(ups[:, one + 1, 0:4], 0.0)
                    pair = lambda z: z.rearrange("p (a b) -> p a b", b=2)
                    dve.tensor_scalar(pair(ups[:, one + 1, 4:8])[:, :, 0], pair(ups[:, one, 4:8])[:, :, 1], -1.0, None, ALU.mult)
                    last = dve.tensor_copy(pair(ups[:, one + 1, 4:8])[:, :, 1], pair(ups[:, one, 4:8])[:, :, 0])
                last.then_inc(dve_set, 1)

                def normalise(n):
                    dve.wait_ge(x_read, n * 16 + 16)
                    for t in range(NT):
                        last = dve.bn_stats(stat[:, t, :], x[:, t, :])
                    last.then_inc(stats_made.sem, 1)
                    dve.wait_ge(*stats_made.at(n, 1))
                    dve.memset(spare[:, :], 0.0)
                    for t in range(NT):
                        last = dve.bn_aggr(mv[:, t, :], stat[:, t, :])
                    last.then_inc(centred.sem, 1)
                    dve.wait_ge(*rstd_made.at(n, 2))
                    for t in range(NT):
                        last = dve.tensor_scalar(xn[:, t, :], x[:, t, :], mv[:, t, 0:1], rstd[:, t:t + 1], ALU.subtract, ALU.mult)
                    last.then_inc(xn_made.sem, 1)

                normalise(0)
                dve.wait_ge(pe_set, 1)
                for one in (0, 2):
                    for turn_of in range(2):
                        dve.tensor_copy(weff[:, one + turn_of, :].rearrange("p (h d) -> p h d", d=HD),
                                        X[one][:, 0:2 * P].rearrange("p (h a d) -> p a h d", a=2, d=HD)[:, turn_of, :, :])
                dve.tensor_copy(weff[:, 4, :], X[4][:, 0:P]).then_inc(dve_set, 1)
                dve.memset(vz[:, 0:VZ_HALF], 0.0).then_inc(dve_set, 1)
                dve.wait_ge(dve_set, 3)
                dve.wait_ge(pool_set, 5)
                for half_of in range(2):
                    ones_of = v_columns(half_of, 1, HH * HD if half_of == 0 else 0, 1)
                    last = dve.memset(ones_of, 1.0)
                last.then_inc(dve_set, 1)
                dve.sem_inc(finished.sem, 1)
                dve.wait_ge(loaded, 16 * len(weights))
                with dve.Fori(0, B) as i:
                    link = Chain(dve, chain, i)
                    dve.wait_ge(*lg_ready.at(i, 1))
                    link.then(dve.tensor_tensor(lg_sum[:, :, :], pY[:, 0, 0:NT * E].rearrange("p (t e) -> p t e", t=NT), rb[:, :].unsqueeze(1).to_broadcast([P, NT, E]), ALU.add))
                    dve.tensor_reduce(ltop[:, :], lg_sum[:, :, :], AX.X, ALU.max, negate=True).then_inc(lg_top.sem, 1)
                    for one, (cos, sin, full) in enumerate(((cosq, sinq, qf), (cosk, sink, kf))):
                        dve.wait_ge(*proj_ready.at(i, 2 * one + 2))
                        straight, crossed = ((X[0], X[1]), (X[3], X[2]))[one]
                        dve.tensor_tensor(rot_a[:, :], straight, cos[:, :], ALU.mult)
                        dve.tensor_tensor(rot_b[:, :], crossed, sin[:, :], ALU.mult).then_inc(turned.sem, 1)
                        dve.wait_ge(*turned.at(i, one + 1))
                        link.then(dve.tensor_tensor(full[:, :], rot_a[:, :], rot_b[:, :], ALU.add))
                    for one, full in enumerate((qf, kf)):
                        split3(dve, link, full[:, :], [(qp, kp)[one][:, j, :] for j in range(3)], (rest_q, rest_k)[one][:, :])
                        dve.sem_inc((q_split, k_split)[one].sem, 1)

                    def route():
                        dve.wait_ge(*lg_exp.at(i, 1))
                        link.then(dve.reciprocal(linv[:, :], lsum[:, :]))
                        link.then(dve.tensor_tensor(pr[:, :, :], lg[:, :, :], linv[:, :].unsqueeze(2).to_broadcast([P, NT, E]), ALU.mult))
                        for t in range(NT):
                            other = pr[:, t, :].unsqueeze(1).to_broadcast([P, E, E])
                            own = pr[:, t, :].unsqueeze(2).to_broadcast([P, E, E])
                            dve.tensor_tensor(more[:, t, :, :], other, own, ALU.is_gt)
                            last = dve.tensor_tensor(same[:, t, :, :], other, own, ALU.is_equal)
                        link.then(last)
                        for t in range(NT):
                            last = dve.tensor_tensor(same[:, t, :, :], same[:, t, :, :], earlier[:, :, :], ALU.mult)
                        link.then(last)
                        link.then(dve.tensor_tensor(more[:, :, :, :], more[:, :, :, :], same[:, :, :, :], ALU.add))
                        link.then(dve.tensor_reduce(rank[:, :, :], more[:, :, :, :], AX.X, ALU.add))
                        link.then(dve.scalar_tensor_tensor(comb[:, :, :], rank[:, :, :], 1.5, pr[:, :, :], ALU.is_lt, ALU.mult))

                    def add_expert(e):
                        dve.wait_ge(*down_ready.at(i, e + 1))
                        if e:
                            dve.wait_ge(*added.at(i, e))
                        for t in range(NT):
                            part, share = down_bank(e)[:, t * D:(t + 1) * D], comb[:, t, e:e + 1]
                            if e == 0:
                                last = dve.tensor_scalar(acc[:, t, :], part, share, None, ALU.mult)
                            else:
                                last = dve.scalar_tensor_tensor(acc[:, t, :], part, share, acc[:, t, :], ALU.mult, ALU.add)
                        last.then_inc(added.sem, 1)

                    for kind, n, part in plan:
                        if kind == "route":
                            route()
                        if kind == "score":
                            dve.wait_ge(*scored.at(i, n + 1))
                            dve.tensor_reduce(low[:, n:n + 1], score_bank(n)[:, 0:k_of(n)], AX.X, ALU.min).then_inc(low_made.sem, 1)
                        if kind == "turn_low":
                            dve.wait_ge(*lowT_ready.at(i, 1))
                            split3(dve, link, X[5][0:ITEMS, 0:P], [z[:, :] for z in lowp], rest_low[:, :])
                            dve.sem_inc(low_split.sem, 1)
                        if kind == "down" and part == NT - 1:
                            add_expert(n)
                    normalise(i + 1)
                    dve.wait_ge(*attended.at(i, HH))
                    dve.reciprocal(sums[HH * HD:HH * HD + HH, :], pY[HH * HD:HH * HD + HH, 0, :])
                    dve.wait_ge(*attended.at(i, HN))
                    dve.reciprocal(sums[0:HH, :], pY[0:HH, 1, :]).then_inc(sums_made.sem, 1)
                    dve.wait_ge(*sums_spread.at(i, 1))
                    dve.wait_ge(*halves_kept.at(i, 2))
                    for half_of in range(2):
                        mine = slice(half_of * HH * HD, (half_of + 1) * HH * HD)
                        last = dve.tensor_tensor(yT[mine, :], y_kept[mine, :], X[0][mine, :], ALU.mult)
                    last.then_inc(yT_made.sem, 1)
                    add_expert(E - 1)
                    dve.wait_ge(*g_tanh.at(i, 1))
                    link.then(dve.scalar_tensor_tensor(g_a[:, :, :], g_th[:, :, :], 1.0, acc[:, :, :], ALU.add, ALU.mult))
                    dve.wait_ge(*s_ready.at(i, 1))
                    link.then(dve.scalar_tensor_tensor(g_a[:, :, :], g_a[:, :, :], 0.5, pY[:, 1, :].rearrange("p (t d) -> p t d", t=NT), ALU.mult, ALU.mult))
                    dve.wait_ge(*stored.at(i, 0))
                    dve.wait_ge(x_again_read, i * 16 + 16)
                    link.then(dve.tensor_tensor(x_new[:, :, :], g_a[:, :, :], x_again[:, :, :], ALU.add))
                    dve.sem_inc(finished.sem, 1)
                    link.done()

            @block.scalar
            def _(act):
                with act.Fori(0, B) as i:
                    act.wait_ge(*xT_ready.at(i, 1))
                    act.copy(xnT[:, :], X[2]).then_inc(xT_kept.sem, 1)
                    act.wait_ge(*lg_top.at(i, 1))
                    for t in range(NT):
                        last = act.activation(lg[:, t, :], lg_sum[:, t, :], ACT.Exp, bias=ltop[:, t:t + 1], accum_out=lsum[:, t:t + 1])
                    last.then_inc(lg_exp.sem, 1)
                    act.wait_ge(*proj_ready.at(i, 5))
                    act.wait_ge(dve_set, 4)
                    for half_of in range(2):
                        last = act.copy(v_columns(half_of, HD, half_of * HH * HD, HD), X[5].rearrange("p (t g h d) -> p t g h d", t=NT, g=2, d=HD)[:, :, half_of, :, :])
                    last.then_inc(v_kept.sem, 1)
                    for n in range(E * FC):
                        e, c = n // FC, n % FC
                        act.wait_ge(*up_ready.at(i, n + 1))
                        if e >= 2 and c == 0:
                            act.wait_ge(*down_ready.at(i, e - 1))
                        act.activation(hid[:, e % 2, c, :], up_bank(n), ACT.Gelu).then_inc(hid_made.sem, 1)

                    def keep_half(half_of):
                        mine = slice(half_of * HH * HD, (half_of + 1) * HH * HD)
                        act.wait_ge(*attended.at(i, HH * (half_of + 1)))
                        act.copy(y_kept[mine, :], pY[mine, half_of, :]).then_inc(halves_kept.sem, 1)

                    for h in range(HN):
                        if h == HH + 2:
                            keep_half(0)
                        if h >= 3:
                            act.wait_ge(*attended.at(i, h - 2))
                        for piece in range(PIECES):
                            act.wait_ge(*scored_by_key.at(i, PIECES * h + piece + 1))
                            width = S if piece < 2 else 2 * P
                            act.activation(probT[:, h % 3, piece * S:piece * S + width], X[h % 2 * PIECES + piece][:, 0:width], ACT.Exp, scale=-1.0).then_inc(exp_made.sem, 1)
                    keep_half(1)
                    act.wait_ge(*added.at(i, E))
                    act.activation(g_th[:, :, :], acc[:, :, :], ACT.Tanh, scale=0.5).then_inc(g_tanh.sem, 1)

            @block.tensor
            def _(pe):
                pe.wait_ge(first_loaded, 16 * len(first_weights))
                pe.wait_ge(dve_set, 1)
                for h in range(HN):
                    for one in (0, 2):
                        pe.matmul(X[one][:, h * 2 * HD:(h + 1) * 2 * HD], wdn[:, one // 2, h, :], ups[:, one:one + 2, :].rearrange("l a d -> l (a d)"), start=True, stop=True)
                    last = pe.matmul(X[4][:, h * HD:(h + 1) * HD], wdn[:, 2, h, :], ups[:, 4, :], start=True, stop=True)
                last.then_inc(pe_set, 1)
                pe.wait_ge(dve_set, 2)
                pe.wait_ge(loaded, 16 * len(weights))
                with pe.Fori(0, B) as i:
                    pe.wait_ge(*xn_made.at(i, 1))
                    for t in range(NT):
                        last = pe.transpose(X[2][:, t * P:(t + 1) * P], xn[:, t, :], ident[:, :])
                    last.then_inc(xT_ready.sem, 1)
                    pe.wait_ge(*xT_kept.at(i, 1))
                    for t in range(NT):
                        last = pe.matmul(pY[:, 0, t * E:(t + 1) * E], xnT[:, t * P:(t + 1) * P], rw[:, :], start=True, stop=True)
                    last.then_inc(lg_ready.sem, 1)
                    for n, bank in enumerate((0, 1, 3, 2)):
                        pe.matmul(X[bank], weff[:, n, :], xnT[:, :], start=True, stop=True).then_inc(proj_ready.sem, 1)
                    for t in range(NT):
                        last = pe.matmul(X[5][:, t * P:(t + 1) * P], xnT[:, t * P:(t + 1) * P], weff[:, 4, :], start=True, stop=True)
                    last.then_inc(proj_ready.sem, 1)

                    def scores(n):
                        h, t, k = n // NT, n % NT, k_of(n)
                        if n >= 3:
                            pe.wait_ge(*low_made.at(i, n - 2))
                        elif n == 0:
                            pe.wait_ge(terms_read, i * 16 * LOADS + 16 * LOADS)
                            pe.wait_ge(*v_kept.at(i, 1))
                        elif n == 1:
                            pe.wait_ge(*lg_top.at(i, 1))
                        else:
                            pe.wait_ge(*finished.at(i, 0))
                        pe.matmul(score_bank(n)[:, 0:k], qs[0:KR6, h, t * P:k], ks[0:KR6, h, 0:k], start=True, stop=True)
                        pe.matmul(score_bank(n)[:, t * P:k], identb[:, :], maskb[:, :], start=False, stop=True,
                                  skip_group_check=True).then_inc(scored.sem, 1)

                    def up(e, c):
                        n = e * FC + c
                        if n >= 3:
                            pe.wait_ge(*hid_made.at(i, n - 2))
                        elif n == 0:
                            pe.wait_ge(*turned.at(i, 1))
                            pe.wait_ge(moe_loaded, 16 * len(moe_weights))
                        elif n == 2:
                            pe.wait_ge(*turned.at(i, 2))
                        pe.matmul(up_bank(n), wup[:, e, c * P:(c + 1) * P], xnT[:, :], start=True, stop=True).then_inc(up_ready.sem, 1)

                    def down(e, t):
                        if t == 0:
                            pe.wait_ge(*hid_made.at(i, (e + 1) * FC))
                            if e >= 2:
                                pe.wait_ge(*added.at(i, e - 1))
                        for c in range(FC):
                            last = pe.matmul(down_bank(e)[:, t * D:(t + 1) * D], hid[:, e % 2, c, t * P:(t + 1) * P], wdown[:, e * FC + c, :],
                                             start=(c == 0), stop=(c == FC - 1))
                        if t == NT - 1:
                            last.then_inc(down_ready.sem, 1)

                    def turn_low():
                        pe.wait_ge(*low_made.at(i, ITEMS))
                        pe.transpose(X[5][:, 0:P], low[:, :], ident[:, :]).then_inc(lowT_ready.sem, 1)

                    for kind, n, part in plan:
                        if kind == "score":
                            scores(n)
                        if kind == "up":
                            up(n, part)
                        if kind == "down":
                            down(n, part)
                        if kind == "turn_low":
                            turn_low()

                    place_of = (0, S, 2 * S, S + 3 * P)

                    def scores_by_key(h):
                        for piece, tiles in enumerate(((0,), (1, 3), (2,))):
                            if h >= 2:
                                pe.wait_ge(*exp_made.at(i, PIECES * (h - 2) + piece + 1))
                            for u in tiles:
                                at = place_of[u] - piece * S
                                bank = X[h % 2 * PIECES + piece]
                                pe.matmul(bank[:, at:at + S - u * P], ks[:, h, u * P:(u + 1) * P], qs[:, h, u * P:S], start=True, stop=True)
                                last = pe.matmul(bank[:, at:at + P], maskb[:, :], identb[:, :], start=False, stop=True, skip_group_check=True)
                            last.then_inc(scored_by_key.sem, 1)

                    def attend(h):
                        pe.wait_ge(*exp_made.at(i, PIECES * (h + 1)))
                        for u in range(NT):
                            at = place_of[u]
                            last = pe.matmul(pY[:, h // HH, u * P:S], v_at(u, h), probT[:, h % 3, at:at + S - u * P],
                                             start=(h % HH == 0 and u == 0), stop=(h % HH == HH - 1 and u == NT - 1),
                                             skip_group_check=True)
                        last.then_inc(attended.sem, 1)

                    pe.wait_ge(*hid_made.at(i, E * FC))
                    pe.wait_ge(*added.at(i, E - 1))
                    pe.wait_ge(low_sent, i * 48 + 48)
                    for h in range(HN + 1):
                        if h < HN:
                            scores_by_key(h)
                        if h:
                            attend(h - 1)
                    for t in range(NT):
                        down(E - 1, t)
                    pe.wait_ge(*sums_made.at(i, 1))
                    pe.matmul(X[0], gather[:, :], sums[:, :], start=True, stop=True).then_inc(sums_spread.sem, 1)
                    pe.wait_ge(*yT_made.at(i, 1))
                    for t in range(NT):
                        last = pe.matmul(pY[:, 1, t * P:(t + 1) * P], yT[:, t * P:(t + 1) * P], wc[:, :], start=True, stop=True)
                    last.then_inc(s_ready.sem, 1)


def host_arrays(inputs):
    a = {k: np.ascontiguousarray(v) for k, v in inputs.items()}
    out = {}
    keep = lambda *names: out.update({n: a[n] for n in names})
    t = lambda z: np.ascontiguousarray(z.T)
    out["x0"] = a["L0_attn_x"].reshape(B * S, D)
    keep("L0_attn_w_q", "L0_attn_w_k", "L0_attn_w_v2")
    out["L0_wv1T"] = t(a["L0_attn_w_v1"])
    out["L0_wgT"], out["L0_wuT"], out["L0_wdT"] = t(a["L0_ffn_w_gate"]), t(a["L0_ffn_w_up"]), t(a["L0_ffn_w_down"])
    out["ident"] = np.eye(P, dtype=np.float32)
    out["identb"] = np.eye(P).astype(mybir.dt.np(BF16))
    out["maskb"] = (BIG * (np.arange(P)[None, :] > np.arange(P)[:, None])).astype(mybir.dt.np(BF16))
    t = lambda z: np.ascontiguousarray(z.T)
    pad = lambda z: np.concatenate([z, np.zeros((HID4P - HID4, D), z.dtype)])
    for n in ("L1_attn_Wq", "L1_attn_Wr", "L1_attn_Wout", "L1_ffn_w_down"):
        out[n] = a[n]
    out["L1_WqT"], out["L1_WvT"] = t(a["L1_attn_Wq"]), t(a["L1_attn_Wv"])
    out["L1_uT"], out["L1_vT"] = t(a["L1_attn_u_bias"]), t(a["L1_attn_v_bias"])
    out["L1_gammaT"], out["L1_betaT"] = a["L1_attn_gamma"].reshape(D, 1), a["L1_attn_beta"].reshape(D, 1)
    out["L1_bout"] = a["L1_attn_bout"].reshape(1, D)
    out["L1_wg"], out["L1_wu"] = pad(a["L1_ffn_w_gate"]), pad(a["L1_ffn_w_up"])
    out["ones_row"] = np.ones((1, P), np.float32)
    place = np.arange(B, dtype=np.float32)[:, None]
    div = np.exp(np.arange(0, D, 2, dtype=np.float32) * np.float32(-np.log(10000.0) / D)).astype(np.float32)
    ang = (place * div).astype(np.float32)
    pe = np.stack([np.sin(ang), np.cos(ang)], axis=-1).reshape(B, D).astype(np.float32)
    out["L1_peT"] = t(pe[::-1])
    tok = np.arange(P)
    r = np.arange(B * B)
    c = np.float32(1 / np.sqrt(D))
    own_i = (r[:, None] // B == tok[None, :] // 16).astype(np.float32) * c
    out["L1_own_i"] = np.ascontiguousarray(np.tile(own_i, (1, NT)))
    own_b = (np.arange(16)[:, None] == tok[None, :] % 16).astype(np.float32)
    out["L1_own_b"] = np.ascontiguousarray(np.tile(own_b, (1, NT)))
    i, jj, j = r[:, None] // B, r[:, None] % B, tok[None, :] // 16
    put = (((jj == 7 + j - i) & (j <= i)) | ((jj == j - i - 2) & (j >= i + 2))).astype(np.float32)
    out["L1_is_own"] = np.ascontiguousarray(np.broadcast_to((r % B >= 7 - r // B), (P, B * B))).astype(np.float32)
    out["L1_is_next"] = np.ascontiguousarray(np.broadcast_to((r % B <= 5 - r // B), (P, B * B))).astype(np.float32)
    late = np.ones((B, B, P), np.float32)
    late[0] = np.arange(B)[:, None] <= tok[None, :] % 16
    out["L1_late"] = late.reshape(B, B * P)
    out["L1_place"] = np.concatenate([put, np.float32(-BIG) * (1 - own_b)]).astype(np.float32)
    t = lambda z: np.ascontiguousarray(z.T)
    for n in ("q", "k", "v"):
        out[f"L3_W{n}T"] = np.ascontiguousarray(a[f"L3_attn_W{n}_down"].reshape(D, 16, 64).transpose(2, 1, 0))
    for n in ("Wq_up_c", "Wq_up_e", "Wk_up_c", "Wk_up_e", "Wv_up", "Wc"):
        out[f"L3_attn_{n}"] = a[f"L3_attn_{n}"]
    inv_freq = (1.0 / np.float32(10000.0) ** (np.arange(0, 4, 2, dtype=np.float32) / np.float32(4))).astype(np.float32)
    ang = (np.arange(S, dtype=np.float32)[:, None] * inv_freq[None, :]).astype(np.float32)
    ang = np.concatenate([ang, ang], axis=-1)
    cos, sin = np.ones((S, HD), np.float32), np.zeros((S, HD), np.float32)
    cos[:, 4:], sin[:, 4:] = np.cos(ang), np.sin(ang)
    cos, sin = np.tile(cos.T, (HN, 1)), np.tile(sin.T, (HN, 1))
    neg = np.float32(-1 / np.sqrt(HD))
    out["L3_cosq"], out["L3_sinq"] = np.ascontiguousarray(cos), np.ascontiguousarray(sin)
    out["L3_cosk"], out["L3_sink"] = np.ascontiguousarray(cos * neg), np.ascontiguousarray(sin * neg)
    out["L3_ffn_router_w"] = a["L3_ffn_router_w"]
    out["L3_rb"] = a["L3_ffn_router_b"].reshape(1, 8)
    out["L3_earlier"] = np.ascontiguousarray(np.broadcast_to(np.tril(np.ones((8, 8), np.float32), -1), (P, 8, 8)))
    out["L3_upT"] = np.ascontiguousarray(a["L3_ffn_expert_up"].transpose(2, 0, 1))
    out["L3_downT"] = np.ascontiguousarray(a["L3_ffn_expert_down"].transpose(2, 0, 1).reshape(4, P, 8, D).transpose(1, 2, 0, 3).reshape(P, 32, D))
    out["L3_minus"] = np.full((3, HN * S), -1, mybir.dt.np(BF16))
    r, c = np.arange(P)[:, None], np.arange(P)[None, :]
    out["gather"] = (((r < 8) & (c >= 64) & ((c - 64) // HD == r)) | ((r >= 64) & (c < 64) & (c // HD == r - 64))).astype(np.float32)
    pad = lambda z: np.concatenate([z, np.zeros((HID4P - HID4, D), z.dtype)])
    for n in ("L2_attn_w_attn", "L2_attn_w_proj", "L2_ffn_w_down"):
        out[n] = a[n]
    ek, ev = a["L2_attn_embk"], a["L2_attn_embv"]
    out["L2_last_k"] = np.tile(ek[-1], HN).reshape(D, 1)
    out["L2_place_k"] = np.ascontiguousarray(ek[::-1].T)
    out["L2_place_last"] = ek[-1].reshape(HD, 1)
    out["L2_last_v"] = np.tile(ev[-1], HN).reshape(1, D)
    out["L2_place_v"] = np.ascontiguousarray(ev[::-1])
    out["L2_wg"], out["L2_wu"] = pad(a["L2_ffn_w_gate"]), pad(a["L2_ffn_w_up"])
    row, tile, c = np.arange(P)[:, None, None], np.arange(NT)[None, :, None], np.arange(P)[None, None, :]
    out["spread_t"] = (row == tile * 32 + c // HD).astype(np.float32)
    return out


def build(nc, w, result):
    x1, x2, x3 = [nc.dram_tensor(f"x_after_{n}", (B * S, D), F32).ap() for n in range(3)]
    layer0(nc, w, w["x0"], x1)
    layer1(nc, w, x1, x2)
    layer2(nc, w, x2, x3)
    layer3(nc, w, x3, result)


def kernel(**inputs):
    import concourse.bacc as bacc
    from concourse.bass_utils import run_bass_kernel_spmd

    nc = bacc.Bacc("TRN2", target_bir_lowering=False, num_devices=1)
    arrays = host_arrays(inputs)
    w = {name: nc.dram_tensor(name, a.shape, mybir.dt.from_np(a.dtype), kind="ExternalInput").ap() for name, a in arrays.items()}
    result = nc.dram_tensor("result", (B * S, D), F32, kind="ExternalOutput").ap()
    build(nc, w, result)
    r = run_bass_kernel_spmd(nc, [arrays], core_ids=[0])
    return r.results[0]["result"].reshape(B, S, D)
```
